# Optimizing a Trainium2 kernel written in Bass

```python
import numpy as np
import jax
import jax.numpy as jnp

def _softmax(x, axis=-1):
    return jax.nn.softmax(x, axis=axis)

def _gelu(x):
    return jax.nn.gelu(x, approximate=True)

def _silu(x):
    return jax.nn.silu(x)

def _sigmoid(x):
    return jax.nn.sigmoid(x)

def _layernorm(x, axis=-1, eps=1e-05):
    m = jnp.mean(x, axis=axis, keepdims=True)
    v = jnp.var(x, axis=axis, keepdims=True)
    return (x - m) / jnp.sqrt(v + eps)

def _scatter_add(tgt, idx, src, axis=0):
    return tgt.at[idx].add(src)

def _segment_sum(src, seg, n):
    return jax.ops.segment_sum(src, seg, n)
kernel_name = 'mk_seq_preln_d1_jaxref_r4_4f69de'

def setup_inputs(seed: int=0):
    np.random.seed(seed)
    _w = jnp.asarray

    def _L0_attn_setup():
        import jax, jax.numpy as jnp
        import numpy as np
        HIDDEN = 256
        N_HEADS = 16
        HEAD_DIM = HIDDEN // N_HEADS
        WINDOW = 64
        HALF_W = WINDOW // 2
        GLOBAL_TOKENS = (0,)

        def _longformer_mask(seq_len: int) -> jnp.ndarray:
            idx = jnp.arange(seq_len)
            mask = jnp.abs(idx[:, None] - idx[None, :]) <= HALF_W
            for g in GLOBAL_TOKENS:
                if 0 <= g < seq_len:
                    mask = mask.at[g, :].set(True)
                    mask = mask.at[:, g].set(True)
            return mask
        key = jax.random.key(seed)
        ks = jax.random.split(key, 5)
        B, S = (1, 1024)
        scale = 0.02
        return {'x': jax.random.normal(ks[0], (B, S, HIDDEN), dtype=jnp.float32), 'Wq': jax.random.normal(ks[1], (HIDDEN, HIDDEN), dtype=jnp.float32) * scale, 'Wk': jax.random.normal(ks[2], (HIDDEN, HIDDEN), dtype=jnp.float32) * scale, 'Wv': jax.random.normal(ks[3], (HIDDEN, HIDDEN), dtype=jnp.float32) * scale, 'Wo': jax.random.normal(ks[4], (HIDDEN, HIDDEN), dtype=jnp.float32) * scale}
    _L0_attn_in = _L0_attn_setup()

    def _L0_ffn_setup():
        import jax, jax.numpy as jnp
        import numpy as np
        import math
        D_MODEL = 256
        D_FF = 1024
        NUM_EXPERTS = 8
        NUM_SHARED = 1
        E_ROUTED = NUM_EXPERTS - NUM_SHARED
        TOP_K = 2
        CAP_FACTOR = 1.25
        B, S = (4, 512)
        T = B * S
        CAPACITY = math.ceil(CAP_FACTOR * T * TOP_K / E_ROUTED)
        SHARED_SCALE = 1.0

        def _layernorm(x, g, b, eps=1e-05):
            mu = jnp.mean(x, axis=-1, keepdims=True)
            var = jnp.mean((x - mu) ** 2, axis=-1, keepdims=True)
            return (x - mu) * jax.lax.rsqrt(var + eps) * g + b
        key = jax.random.key(seed)
        ks = jax.random.split(key, 10)
        s = 0.02
        return {'x': jax.random.normal(ks[0], (B, S, D_MODEL), dtype=jnp.float32), 'ln_g': jnp.ones((D_MODEL,), jnp.float32), 'ln_b': jnp.zeros((D_MODEL,), jnp.float32), 'Wr': jax.random.normal(ks[1], (D_MODEL, E_ROUTED), jnp.float32) * s, 'W1': jax.random.normal(ks[2], (E_ROUTED, D_MODEL, D_FF), jnp.float32) * s, 'W3': jax.random.normal(ks[3], (E_ROUTED, D_MODEL, D_FF), jnp.float32) * s, 'W2': jax.random.normal(ks[4], (E_ROUTED, D_FF, D_MODEL), jnp.float32) * s, 'W1s': jax.random.normal(ks[5], (D_MODEL, D_FF), jnp.float32) * s, 'W3s': jax.random.normal(ks[6], (D_MODEL, D_FF), jnp.float32) * s, 'W2s': jax.random.normal(ks[7], (D_FF, D_MODEL), jnp.float32) * s}
    _L0_ffn_in = _L0_ffn_setup()
    _d = {'L0_attn_x': _L0_attn_in['x'], 'L0_attn_Wq': _L0_attn_in['Wq'], 'L0_attn_Wk': _L0_attn_in['Wk'], 'L0_attn_Wv': _L0_attn_in['Wv'], 'L0_attn_Wo': _L0_attn_in['Wo'], 'L0_ffn_ln_g': _L0_ffn_in['ln_g'], 'L0_ffn_ln_b': _L0_ffn_in['ln_b'], 'L0_ffn_Wr': _L0_ffn_in['Wr'], 'L0_ffn_W1': _L0_ffn_in['W1'], 'L0_ffn_W3': _L0_ffn_in['W3'], 'L0_ffn_W2': _L0_ffn_in['W2'], 'L0_ffn_W1s': _L0_ffn_in['W1s'], 'L0_ffn_W3s': _L0_ffn_in['W3s'], 'L0_ffn_W2s': _L0_ffn_in['W2s']}
    _x0 = _d['L0_attn_x']
    _d['L0_attn_x'] = jax.random.normal(jax.random.fold_in(jax.random.key(seed), 1), (16, 1024, 256), dtype=_x0.dtype)
    del _x0
    return _d

def reference(L0_attn_x, L0_attn_Wq, L0_attn_Wk, L0_attn_Wv, L0_attn_Wo, L0_ffn_ln_g, L0_ffn_ln_b, L0_ffn_Wr, L0_ffn_W1, L0_ffn_W3, L0_ffn_W2, L0_ffn_W1s, L0_ffn_W3s, L0_ffn_W2s):

    def _L0_attn_ref(x, Wq, Wk, Wv, Wo):
        import jax, jax.numpy as jnp
        import numpy as np
        HIDDEN = 256
        N_HEADS = 16
        HEAD_DIM = HIDDEN // N_HEADS
        WINDOW = 64
        HALF_W = WINDOW // 2
        GLOBAL_TOKENS = (0,)

        def _longformer_mask(seq_len: int) -> jnp.ndarray:
            idx = jnp.arange(seq_len)
            mask = jnp.abs(idx[:, None] - idx[None, :]) <= HALF_W
            for g in GLOBAL_TOKENS:
                if 0 <= g < seq_len:
                    mask = mask.at[g, :].set(True)
                    mask = mask.at[:, g].set(True)
            return mask
        B, S, H = x.shape
        scale = HEAD_DIM ** (-0.5)

        def proj(W):
            return jnp.einsum('bsh,oh->bso', x, W).reshape(B, S, N_HEADS, HEAD_DIM).transpose(0, 2, 1, 3)
        q, k, v = (proj(Wq), proj(Wk), proj(Wv))
        scores = jnp.einsum('bnsd,bntd->bnst', q, k) * scale
        mask = _longformer_mask(S)
        scores = jnp.where(mask[None, None], scores, jnp.float32(-jnp.inf))
        attn = jax.nn.softmax(scores, axis=-1)
        out = jnp.einsum('bnst,bntd->bnsd', attn, v)
        out = out.transpose(0, 2, 1, 3).reshape(B, S, H)
        return jnp.einsum('bsh,oh->bso', out, Wo)

    def _L0_ffn_ref(x, ln_g, ln_b, Wr, W1, W3, W2, W1s, W3s, W2s):
        import jax, jax.numpy as jnp
        import numpy as np
        import math
        D_MODEL = 256
        D_FF = 1024
        NUM_EXPERTS = 8
        NUM_SHARED = 1
        E_ROUTED = NUM_EXPERTS - NUM_SHARED
        TOP_K = 2
        CAP_FACTOR = 1.25
        B, S = (4, 512)
        T = B * S
        CAPACITY = math.ceil(CAP_FACTOR * T * TOP_K / E_ROUTED)
        SHARED_SCALE = 1.0

        def _layernorm(x, g, b, eps=1e-05):
            mu = jnp.mean(x, axis=-1, keepdims=True)
            var = jnp.mean((x - mu) ** 2, axis=-1, keepdims=True)
            return (x - mu) * jax.lax.rsqrt(var + eps) * g + b
        Bx, Sx, D = x.shape
        Tn = Bx * Sx
        h = _layernorm(x, ln_g, ln_b).reshape(Tn, D)
        logits = h @ Wr
        top_vals, top_idx = jax.lax.top_k(logits, TOP_K)
        gates = jax.nn.softmax(top_vals, axis=-1)
        idx = top_idx.T.reshape(-1)
        gat = gates.T.reshape(-1)
        tok = jnp.tile(jnp.arange(Tn), TOP_K)
        onehot = jax.nn.one_hot(idx, E_ROUTED, dtype=jnp.int32)
        pos = jnp.sum(jnp.cumsum(onehot, axis=0) * onehot, axis=-1) - 1
        keep = pos < CAPACITY
        pos_c = jnp.where(keep, pos, CAPACITY)
        xe = jnp.zeros((E_ROUTED, CAPACITY, D), h.dtype).at[idx, pos_c].set(h[tok], mode='drop')
        a = jnp.einsum('ecd,edf->ecf', xe, W1)
        b = jnp.einsum('ecd,edf->ecf', xe, W3)
        ye = jnp.einsum('ecf,efd->ecd', jax.nn.silu(a) * b, W2)
        out_slots = ye[jnp.clip(idx, 0, E_ROUTED - 1), jnp.clip(pos_c, 0, CAPACITY - 1)]
        out_slots = out_slots * (gat * keep.astype(gat.dtype))[:, None]
        routed = jnp.zeros((Tn, D), h.dtype).at[tok].add(out_slots)
        shared = jax.nn.silu(h @ W1s) * (h @ W3s) @ W2s
        out = routed + SHARED_SCALE * shared
        return out.reshape(Bx, Sx, D)
    x = L0_attn_x
    x = x + _L0_attn_ref(_layernorm(x, axis=-1), L0_attn_Wq, L0_attn_Wk, L0_attn_Wv, L0_attn_Wo)
    x = x + _L0_ffn_ref(_layernorm(x, axis=-1), L0_ffn_ln_g, L0_ffn_ln_b, L0_ffn_Wr, L0_ffn_W1, L0_ffn_W3, L0_ffn_W2, L0_ffn_W1s, L0_ffn_W3s, L0_ffn_W2s)
    return x

_drawn_inputs = setup_inputs


def setup_inputs(seed=0):
    import zlib

    import numpy as np

    out = dict(_drawn_inputs(seed))
    spreads = {'L0_ffn_ln_g': (1.0, 0.6), 'L0_ffn_ln_b': (0.0, 0.8)}
    factors = {'L0_attn_Wq': 8.0,
     'L0_attn_Wk': 8.0,
     'L0_attn_Wv': 4.327,
     'L0_attn_Wo': 4.378,
     'L0_ffn_Wr': 5.169,
     'L0_ffn_W1': 4.905,
     'L0_ffn_W3': 4.847,
     'L0_ffn_W2': 4.852,
     'L0_ffn_W1s': 3.712,
     'L0_ffn_W3s': 3.575,
     'L0_ffn_W2s': 3.574}
    for name, (base, spread) in spreads.items():
        noise = np.random.default_rng([zlib.crc32(name.encode()), seed]).standard_normal(out[name].shape)
        drawn = base * np.exp(spread * noise) if base else spread * noise
        out[name] = jnp.asarray(drawn.astype(out[name].dtype))
    for name, factor in factors.items():
        out[name] = (out[name] * factor).astype(out[name].dtype)
    return out
```

```python
import concourse.bass as bass
from concourse import mybir
from contextlib import ExitStack

F32, BF16, FP16, I32 = mybir.dt.float32, mybir.dt.bfloat16, mybir.dt.float16, mybir.dt.int32
ALU = mybir.AluOpType
ACT = mybir.ActivationFunctionType
AX = mybir.AxisListType

P = 128
D = 256
FT = D // P
HEADS, HD = 16, 16
PAIRS = HEADS // 2
PIECES = 4
HALF_W = 32
WIN = P + 2 * HALF_W
SCALE = HD ** -0.5
EPS = 1e-5
MASKED = -1e30


class Signal:

    def __init__(self, nc, name, per, unit=1, credit=1):
        self.sem = nc.alloc_semaphore(name)
        self.per, self.unit, self.credit = per, unit, credit

    def start(self, engine):
        if self.credit:
            engine.sem_inc(self.sem, self.credit * self.per * self.unit)

    def after(self, batch, events):
        if isinstance(batch, int):
            value = ((batch + self.credit) * self.per + events) * self.unit
            assert value > 0
            return value
        return batch * (self.per * self.unit) + (self.credit * self.per + events) * self.unit

    def due(self, batch, events):
        return not isinstance(batch, int) or (batch + self.credit) * self.per + events > 0


def tensors(ctx, nc):
    def sb(name, shape, dt):
        return ctx.enter_context(nc.sbuf_tensor(name, shape, dt))

    def ps(name, shape, dt=F32):
        return ctx.enter_context(nc.psum_tensor(name, shape, dt))
    return sb, ps


def attention(nc, x, wq, wk, wv, wo, y, id32, W, shared, shared_loaded):
    batches, seq, _ = x.shape
    NB = seq // P
    XLEAD = 4
    LAG = dict(stats=-2, norm=-1, spread=-1, project=0, scores=2, maxima=3, weigh=5, gather=7, out=8)
    x_v = x.rearrange("b (s p) d -> b s p d", p=P)
    y_v = y.rearrange("b (s p) d -> b s p d", p=P)
    COLS = seq + 2 * HALF_W

    ctx = ExitStack()
    with nc.cleanup_on_exit(), ctx:
        sb, ps = tensors(ctx, nc)

        def sig(name, per=NB, unit=1):
            s = Signal(nc, name, per, unit)
            signals.append(s)
            return s
        signals = []

        id16 = sb("id16", [P, P], FP16)
        idb = sb("idb", [P, P], BF16)
        band = sb("band", [P, 3, WIN], BF16)
        pick = sb("pick", [P, HEADS, P], BF16)
        first_row = sb("first_row", [P, P], F32)
        near0 = sb("near0", [P, 2], F32)
        wstage = W.up_hi[:, :, :, :].rearrange("p k f o -> p (k f o)").bitcast(F32)\
            .rearrange("p (f n o) -> p f n o", f=FT, n=4)
        whi = sb("whi", [P, FT, 4, D], FP16)
        wlo = sb("wlo", [P, FT, 4, D], FP16)
        x_in = sb("x_in", [P, NB, D], F32)
        x_res = sb("x_res", [P, 4, D], F32)
        st = sb("st", [P, 2, 6], F32)
        mv = sb("mv", [P, 2, 2], F32)
        ve = sb("ve", [P, 2], F32)
        mhalf = sb("mhalf", [P, 1], F32)
        rs = sb("rs", [P, 2], F32)
        xn = sb("xn", [P, 2, D], F32)
        xt_hi = sb("xt_hi", [P, FT, P], FP16)
        xt_lo = sb("xt_lo", [P, FT, P], FP16)
        q_tok = sb("q_tok", [P, HEADS, PIECES, HD], FP16)
        k_tok = sb("k_tok", [P, HEADS, PIECES, HD], FP16)
        k_st = sb("k_st", [P, PAIRS, COLS], FP16)
        q_ev = sb("q_ev", [P, PAIRS, COLS], FP16)
        q_od = sb("q_od", [P, PAIRS, COLS], FP16)
        v_sb = sb("v_sb", [P, NB, HEADS, 2 * HD], F32)
        k0 = sb("k0", [P, PAIRS], FP16)
        mx = sb("mx", [P, HEADS], F32)
        mf = sb("mf", [P, HEADS], F32)
        ms = sb("ms", [P, 48], BF16)
        eg = sb("eg", [P, HEADS], F32)
        pg = sb("pg", [P, NB, HEADS], F32)
        ms_t = sb("ms_t", [P, COLS], BF16)
        pt = sb("pt", [P, 4, 2, WIN], F32)
        o_acc = sb("o_acc", [P, 4, COLS], F32)
        v0 = sb("v0", [P, HEADS, HD], F32)
        pgv = sb("pgv", [P, HEADS, HD], F32)
        den = sb("den", [P, HEADS], F32)
        rec = sb("rec", [P, HEADS], F32)
        onum = sb("onum", [P, HEADS, HD], F32)
        o_tok = sb("o_tok", [P, HEADS, HD], F32)
        ot_hi = sb("ot_hi", [P, FT, P], FP16)
        ot_lo = sb("ot_lo", [P, FT, P], FP16)
        y_sb = sb("y_sb", [P, 2, D], F32)
        z_st = sb("z_st", [P, PAIRS * HEADS], FP16)
        s0 = sb("s0", [HEADS, seq], F32)
        m0 = sb("m0", [HEADS, 1], F32)
        nb0 = sb("nb0", [HEADS, 1], F32)
        p0 = sb("p0", [HEADS, seq], F32)
        l0 = sb("l0", [HEADS, 1], F32)
        r0 = sb("r0", [HEADS, 1], F32)
        p0_t = sb("p0_t", [P, NB, HEADS], F32)
        v_keep = sb("v_keep", [P, 2, HEADS, HD], F32)
        own = sb("own", [HEADS, HEADS, HD], F32)
        o0_all = sb("o0_all", [HEADS, D], F32)
        one_col = sb("one_col", [HEADS, 1], F32)
        o0 = sb("o0", [1, D], F32)
        o0_dram = nc.dram_tensor("o0_rows", (batches, D), F32).ap()
        o0_rows = sb("o0_rows_sb", [batches, D], F32)
        x0_rows = sb("x0_rows_sb", [batches, D], F32)
        y0_rows = sb("y0_rows_sb", [batches, D], F32)

        bank_qk = ps("bank_qk", [P, 512])
        bank_v = ps("bank_v", [P, 512])
        bank_m = ps("bank_m", [P, 512])
        bank_s = [ps(f"bank_s{i}", [P, 512]) for i in range(2)]
        bank_w = [ps(f"bank_w{i}", [P, 512]) for i in range(2)]
        bank_o = ps("bank_o", [P, 512])
        qk_ps = bank_qk[:, :].rearrange("p (t h d) -> p t h d", t=2, h=HEADS)
        kst_ps = bank_qk[:, :].bitcast(FP16).rearrange("p (j t) -> p j t", j=PAIRS)
        gat_ps = bank_qk[:, :].rearrange("p (h d) -> p h d", h=HEADS)
        v_ps = bank_v[:, 0:D].rearrange("p (h d) -> p h d", h=HEADS)
        qst_ps = bank_v[:, :].bitcast(FP16).rearrange("p (j t) -> p j t", j=PAIRS)
        wo_ps = bank_v[:, 0:D]
        tr_ps = bank_m[:, 0:D].rearrange("p (f t) -> p f t", f=FT)
        mst_ps = bank_m[:, :].bitcast(BF16)
        g_ps = bank_m[:, 0:HEADS]

        w_in = nc.alloc_semaphore("w_in")
        w_hi_done = nc.alloc_semaphore("w_hi_done")
        w_lo_done = nc.alloc_semaphore("w_lo_done")
        setup = nc.alloc_semaphore("setup")
        passed = nc.alloc_semaphore("passed")
        zeroed = nc.alloc_semaphore("zeroed")
        fin = nc.alloc_semaphore("fin")
        fin_dma = nc.alloc_semaphore("fin_dma")
        x_loaded = [sig(f"x_loaded{s}", 1, 16) for s in range(NB)]
        res_loaded = [sig(f"res_loaded{s}", 2, 16) for s in range(4)]
        y_stored = [sig(f"y_stored{s}", NB // 2, 16) for s in range(2)]
        o0_stored = sig("o0_stored", 1, 16)
        (stats_raw, stats_done, var_eps, rstd_done, normed, spread, xt_hi_done, xt_split, qk_done, v_done,
         qk_hi, qk_split, v_copied, kst_done, qst_done, kst_copied, g_done, mf_done, ms_hi, ms_lo,
         e_part, e_done, pg_done, mst_done, mst_copied, gat_done, den_done, rec_done, pgv_done,
         num_done, o_done, otr_done, ot_hi_done, ot_split, wo_done, y_ready) = [sig(n) for n in (
             "stats_raw", "stats_done", "var_eps", "rstd_done", "normed", "spread", "xt_hi_done",
             "xt_split", "qk_done", "v_done", "qk_hi", "qk_split", "v_copied", "kst_done", "qst_done",
             "kst_copied", "g_done", "mf_done", "ms_hi", "ms_lo", "e_part", "e_done", "pg_done",
             "mst_done", "mst_copied", "gat_done", "den_done", "rec_done", "pgv_done", "num_done",
             "o_done", "otr_done", "ot_hi_done", "ot_split", "wo_done", "y_ready")]
        qst_copied = sig("qst_copied", 2 * NB)
        scored = sig("scored", PAIRS * NB)
        maxed = sig("maxed", PAIRS * NB)
        weighed = sig("weighed", PAIRS * NB)
        exped = sig("exped", PAIRS * NB)
        valued = sig("valued", 2 * NB)
        added = sig("added", 2 * NB)
        o_copied = sig("o_copied", 2 * NB)
        (k0_copied, z_copied, v0_done, v0_copied, m0_done, nb0_done, p0_done, r0_done, p0t_done,
         p0t_copied, o0_done, o0_scaled, o0_sum, o0_copied, v_kept) = [sig(n, 1) for n in (
             "k0_copied", "z_copied", "v0_done", "v0_copied", "m0_done", "nb0_done", "p0_done",
             "r0_done", "p0t_done", "p0t_copied", "o0_done", "o0_scaled", "o0_sum", "o0_copied",
             "v_kept")]
        s0_done = sig("s0_done", 2)
        s0_copied = sig("s0_copied", 2)

        def place(b, s, lag):
            q = s - lag
            batch = b + q // NB
            if isinstance(b, int) and not 0 <= batch < batches:
                return None
            return batch, q % NB

        def turns(engine, body):
            for s in range(-3, 0):
                body(0, s)
            for s in range(NB):
                body(0, s)
            with engine.Fori(1, batches - 1) as b:
                for s in range(NB):
                    body(b, s)
            for b, n in ((batches - 1, NB), (batches, LAG["out"] + 1)):
                for s in range(n):
                    body(b, s)

        def cols(s, extra=0):
            return slice(HALF_W + s * P - extra, HALF_W + (s + 1) * P + extra)

        block = ctx.enter_context(nc.Block())

        @block.sync
        def _(sp):
            for n, w in enumerate((wq, wk, wv, wo)):
                sp.dma_start(wstage[:, :, n, :], w.rearrange("(f p) o -> p f o", p=P)).then_inc(w_in, 16)
            for s in x_loaded:
                s.start(sp)
            for s in res_loaded:
                s.start(sp)
            for s in y_stored:
                s.start(sp)
            o0_stored.start(sp)

            def slot(b, s):
                if at := place(b, s, -XLEAD):
                    c, t = at
                    sp.wait_ge(normed.sem, normed.after(c, t + 1 - NB))
                    sp.dma_start(x_in[:, t, :], x_v[c, t]).then_inc(x_loaded[t].sem, 16)
                if at := place(b, s, LAG["out"] - 2):
                    c, t = at
                    sp.wait_ge(y_ready.sem, y_ready.after(c, t - 3))
                    sp.sem_inc(passed, 1)
                    sp.dma_start(x_res[:, t % 4, :], x_v[c, t]).then_inc(res_loaded[t % 4].sem, 16)
                if at := place(b, s, LAG["out"]):
                    c, t = at
                    sp.wait_ge(y_ready.sem, y_ready.after(c, t + 1))
                    sp.sem_inc(passed, 1)
                    sp.dma_start(y_v[c, t], y_sb[:, t % 2, :]).then_inc(y_stored[t % 2].sem, 16)
                if s == 5 and (at := place(b, s, NB)):
                    c = at[0]
                    sp.wait_ge(o0_copied.sem, o0_copied.after(c, 1))
                    sp.dma_start(o0_dram[bass.ds(c, 1), :], o0[:, :]).then_inc(o0_stored.sem, 16)
            for s in range(-XLEAD, -3):
                slot(0, s)
            W.load(sp, *shared, shared_loaded)
            turns(sp, slot)
            sp.wait_ge(shared_loaded, 48)
            sp.wait_ge(o0_stored.sem, o0_stored.after(batches - 1, 1))
            sp.dma_start(o0_rows[:, :], o0_dram).then_inc(fin_dma, 16)
            sp.dma_start(x0_rows[:, :], x[:, 0, :]).then_inc(fin_dma, 16)
            for s in y_stored:
                sp.wait_ge(s.sem, s.after(batches - 1, NB // 2))
            sp.wait_ge(fin, 5)
            sp.dma_start(y[:, 0, :], y0_rows[:, :]).then_inc(fin_dma, 16)
            sp.wait_ge(fin_dma, 48)

        @block.gpsimd
        def _(pool):
            for s in signals:
                if s.unit == 1:
                    s.start(pool)
            G = nc.gpsimd
            G.memset(id32[:, :], 0.0).then_inc(zeroed, 1)
            G.memset(idb[:, :], 0.0).then_inc(zeroed, 1)
            G.memset(band[:, :, :], 0.0).then_inc(zeroed, 1)
            G.memset(pick[:, :, :], 0.0).then_inc(zeroed, 1)
            G.memset(first_row[:, :], 0.0).then_inc(zeroed, 1)
            G.memset(near0[:, :], 0.0).then_inc(zeroed, 1)
            G.memset(own[:, :, :], 0.0).then_inc(zeroed, 1)
            G.memset(one_col[:, :], 1.0).then_inc(setup, 1)
            G.memset(mhalf[:, :], -0.5).then_inc(setup, 1)
            G.memset(v_sb[:, :, :, :], 1.0).then_inc(setup, 1)
            pool.wait_ge(zeroed, 7)

            def fill(out, op, value, base, mult, pattern):
                return G.affine_select(out=out, in_=out, compare_op=op, fill=value, base=base,
                                       channel_multiplier=mult, pattern=pattern)
            fill(id32[:, :], ALU.not_equal, 1.0, 0, 1, [[-1, P]]).then_inc(zeroed, 1)
            fill(idb[:, :], ALU.not_equal, 1.0, 0, 1, [[-1, P]]).then_inc(zeroed, 1)
            fill(band[:, :, :], ALU.is_ge, MASKED, 0, -1, [[0, 3], [1, WIN]]).then_inc(zeroed, 1)
            fill(pick[:, :, :], ALU.not_equal, 1.0, 0, 1, [[-1, HEADS], [0, P]]).then_inc(zeroed, 1)
            fill(first_row[:, :], ALU.not_equal, 1.0, 0, 1, [[0, P]]).then_inc(zeroed, 1)
            fill(near0[:, 1:2], ALU.is_gt, MASKED, -HALF_W, 1, [[0, 1]]).then_inc(zeroed, 1)
            fill(own[:, :, :], ALU.not_equal, 1.0, 0, 1, [[-1, HEADS], [0, HD]]).then_inc(zeroed, 1)
            pool.wait_ge(zeroed, 14)
            fill(band[:, :, :], ALU.is_ge, MASKED, 2 * HALF_W, 1, [[0, 3], [-1, WIN]]).then_inc(zeroed, 1)
            fill(pick[:, :, :], ALU.not_equal, 1.0, -32, 1, [[-1, HEADS], [0, P]]).then_inc(zeroed, 1)
            G.tensor_copy(id16[:, :], id32[:, :]).then_inc(setup, 1)
            pool.wait_ge(zeroed, 16)
            G.memset(band[:, 1, 0:HALF_W], MASKED).then_inc(setup, 1)
            G.memset(band[:, 2, HALF_W + P:WIN], MASKED).then_inc(setup, 1)

            def slot(b, s):
                if at := place(b, s, LAG["stats"]):
                    c, t = at
                    pool.wait_ge(stats_done.sem, stats_done.after(c, t + 1))
                    pool.sem_inc(passed, 1)
                    G.tensor_scalar(ve[:, t % 2:t % 2 + 1], mv[:, t % 2, 1:2], EPS, None, ALU.add)\
                        .then_inc(var_eps.sem, 1)
                    pool.wait_ge(var_eps.sem, var_eps.after(c, t + 1))
                    pool.wait_ge(normed.sem, normed.after(c, t - 1))
                    G.tensor_tensor(rs[:, t % 2:t % 2 + 1], ve[:, t % 2:t % 2 + 1], mhalf[:, :], ALU.pow)\
                        .then_inc(rstd_done.sem, 1)
                if at := place(b, s, LAG["gather"]):
                    c, t = at
                    pool.wait_ge(pg_done.sem, pg_done.after(c, t + 1))
                    pool.wait_ge(v0_copied.sem, v0_copied.after(c, 1))
                    pool.wait_ge(num_done.sem, num_done.after(c, t))
                    G.tensor_tensor(pgv[:, :, :], v0[:, :, :],
                                    pg[:, t, :].unsqueeze(2).to_broadcast([P, HEADS, HD]), ALU.mult)\
                        .then_inc(pgv_done.sem, 1)
                    pool.wait_ge(num_done.sem, num_done.after(c, t + 1))
                    pool.wait_ge(otr_done.sem, otr_done.after(c, t))
                    G.tensor_tensor(o_tok[:, :, :], onum[:, :, :],
                                    rec[:, :].unsqueeze(2).to_broadcast([P, HEADS, HD]), ALU.mult)\
                        .then_inc(o_done.sem, 1)
                if s == 4 and (at := place(b, s, s)):
                    c = at[0]
                    pool.wait_ge(v_copied.sem, v_copied.after(c, 2))
                    pool.wait_ge(o0_done.sem, o0_done.after(c, 0))
                    pool.sem_inc(passed, 1)
                    G.tensor_copy(v_keep[:, :, :, :], v_sb[:, 0:2, :, 0:HD]).then_inc(v_kept.sem, 1)
            turns(pool, slot)

        @block.vector
        def _(dve):
            V = nc.vector
            V.memset(k_st[:, :, :].bitcast(I32), 0).then_inc(setup, 1)
            V.memset(q_ev[:, :, :].bitcast(I32), 0).then_inc(setup, 1)
            V.memset(q_od[:, :, :].bitcast(I32), 0).then_inc(setup, 1)
            V.memset(ms_t[:, :], 0.0).then_inc(setup, 1)
            V.memset(ms[:, :], 0.0).then_inc(setup, 1)
            V.memset(z_st[:, :], 0.0).then_inc(setup, 1)
            V.memset(o_acc[:, :, :], 0.0).then_inc(setup, 1)
            for n in range(4):
                dve.wait_ge(w_hi_done, n + 1)
                V.tensor_tensor(wlo[:, :, n, :], wstage[:, :, n, :], whi[:, :, n, :], ALU.subtract)\
                    .then_inc(w_lo_done, 1)
            dve.wait_ge(setup, 13)

            def slot(b, s):
                if at := place(b, s, LAG["maxima"]):
                    c, t = at
                    dve.wait_ge(g_done.sem, g_done.after(c, t + 1))
                    dve.wait_ge(maxed.sem, maxed.after(c, PAIRS * (t + 1)))
                    V.tensor_tensor(mf[:, :], g_ps, mx[:, :], ALU.max).then_inc(mf_done.sem, 1)
                    dve.wait_ge(mf_done.sem, mf_done.after(c, t + 1))
                    dve.wait_ge(mst_done.sem, mst_done.after(c, t))
                    V.tensor_scalar(ms[:, 0:HEADS], mf[:, :], -1.0, None, ALU.mult).then_inc(ms_hi.sem, 1)
                    dve.wait_ge(ms_hi.sem, ms_hi.after(c, t + 1))
                    V.scalar_tensor_tensor(out=ms[:, 32:48], in0=mf[:, :], scalar=-1.0, in1=ms[:, 0:HEADS],
                                           op0=ALU.mult, op1=ALU.subtract).then_inc(ms_lo.sem, 1)
                    dve.wait_ge(pg_done.sem, pg_done.after(c, t))
                    V.tensor_tensor(eg[:, :], g_ps, ms[:, 0:HEADS], ALU.add).then_inc(e_part.sem, 1)
                    dve.wait_ge(e_part.sem, e_part.after(c, t + 1))
                    dve.wait_ge(ms_lo.sem, ms_lo.after(c, t + 1))
                    near = near0[:, 1:2] if t == 0 else near0[:, 0:1]
                    V.scalar_tensor_tensor(out=eg[:, :], in0=eg[:, :], scalar=near, in1=ms[:, 32:48],
                                           op0=ALU.add, op1=ALU.add).then_inc(e_done.sem, 1)
                if s == 2 and (at := place(b, s, LAG["scores"])):
                    c = at[0]
                    dve.wait_ge(kst_copied.sem, kst_copied.after(c, 1))
                    dve.wait_ge(g_done.sem, g_done.after(c, 0))
                    V.tensor_copy(k0[:, :], k_st[:, :, HALF_W]).then_inc(k0_copied.sem, 1)
                    dve.wait_ge(qst_copied.sem, qst_copied.after(c, 2))
                    dve.wait_ge(s0_done.sem, s0_done.after(c, 0))
                    V.tensor_copy(z_st[0:64, 0:PAIRS * HEADS:HEADS + 2], q_ev[0:64, :, HALF_W])
                    V.tensor_copy(z_st[64:P, 1:PAIRS * HEADS:HEADS + 2], q_od[64:P, :, HALF_W])\
                        .then_inc(z_copied.sem, 1)

                def stats():
                    if at := place(b, s, LAG["stats"]):
                        c, t = at
                        dve.wait_ge(x_loaded[t].sem, x_loaded[t].after(c, 1))
                        V.bn_stats(st[:, t % 2, :], x_in[:, t, :]).then_inc(stats_raw.sem, 1)
                        dve.wait_ge(stats_raw.sem, stats_raw.after(c, t + 1))
                        dve.sem_inc(passed, 1)
                        V.bn_aggr(mv[:, t % 2, :], st[:, t % 2, :]).then_inc(stats_done.sem, 1)

                def norm():
                    if at := place(b, s, LAG["norm"]):
                        c, t = at
                        dve.wait_ge(rstd_done.sem, rstd_done.after(c, t + 1))
                        dve.wait_ge(spread.sem, spread.after(c, t - 1))
                        V.tensor_scalar(xn[:, t % 2, :], x_in[:, t, :], mv[:, t % 2, 0:1], rs[:, t % 2:t % 2 + 1],
                                        ALU.subtract, ALU.mult).then_inc(normed.sem, 1)

                def maxima(p):
                    if at := place(b, s, LAG["scores"]):
                        c, t = at
                        n = PAIRS * t + p
                        dve.wait_ge(scored.sem, scored.after(c, n + 1))
                        if p == 0:
                            dve.wait_ge(mf_done.sem, mf_done.after(c, t))
                        V.tensor_reduce(mx[:, 2 * p:2 * p + 2],
                                        bank_s[p % 2][:, 0:2 * WIN].rearrange("p (h k) -> p h k", h=2),
                                        AX.X, ALU.max).then_inc(maxed.sem, 1)

                def split_qk():
                    if at := place(b, s, LAG["project"]):
                        c, t = at
                        dve.wait_ge(qk_hi.sem, qk_hi.after(c, t + 1))
                        wide = [P, HEADS, 2, HD]
                        V.tensor_tensor(q_tok[:, :, 1:4:2, :], qk_ps[:, 0].unsqueeze(2).to_broadcast(wide),
                                        q_tok[:, :, 0:4:2, :], ALU.subtract)
                        V.tensor_tensor(k_tok[:, :, 2:4, :], qk_ps[:, 1].unsqueeze(2).to_broadcast(wide),
                                        k_tok[:, :, 0:2, :], ALU.subtract).then_inc(qk_split.sem, 1)

                def shift_rows():
                    if at := place(b, s, LAG["maxima"]):
                        c, t = at
                        dve.wait_ge(mst_done.sem, mst_done.after(c, t + 1))
                        V.tensor_copy(ms_t[0:48, cols(t)], mst_ps[0:48, 0:P]).then_inc(mst_copied.sem, 1)

                def copy_k():
                    if at := place(b, s, LAG["project"]):
                        c, t = at
                        dve.wait_ge(kst_done.sem, kst_done.after(c, t + 1))
                        if t == 0:
                            dve.wait_ge(s0_done.sem, s0_done.after(c, 0))
                        V.tensor_copy(k_st[:, :, cols(t)], kst_ps).then_inc(kst_copied.sem, 1)

                def split_o():
                    if at := place(b, s, LAG["out"]):
                        c, t = at
                        dve.wait_ge(ot_hi_done.sem, ot_hi_done.after(c, t + 1))
                        V.tensor_tensor(ot_lo[:, :, :], tr_ps, ot_hi[:, :, :], ALU.subtract).then_inc(ot_split.sem, 1)

                def split_x():
                    if at := place(b, s, LAG["spread"]):
                        c, t = at
                        dve.wait_ge(xt_hi_done.sem, xt_hi_done.after(c, t + 1))
                        V.tensor_tensor(xt_lo[:, :, :], tr_ps, xt_hi[:, :, :], ALU.subtract).then_inc(xt_split.sem, 1)

                def add_o(half):
                    if at := place(b, s, LAG["weigh"]):
                        c, t = at
                        dve.wait_ge(valued.sem, valued.after(c, 2 * t + half + 1))
                        src = bank_o[:, :].rearrange("p (g w) -> p g w", g=2)
                        dst = o_acc[:, 2 * half:2 * half + 2, s_of(t):s_of(t) + 2 * HALF_W]
                        dve.wait_ge(o_copied.sem, o_copied.after(c, 2 * t + half - 1))
                        if t == 0:
                            dve.wait_ge(gat_done.sem, gat_done.after(c, 2 - NB))
                            V.tensor_copy(dst, src[:, :, 0:2 * HALF_W]).then_inc(added.sem, 1)
                        else:
                            V.tensor_tensor(dst, src[:, :, 0:2 * HALF_W], dst, ALU.add).then_inc(added.sem, 1)

                def sums():
                    if at := place(b, s, LAG["gather"]):
                        c, t = at
                        dve.wait_ge(gat_done.sem, gat_done.after(c, t + 1))
                        dve.wait_ge(pg_done.sem, pg_done.after(c, t + 1))
                        V.tensor_tensor(den[:, :], gat_ps[:, :, HD], pg[:, t, :], ALU.add).then_inc(den_done.sem, 1)
                        dve.wait_ge(pgv_done.sem, pgv_done.after(c, t + 1))
                        dve.wait_ge(o_done.sem, o_done.after(c, t))
                        V.tensor_tensor(onum[:, :, :], gat_ps[:, :, 0:HD], pgv[:, :, :], ALU.add)
                        dve.wait_ge(den_done.sem, den_done.after(c, t + 1))
                        V.reciprocal(rec[:, :], den[:, :]).then_inc(num_done.sem, 1)

                def residual():
                    if at := place(b, s, LAG["out"]):
                        c, t = at
                        dve.wait_ge(wo_done.sem, wo_done.after(c, t + 1))
                        dve.wait_ge(res_loaded[t % 4].sem, res_loaded[t % 4].after(c, t // 4 + 1))
                        dve.wait_ge(y_stored[t % 2].sem, y_stored[t % 2].after(c, t // 2))
                        V.tensor_tensor(y_sb[:, t % 2, :], wo_ps, x_res[:, t % 4, :], ALU.add)\
                            .then_inc(y_ready.sem, 1)

                def copy_v0():
                    if s == 7 and (at := place(b, s, 7)):
                        c = at[0]
                        dve.wait_ge(v0_done.sem, v0_done.after(c, 1))
                        dve.wait_ge(pgv_done.sem, pgv_done.after(c, 0))
                        V.tensor_copy(v0[:, :, :], bank_m[:, 0:D].rearrange("p (h d) -> p h d", h=HEADS))\
                            .then_inc(v0_copied.sem, 1)

                copy_v0()
                maxima(0)
                split_qk()
                maxima(1)
                split_o()
                maxima(2)
                copy_k()
                shift_rows()
                maxima(3)
                stats()
                maxima(4)
                sums()
                add_o(0)
                maxima(5)
                residual()
                norm()
                maxima(6)
                maxima(7)
                split_x()
                add_o(1)
                if s == 0 and (at := place(b, s, NB)):
                    c = at[0]
                    dve.wait_ge(s0_copied.sem, s0_copied.after(c, 2))
                    V.tensor_reduce(m0[:, :], s0[:, :], AX.X, ALU.max).then_inc(m0_done.sem, 1)
                    dve.wait_ge(m0_done.sem, m0_done.after(c, 1))
                    V.tensor_scalar(nb0[:, :], m0[:, :], -SCALE, None, ALU.mult).then_inc(nb0_done.sem, 1)
                if s == 1 and (at := place(b, s, NB)):
                    c = at[0]
                    dve.wait_ge(p0_done.sem, p0_done.after(c, 1))
                    V.reciprocal(r0[:, :], l0[:, :]).then_inc(r0_done.sem, 1)
                    dve.wait_ge(o0_done.sem, o0_done.after(c, 1))
                    dve.wait_ge(r0_done.sem, r0_done.after(c, 1))
                    V.scalar_tensor_tensor(out=o0_all[:, :], in0=bank_m[0:HEADS, 0:D], scalar=r0[:, 0:1],
                                           in1=own[:, :, :].rearrange("p h d -> p (h d)"),
                                           op0=ALU.mult, op1=ALU.mult).then_inc(o0_scaled.sem, 1)

            def s_of(t):
                return t * P
            turns(dve, slot)
            dve.wait_ge(fin, 2)
            V.tensor_tensor(ot_lo[:, :, 0:batches], tr_ps[:, :, 0:batches], ot_hi[:, :, 0:batches],
                            ALU.subtract).then_inc(fin, 1)
            dve.wait_ge(fin, 4)
            dve.wait_ge(fin_dma, 32)
            V.tensor_tensor(y0_rows[:, :], wo_ps[0:batches, :], x0_rows[:, :], ALU.add).then_inc(fin, 1)

        @block.scalar
        def _(act):
            A = nc.scalar
            for n in range(4):
                act.wait_ge(w_in, 64)
                A.activation(whi[:, :, n, :], wstage[:, :, n, :], ACT.Copy).then_inc(w_hi_done, 1)
            act.wait_ge(setup, 13)

            def slot(b, s):
                def exps(p):
                    if at := place(b, s, LAG["weigh"]):
                        c, t = at
                        n = PAIRS * t + p
                        act.wait_ge(weighed.sem, weighed.after(c, n + 1))
                        act.wait_ge(valued.sem, valued.after(c, 2 * t + (p // 4) - (1 if p % 4 < 4 else 0)))
                        A.activation(pt[:, p % 4, :, :], bank_w[p % 2][:, 0:2 * WIN]
                                     .rearrange("p (h k) -> p h k", h=2), ACT.Exp, scale=SCALE)\
                            .then_inc(exped.sem, 1)

                def qk_high():
                    if at := place(b, s, LAG["project"]):
                        c, t = at
                        act.wait_ge(qk_done.sem, qk_done.after(c, t + 1))
                        wide = [P, HEADS, 2, HD]
                        act.wait_ge(qst_done.sem, qst_done.after(c, t))
                        act.wait_ge(kst_done.sem, kst_done.after(c, t))
                        A.activation(q_tok[:, :, 0:4:2, :], qk_ps[:, 0].unsqueeze(2).to_broadcast(wide), ACT.Copy)
                        A.activation(k_tok[:, :, 0:2, :], qk_ps[:, 1].unsqueeze(2).to_broadcast(wide), ACT.Copy)\
                            .then_inc(qk_hi.sem, 1)

                def copy_v():
                    if at := place(b, s, LAG["project"]):
                        c, t = at
                        act.wait_ge(v_done.sem, v_done.after(c, t + 1))
                        if t < 2:
                            act.wait_ge(v_kept.sem, v_kept.after(c, 0))
                        else:
                            act.wait_ge(o0_done.sem, o0_done.after(c, 0))
                        act.wait_ge(v0_done.sem, v0_done.after(c, 0))
                        A.activation(v_sb[:, t, :, 0:HD], v_ps, ACT.Copy).then_inc(v_copied.sem, 1)

                def copy_q():
                    if at := place(b, s, LAG["project"]):
                        c, t = at
                        act.wait_ge(qst_done.sem, qst_done.after(c, t + 1))
                        if t == 0:
                            act.wait_ge(z_copied.sem, z_copied.after(c, 0))
                        A.activation(q_ev[0:64, :, cols(t)], qst_ps[0:64], ACT.Copy).then_inc(qst_copied.sem, 1)
                        A.activation(q_od[64:P, :, cols(t)], qst_ps[64:P], ACT.Copy).then_inc(qst_copied.sem, 1)

                def o_high():
                    if at := place(b, s, LAG["out"]):
                        c, t = at
                        act.wait_ge(otr_done.sem, otr_done.after(c, t + 1))
                        act.wait_ge(wo_done.sem, wo_done.after(c, t))
                        A.activation(ot_hi[:, :, :], tr_ps, ACT.Copy).then_inc(ot_hi_done.sem, 1)

                def x_high():
                    if at := place(b, s, LAG["spread"]):
                        c, t = at
                        act.wait_ge(spread.sem, spread.after(c, t + 1))
                        act.wait_ge(v_done.sem, v_done.after(c, t))
                        A.activation(xt_hi[:, :, :], tr_ps, ACT.Copy).then_inc(xt_hi_done.sem, 1)

                def weight0():
                    if at := place(b, s, LAG["maxima"]):
                        c, t = at
                        act.wait_ge(e_done.sem, e_done.after(c, t + 1))
                        act.wait_ge(num_done.sem, num_done.after(c, t + 1 - NB))
                        A.activation(pg[:, t, :], eg[:, :], ACT.Exp, scale=SCALE).then_inc(pg_done.sem, 1)

                def copy_o(half):
                    if at := place(b, s, LAG["weigh"]):
                        c, t = at
                        act.wait_ge(added.sem, added.after(c, 2 * t + half + 1))
                        src = bank_o[:, :].rearrange("p (g w) -> p g w", g=2)
                        act.wait_ge(gat_done.sem, gat_done.after(c, t + 2 - NB))
                        A.activation(o_acc[:, 2 * half:2 * half + 2, t * P + 2 * HALF_W:t * P + WIN],
                                     src[:, :, 2 * HALF_W:WIN], ACT.Copy).then_inc(o_copied.sem, 1)

                last = place(b, s, NB)
                if s == 0 and last:
                    c = last[0]
                    for half in range(2):
                        act.wait_ge(s0_done.sem, s0_done.after(c, half + 1))
                        A.activation(s0[:, half * 512:(half + 1) * 512], bank_m[0:HEADS, :], ACT.Copy)\
                            .then_inc(s0_copied.sem, 1)
                weight0()
                exps(0)
                qk_high()
                exps(1)
                o_high()
                copy_v()
                exps(2)
                exps(3)
                copy_q()
                exps(4)
                copy_o(0)
                exps(5)
                exps(6)
                exps(7)
                x_high()
                if s == 0 and last:
                    c = last[0]
                    act.wait_ge(nb0_done.sem, nb0_done.after(c, 1))
                    act.wait_ge(p0t_done.sem, p0t_done.after(c, 0))
                    act.wait_ge(r0_done.sem, r0_done.after(c, 0))
                    A.activation(p0[:, :], s0[:, :], ACT.Exp, bias=nb0[:, 0:1], scale=SCALE, accum_out=l0[:, 0:1])\
                        .then_inc(p0_done.sem, 1)
                if s == 1 and last:
                    c = last[0]
                    act.wait_ge(p0t_done.sem, p0t_done.after(c, 1))
                    A.activation(p0_t[:, :, :], bank_m[:, 0:P].rearrange("p (k h) -> p k h", k=NB), ACT.Copy)\
                        .then_inc(p0t_copied.sem, 1)
                copy_o(1)
                if s == 1 and last:
                    c = last[0]
                    act.wait_ge(o0_sum.sem, o0_sum.after(c, 1))
                    act.wait_ge(o0_stored.sem, o0_stored.after(c, 0))
                    A.activation(o0[:, :], bank_m[0:1, 0:D], ACT.Copy).then_inc(o0_copied.sem, 1)
            turns(act, slot)
            act.wait_ge(fin, 1)
            A.activation(ot_hi[:, :, 0:batches], tr_ps[:, :, 0:batches], ACT.Copy).then_inc(fin, 1)

        @block.tensor
        def _(pe):
            T = nc.tensor
            pe.wait_ge(w_lo_done, 4)
            pe.wait_ge(setup, 13)

            def halves(out, left_hi, left_lo, n):
                last = None
                for f in range(FT):
                    for k, (l, w) in enumerate(((left_hi, whi), (left_hi, wlo), (left_lo, whi))):
                        last = T.matmul(out, l[:, f, :], w[:, f, n, :], start=f == k == 0,
                                        stop=f == FT - 1 and k == 2)
                return last

            def slot(b, s):
                last = place(b, s, NB)
                if s == 0 and last:
                    c = last[0]
                    pe.wait_ge(z_copied.sem, z_copied.after(c, 1))
                    pe.wait_ge(kst_copied.sem, kst_copied.after(c, NB))
                    prev = place(b, s, LAG["maxima"])
                    pe.wait_ge(e_part.sem, e_part.after(prev[0], prev[1] + 1))
                    for half in range(2):
                        pe.wait_ge(s0_copied.sem, s0_copied.after(c, half))
                        for j in range(PAIRS):
                            mm = T.matmul(bank_m[0:HEADS, :], z_st[:, j * HEADS:(j + 1) * HEADS],
                                          k_st[:, j, HALF_W + half * 512:HALF_W + (half + 1) * 512],
                                          start=j == 0, stop=j == PAIRS - 1)
                        mm.then_inc(s0_done.sem, 1)

                def project():
                    if at := place(b, s, LAG["project"]):
                        c, t = at
                        pe.wait_ge(xt_split.sem, xt_split.after(c, t + 1))
                        pe.wait_ge(num_done.sem, num_done.after(c, t - LAG["gather"]))
                        halves(bank_qk[:, :], xt_hi, xt_lo, slice(0, 2)).then_inc(qk_done.sem, 1)
                        if prev := place(b, s - 1, LAG["out"]):
                            pe.wait_ge(y_ready.sem, y_ready.after(prev[0], prev[1] + 1))
                        halves(bank_v[:, 0:D], xt_hi, xt_lo, 2).then_inc(v_done.sem, 1)

                def scores(p):
                    if at := place(b, s, LAG["scores"]):
                        c, t = at
                        n = PAIRS * t + p
                        bank = bank_s[p % 2]
                        variant = 1 if t == 0 else 2 if t == NB - 1 else 0
                        if p == 0:
                            pe.wait_ge(kst_copied.sem, kst_copied.after(c, min(t + 2, NB)))
                            pe.wait_ge(qst_copied.sem, qst_copied.after(c, 2 * (t + 1)))
                        pe.wait_ge(maxed.sem, maxed.after(c, n - 1))
                        for i, q in enumerate((q_ev, q_od)):
                            T.matmul(bank[:, i * WIN:(i + 1) * WIN], q[:, p, cols(t)],
                                     k_st[:, p, cols(t, HALF_W)], start=i == 0, stop=False,
                                     skip_group_check=True)
                        T.matmul(bank[:, 0:2 * WIN], idb[:, :],
                                 band[:, variant, :].unsqueeze(1).to_broadcast([P, 2, WIN]), start=False, stop=True,
                                 skip_group_check=True).then_inc(scored.sem, 1)

                def weigh(p):
                    if at := place(b, s, LAG["weigh"]):
                        c, t = at
                        n = PAIRS * t + p
                        bank = bank_w[p % 2]
                        if p == 0:
                            pe.wait_ge(mst_copied.sem, mst_copied.after(c, min(t + 2, NB)))
                            pe.wait_ge(qst_copied.sem, qst_copied.after(c, 2 * min(t + 2, NB)))
                        pe.wait_ge(exped.sem, exped.after(c, n - 1))
                        for i, q in enumerate((q_ev, q_od)):
                            T.matmul(bank[:, i * WIN:(i + 1) * WIN], k_st[:, p, cols(t)],
                                     q[:, p, cols(t, HALF_W)], start=i == 0, stop=False,
                                     skip_group_check=True)
                        for i in range(2):
                            T.matmul(bank[:, i * WIN:(i + 1) * WIN], pick[:, 2 * p + i, :],
                                     ms_t[:, cols(t, HALF_W)], start=False, stop=False, skip_group_check=True)
                        T.matmul(bank[:, 0:2 * WIN], idb[:, :],
                                 band[:, 0, :].unsqueeze(1).to_broadcast([P, 2, WIN]), start=False, stop=True,
                                 skip_group_check=True).then_inc(weighed.sem, 1)

                def values(g):
                    if at := place(b, s, LAG["weigh"]):
                        c, t = at
                        if g == 0:
                            pe.wait_ge(v_copied.sem, v_copied.after(c, t + 1))
                        if g % 2 == 0:
                            pe.wait_ge(o_copied.sem, o_copied.after(c, 2 * t + g // 2))
                        pe.wait_ge(exped.sem, exped.after(c, PAIRS * t + 2 * g + 2))
                        for i in range(4):
                            h = 4 * g + i
                            mm = T.matmul(bank_o[32 * i:32 * i + 32, (g % 2) * 256:(g % 2) * 256 + WIN],
                                          v_sb[:, t, h, :], pt[:, (h // 2) % 4, h % 2, :], start=True, stop=True)
                        if g % 2:
                            mm.then_inc(valued.sem, 1)

                def rows_of_o():
                    if at := place(b, s, LAG["out"]):
                        c, t = at
                        pe.wait_ge(o_done.sem, o_done.after(c, t + 1))
                        if prev := place(b, s, LAG["maxima"]):
                            pe.wait_ge(e_part.sem, e_part.after(prev[0], prev[1] + 1))
                        if s == 0:
                            pe.wait_ge(s0_copied.sem, s0_copied.after(c, 2))
                        for f in range(FT):
                            mm = T.transpose(tr_ps[:, f, :], o_tok[:, 8 * f:8 * f + 8, :].rearrange("p h d -> p (h d)"),
                                             id32[:, :])
                        mm.then_inc(otr_done.sem, 1)

                def shift_rows():
                    if at := place(b, s, LAG["maxima"]):
                        c, t = at
                        pe.wait_ge(ms_lo.sem, ms_lo.after(c, t + 1))
                        pe.wait_ge(e_part.sem, e_part.after(c, t + 1))
                        if prev := place(b, s, LAG["out"]):
                            pe.wait_ge(ot_split.sem, ot_split.after(prev[0], prev[1] + 1))
                        pe.sem_inc(passed, 1)
                        T.transpose(mst_ps[0:48, 0:P], ms[:, :], idb[:, :]).then_inc(mst_done.sem, 1)

                def stack_k():
                    if at := place(b, s, LAG["project"]):
                        c, t = at
                        pe.wait_ge(qk_split.sem, qk_split.after(c, t + 1))
                        for j in range(PAIRS):
                            mm = T.transpose(kst_ps[:, j, :], k_tok[:, 2 * j:2 * j + 2].rearrange("p h r d -> p (h r d)"),
                                             id16[:, :])
                        mm.then_inc(kst_done.sem, 1)

                def stack_q():
                    if at := place(b, s, LAG["project"]):
                        c, t = at
                        pe.wait_ge(v_copied.sem, v_copied.after(c, t + 1))
                        for j in range(PAIRS):
                            mm = T.transpose(qst_ps[:, j, :], q_tok[:, 2 * j:2 * j + 2].rearrange("p h r d -> p (h r d)"),
                                             id16[:, :])
                        mm.then_inc(qst_done.sem, 1)

                def gather():
                    if at := place(b, s, LAG["gather"]):
                        c, t = at
                        pe.wait_ge(o_copied.sem, o_copied.after(c, 2 * min(t + 2, NB)))
                        if prev := place(b, s, LAG["project"]):
                            pe.wait_ge(kst_copied.sem, kst_copied.after(prev[0], prev[1] + 1))
                        for g in range(4):
                            mm = T.transpose(bank_qk[:, g * P:(g + 1) * P], o_acc[:, g, cols(t)], id32[:, :])
                        mm.then_inc(gat_done.sem, 1)

                def out():
                    if at := place(b, s, LAG["out"]):
                        c, t = at
                        pe.wait_ge(ot_split.sem, ot_split.after(c, t + 1))
                        if prev := place(b, s, LAG["project"]):
                            pe.wait_ge(qst_copied.sem, qst_copied.after(prev[0], 2 * (prev[1] + 1)))
                        halves(wo_ps, ot_hi, ot_lo, 3).then_inc(wo_done.sem, 1)

                def spread_x():
                    if at := place(b, s, LAG["spread"]):
                        c, t = at
                        pe.wait_ge(normed.sem, normed.after(c, t + 1))
                        if prev := place(b, s, LAG["maxima"]):
                            pe.wait_ge(mst_copied.sem, mst_copied.after(prev[0], prev[1] + 1))
                        if prev := place(b, s, LAG["out"]):
                            pe.wait_ge(ot_split.sem, ot_split.after(prev[0], prev[1] + 1))
                        for f in range(FT):
                            mm = T.transpose(tr_ps[:, f, :], xn[:, t % 2, f * P:(f + 1) * P], id32[:, :])
                        mm.then_inc(spread.sem, 1)

                def key0():
                    if at := place(b, s, LAG["scores"]):
                        c, t = at
                        pe.wait_ge(k0_copied.sem, k0_copied.after(c, 1))
                        if prev := place(b, s, LAG["spread"]):
                            pe.wait_ge(xt_split.sem, xt_split.after(prev[0], prev[1] + 1))
                        for j in range(PAIRS):
                            for i, q in enumerate((q_ev, q_od)):
                                mm = T.matmul(g_ps[:, 2 * j + i:2 * j + i + 1], q[:, j, cols(t)], k0[:, j:j + 1],
                                              start=True, stop=True)
                        mm.then_inc(g_done.sem, 1)

                def first_values():
                    if s == 7 and (at := place(b, s, 7)):
                        c = at[0]
                        if prev := place(b, s, LAG["maxima"]):
                            pe.wait_ge(e_part.sem, e_part.after(prev[0], prev[1] + 1))
                        pe.wait_ge(v_copied.sem, v_copied.after(c, 1))
                        T.matmul(bank_m[:, 0:D], first_row[:, :], v_sb[:, 0, :, 0:HD], start=True, stop=True)\
                            .then_inc(v0_done.sem, 1)
                        pe.wait_ge(v0_copied.sem, v0_copied.after(c, 1))

                first_values()
                project()
                scores(0), weigh(0)
                rows_of_o()
                scores(1), weigh(1)
                stack_k()
                shift_rows()
                scores(2), weigh(2)
                stack_q()
                scores(3), weigh(3)
                values(0)
                gather()
                scores(4), weigh(4)
                out()
                scores(5), weigh(5)
                values(1)
                scores(6), weigh(6)
                scores(7), weigh(7)
                values(2)
                spread_x()
                if not (s == 1 and last):
                    key0()
                if s == 1 and last:
                    c = last[0]
                    pe.wait_ge(p0_done.sem, p0_done.after(c, 1))
                    if prev := place(b, s, LAG["spread"]):
                        pe.wait_ge(xt_split.sem, xt_split.after(prev[0], prev[1] + 1))
                    pe.sem_inc(passed, 1)
                    for k in range(NB):
                        mm = T.transpose(bank_m[:, k * HEADS:(k + 1) * HEADS], p0[:, k * P:(k + 1) * P],
                                         id32[0:HEADS, 0:HEADS])
                    mm.then_inc(p0t_done.sem, 1)
                    values(3)
                    pe.wait_ge(p0t_copied.sem, p0t_copied.after(c, 1))
                    pe.wait_ge(v_kept.sem, v_kept.after(c, 1))
                    for k in range(NB):
                        v = v_keep[:, k, :, :] if k < 2 else v_sb[:, k, :, 0:HD]
                        mm = T.matmul(bank_m[0:HEADS, 0:D], p0_t[:, k, :], v, start=k == 0, stop=k == NB - 1)
                    mm.then_inc(o0_done.sem, 1)
                    pe.wait_ge(o0_scaled.sem, o0_scaled.after(c, 1))
                    pe.sem_inc(passed, 1)
                    T.matmul(bank_m[0:1, 0:D], one_col[:, :], o0_all[:, :], start=True, stop=True)\
                        .then_inc(o0_sum.sem, 1)
                    pe.wait_ge(o0_copied.sem, o0_copied.after(c, 1))
                    key0()
                else:
                    values(3)
            turns(pe, slot)
            pe.wait_ge(fin_dma, 32)
            for f in range(FT):
                mm = T.transpose(tr_ps[:, f, 0:batches], o0_rows[:, f * P:(f + 1) * P], id32[0:batches, 0:batches])
            mm.then_inc(fin, 1)
            pe.wait_ge(fin, 3)
            for f in range(FT):
                for k, (l, w) in enumerate(((ot_hi, whi), (ot_hi, wlo), (ot_lo, whi))):
                    mm = T.matmul(wo_ps[0:batches, :], l[:, f, 0:batches], w[:, f, 3, :], start=f == k == 0,
                                  stop=f == FT - 1 and k == 2)
            mm.then_inc(fin, 1)


EXPERTS, TOP, FF = 7, 2, 1024
FC = FF // P
CAPACITY = 732
SUB = 122
CHUNK_BLOCKS = 3
SLOT_BLOCKS = CAPACITY // SUB
NOWHERE = 1 << 20


class Weights:

    def __init__(self, sb):
        self.stage_up = sb("stage_up", [P, 2, FT, FF], F32)
        self.stage_down = sb("stage_down", [P, FC, D], F32)
        self.up_hi = sb("up_hi", [P, 2, FT, FF], FP16)
        self.up_lo = sb("up_lo", [P, 2, FT, FF], FP16)
        self.down_hi = sb("down_hi", [P, FC, D], FP16)
        self.down_lo = sb("down_lo", [P, FC, D], FP16)

    def load(self, sp, w1, w3, w2, done):
        sp.dma_start(self.stage_up[:, 0], w1.rearrange("(f p) o -> p f o", p=P)).then_inc(done, 16)
        sp.dma_start(self.stage_up[:, 1], w3.rearrange("(f p) o -> p f o", p=P)).then_inc(done, 16)
        sp.dma_start(self.stage_down[:, :, :], w2.rearrange("(f p) o -> p f o", p=P)).then_inc(done, 16)


def shared_ffn(nc, W, persist, w_loaded, y, g, b_, wr, ew1, ew3, ew2, z, out, ew_loaded):
    batches = y.shape[0]
    NCH = 2
    CT = 512
    CB = CT // P
    y_v = y.rearrange("b (s j p) d -> b s p j d", p=P, j=CB)
    z_v = z.rearrange("(b s j p) d -> b s p j d", p=P, j=CB, s=NCH)
    out_v = out.rearrange("b (s j p) d -> b s p j d", p=P, j=CB)
    logits, gcol, bcol, wr_hi, wr_lo, id32 = persist

    ctx = ExitStack()
    with nc.cleanup_on_exit(), ctx:
        sb, ps = tensors(ctx, nc)
        signals = []

        def sig(name, per=NCH, unit=1):
            s = Signal(nc, name, per, unit)
            signals.append(s)
            return s

        y_in = sb("f_y_in", [P, 2, CB, D], F32)
        st = sb("f_st", [P, CB, 6], F32)
        mv = sb("f_mv", [P, CB, 2], F32)
        mhalf = sb("f_mhalf", [P, CB], F32)
        tmp = sb("f_tmp", [P, 6, CB], F32)
        fac = sb("f_fac", [P, CB], F32)
        z_sb = sb("f_z_sb", [P, CB, D], F32)
        h32 = sb("f_h32", [P, FT, CT], F32)
        h_hi = sb("f_h_hi", [P, 2, FT, CT], FP16)
        h_lo = sb("f_h_lo", [P, 2, FT, CT], FP16)
        th = sb("f_th", [P, 2, CT], F32)
        u = sb("f_u", [P, 2, CT], F32)
        g32 = sb("f_g32", [P, 3, CT], F32)
        g_hi = sb("f_g_hi", [P, FC, CT], FP16)
        g_lo = sb("f_g_lo", [P, FC, CT], FP16)
        o_sb = sb("f_o_sb", [P, CB, D], F32)
        wr32 = sb("f_wr32", [P, FT, EXPERTS], F32)

        bank_a = [ps(f"f_bank_a{i}", [P, CT]) for i in range(2)]
        bank_b = [ps(f"f_bank_b{i}", [P, CT]) for i in range(2)]
        bank_d = [ps(f"f_bank_d{i}", [P, CT]) for i in range(2)]
        bank_t = [ps(f"f_bank_t{i}", [P, CT]) for i in range(2)]

        small = nc.alloc_semaphore("f_small")
        small_ready = nc.alloc_semaphore("f_small_ready")
        w_ready = nc.alloc_semaphore("f_w_ready")
        w_high = nc.alloc_semaphore("f_w_high")
        setup = nc.alloc_semaphore("f_setup")
        passed = nc.alloc_semaphore("f_passed")
        y_loaded = [sig(f"f_y_loaded{i}", 1, 16) for i in range(2)]
        z_stored = sig("f_z_stored", NCH, 16)
        o_stored = sig("f_o_stored", NCH, 16)
        (stats_raw, stats_done, pv1, pv2, pv3, pv4, pv5, pv6, fac_done, z_ready, h_hi_done, h_done,
         logit_done, logit_copied, o_ready) = [sig("f_" + n) for n in (
             "stats_raw", "stats_done", "pv1", "pv2", "pv3", "pv4", "pv5", "pv6", "fac_done", "z_ready",
             "h_hi_done", "h_done", "logit_done", "logit_copied", "o_ready")]
        turned = sig("f_turned", FT * NCH)
        h32_done = sig("f_h32_done", FT * NCH)
        (up_a, up_b, gated, u_done, g_done, g_hi_done, g_split, down_done) = [sig("f_" + n, FC * NCH) for n in (
            "up_a", "up_b", "gated", "u_done", "g_done", "g_hi_done", "g_split", "down_done")]
        block = ctx.enter_context(nc.Block())

        def place(b, s, lag):
            q = s - lag
            batch = b + q // NCH
            if isinstance(b, int) and not 0 <= batch < batches:
                return None
            return batch, q % NCH

        def turns(engine, body):
            body(0, -1)
            for s in range(NCH):
                body(0, s)
            with engine.Fori(1, batches - 1) as b:
                for s in range(NCH):
                    body(b, s)
            for s in range(NCH):
                body(batches - 1, s)
            body(batches, 0)

        @block.sync
        def _(sp):
            for s in signals:
                if s.unit == 16:
                    s.start(sp)
            sp.dma_start(wr32[:, :, :], wr.rearrange("(f p) o -> p f o", p=P)).then_inc(small, 16)
            sp.dma_start(gcol[:, :], g).then_inc(small, 16)
            sp.dma_start(bcol[:, :], b_).then_inc(small, 16)

            def slot(b, s):
                if at := place(b, s, -1):
                    c, t = at
                    sp.wait_ge(o_ready.sem, o_ready.after(c, t - 1))
                    sp.sem_inc(passed, 1)
                    sp.dma_start(y_in[:, t], y_v[c, t]).then_inc(y_loaded[t].sem, 16)
                    sp.wait_ge(z_ready.sem, z_ready.after(c, t + 1))
                    sp.dma_start(z_v[c, t], z_sb[:, :, :]).then_inc(z_stored.sem, 16)
                if at := place(b, s, 1):
                    c, t = at
                    sp.wait_ge(o_ready.sem, o_ready.after(c, t + 1))
                    sp.sem_inc(passed, 1)
                    sp.dma_start(out_v[c, t], o_sb[:, :, :]).then_inc(o_stored.sem, 16)
                if isinstance(b, int) and b == 0 and s == 0:
                    sp.wait_ge(w_ready, 3)
                    W.load(sp, ew1[0], ew3[0], ew2[0], ew_loaded)
            turns(sp, slot)
            sp.wait_ge(z_stored.sem, z_stored.after(batches - 1, NCH))
            sp.wait_ge(o_stored.sem, o_stored.after(batches - 1, NCH))
            sp.wait_ge(ew_loaded, 48)

        @block.gpsimd
        def _(pool):
            G = nc.gpsimd
            for s in signals:
                if s.unit == 1:
                    s.start(pool)
            G.memset(mhalf[:, :], -0.5).then_inc(setup, 1)
            pool.wait_ge(setup, 1)

            def slot(b, s):
                def factor():
                    if at := place(b, s, -1):
                        c, t = at
                        n = t + 1
                        var = mv[:, :, 1]
                        pool.wait_ge(stats_done.sem, stats_done.after(c, n))
                        pool.sem_inc(passed, 1)
                        G.tensor_scalar(tmp[:, 0], var, EPS, None, ALU.add).then_inc(pv1.sem, 1)
                        pool.wait_ge(pv1.sem, pv1.after(c, n))
                        G.tensor_tensor(tmp[:, 1], tmp[:, 0], mhalf[:, :], ALU.pow).then_inc(pv2.sem, 1)
                        pool.wait_ge(pv2.sem, pv2.after(c, n))
                        G.tensor_tensor(tmp[:, 2], var, tmp[:, 1], ALU.mult).then_inc(pv3.sem, 1)
                        pool.wait_ge(pv3.sem, pv3.after(c, n))
                        G.tensor_tensor(tmp[:, 3], tmp[:, 2], tmp[:, 1], ALU.mult).then_inc(pv4.sem, 1)
                        pool.wait_ge(pv4.sem, pv4.after(c, n))
                        pool.sem_inc(passed, 1)
                        G.tensor_scalar(tmp[:, 4], tmp[:, 3], EPS, None, ALU.add).then_inc(pv5.sem, 1)
                        pool.wait_ge(pv5.sem, pv5.after(c, n))
                        G.tensor_tensor(tmp[:, 5], tmp[:, 4], mhalf[:, :], ALU.pow).then_inc(pv6.sem, 1)
                        pool.wait_ge(pv6.sem, pv6.after(c, n))
                        G.tensor_tensor(fac[:, :], tmp[:, 5], tmp[:, 1], ALU.mult).then_inc(fac_done.sem, 1)

                def low(f):
                    if at := place(b, s, 0):
                        c, t = at
                        n = FC * t + f
                        pool.wait_ge(g_hi_done.sem, g_hi_done.after(c, n + 1))
                        pool.wait_ge(down_done.sem, down_done.after(c, n + 1 - FC))
                        G.tensor_tensor(g_lo[:, f], g32[:, f % 2], g_hi[:, f], ALU.subtract).then_inc(g_split.sem, 1)

                def low_h():
                    if at := place(b, s, -1):
                        c, t = at
                        pool.wait_ge(h_hi_done.sem, h_hi_done.after(c, t + 1))
                        G.tensor_tensor(h_lo[:, t], h32[:, :, :], h_hi[:, t], ALU.subtract).then_inc(h_done.sem, 1)
                low(0), low(1)
                factor()
                low(2), low(3), low(4)
                low_h()
                low(5), low(6), low(7)
            turns(pool, slot)

        @block.vector
        def _(dve):
            V = nc.vector
            dve.wait_ge(small, 48)
            V.tensor_copy(wr_hi[:, :, :], wr32[:, :, :]).then_inc(small_ready, 1)
            dve.wait_ge(small_ready, 1)
            V.tensor_tensor(wr_lo[:, :, :], wr32[:, :, :], wr_hi[:, :, :], ALU.subtract).then_inc(small_ready, 1)
            dve.wait_ge(w_loaded, 48)
            dve.wait_ge(w_high, 1)
            V.tensor_tensor(W.up_lo[:, 0], W.stage_up[:, 0], W.up_hi[:, 0], ALU.subtract).then_inc(w_ready, 1)
            dve.wait_ge(w_high, 2)
            V.tensor_tensor(W.up_lo[:, 1], W.stage_up[:, 1], W.up_hi[:, 1], ALU.subtract).then_inc(w_ready, 1)
            dve.wait_ge(w_high, 3)
            V.tensor_tensor(W.down_lo[:, :, :], W.stage_down[:, :, :], W.down_hi[:, :, :], ALU.subtract)\
                .then_inc(w_ready, 1)

            def slot(b, s):
                def stats():
                    if at := place(b, s, -1):
                        c, t = at
                        dve.wait_ge(y_loaded[t].sem, y_loaded[t].after(c, 1))
                        for j in range(CB):
                            i = V.bn_stats(st[:, j], y_in[:, t, j])
                        i.then_inc(stats_raw.sem, 1)
                        dve.wait_ge(stats_raw.sem, stats_raw.after(c, t + 1))
                        dve.sem_inc(passed, 1)
                        for j in range(CB):
                            i = V.bn_aggr(mv[:, j], st[:, j])
                        i.then_inc(stats_done.sem, 1)

                def norm():
                    if at := place(b, s, -1):
                        c, t = at
                        dve.wait_ge(fac_done.sem, fac_done.after(c, t + 1))
                        dve.wait_ge(z_stored.sem, z_stored.after(c, t))
                        dve.wait_ge(turned.sem, turned.after(c, FT * t))
                        for j in range(CB):
                            i = V.tensor_scalar(z_sb[:, j], y_in[:, t, j], mv[:, j, 0:1], fac[:, j:j + 1],
                                                ALU.subtract, ALU.mult)
                        i.then_inc(z_ready.sem, 1)

                def gate(f):
                    if at := place(b, s, 0):
                        c, t = at
                        n = FC * t + f
                        dve.wait_ge(gated.sem, gated.after(c, n + 1))
                        dve.wait_ge(g_done.sem, g_done.after(c, n - 1))
                        V.scalar_tensor_tensor(out=u[:, f % 2], in0=th[:, f % 2], scalar=1.0, in1=bank_a[f % 2][:, :],
                                               op0=ALU.add, op1=ALU.mult).then_inc(u_done.sem, 1)
                        dve.wait_ge(u_done.sem, u_done.after(c, n + 1))
                        dve.wait_ge(up_b.sem, up_b.after(c, n + 1))
                        dve.wait_ge(g_split.sem, g_split.after(c, n - 1))
                        V.tensor_tensor(g32[:, f % 2], bank_b[f % 2][:, :], u[:, f % 2], ALU.mult)\
                            .then_inc(g_done.sem, 1)

                def finish():
                    if at := place(b, s, 1):
                        c, t = at
                        dve.wait_ge(down_done.sem, down_done.after(c, FC * (t + 1)))
                        dve.wait_ge(o_stored.sem, o_stored.after(c, t))
                        for i in range(2):
                            ins = V.scalar_tensor_tensor(
                                out=o_sb[:, 2 * i:2 * i + 2].rearrange("p j d -> p (j d)"), in0=bank_d[i][:, :], scalar=0.5,
                                in1=y_in[:, t, 2 * i:2 * i + 2].rearrange("p j d -> p (j d)"),
                                op0=ALU.mult, op1=ALU.add)
                        ins.then_inc(o_ready.sem, 1)

                def keep_logits():
                    if at := place(b, s, -1):
                        c, t = at
                        dve.wait_ge(logit_done.sem, logit_done.after(c, t + 1))
                        n = c * (NCH * CB) + t * CB
                        V.tensor_copy(logits[:, bass.ds(n, CB), :],
                                      bank_t[0][:, 0:CB * 8].rearrange("p (j e) -> p j e", e=8)[:, :, 0:EXPERTS])\
                            .then_inc(logit_copied.sem, 1)
                gate(0), gate(1)
                finish()
                stats()
                gate(2), gate(3)
                norm()
                gate(4), gate(5), gate(6), gate(7)
                keep_logits()
            turns(dve, slot)

        @block.scalar
        def _(act):
            A = nc.scalar
            act.wait_ge(w_loaded, 48)
            A.activation(W.up_hi[:, 0], W.stage_up[:, 0], ACT.Copy).then_inc(w_high, 1)
            A.activation(W.up_hi[:, 1], W.stage_up[:, 1], ACT.Copy).then_inc(w_high, 1)
            A.activation(W.down_hi[:, :, :], W.stage_down[:, :, :], ACT.Copy).then_inc(w_high, 1)
            act.wait_ge(small, 48)

            def slot(b, s):
                def gate(f):
                    if at := place(b, s, 0):
                        c, t = at
                        n = FC * t + f
                        act.wait_ge(up_a.sem, up_a.after(c, n + 1))
                        act.wait_ge(u_done.sem, u_done.after(c, n - 1))
                        A.activation(th[:, f % 2], bank_a[f % 2][:, :], ACT.Tanh, scale=0.5).then_inc(gated.sem, 1)

                def high(f, lag=0):
                    if at := place(b, s, lag):
                        c, t = at
                        n = FC * t + f
                        act.wait_ge(g_done.sem, g_done.after(c, n + 1))
                        act.wait_ge(down_done.sem, down_done.after(c, n + 1 - FC))
                        A.activation(g_hi[:, f], g32[:, f % 2], ACT.Copy).then_inc(g_hi_done.sem, 1)

                def affine():
                    if at := place(b, s, -1):
                        c, t = at
                        for i in range(FT):
                            act.wait_ge(turned.sem, turned.after(c, FT * t + i + 1))
                            act.wait_ge(h_done.sem, h_done.after(c, t))
                            A.activation(h32[:, i], bank_t[i][:, :], ACT.Identity, bias=bcol[:, i:i + 1],
                                         scale=gcol[:, i:i + 1]).then_inc(h32_done.sem, 1)
                        act.wait_ge(h32_done.sem, h32_done.after(c, FT * t + FT))
                        A.activation(h_hi[:, t], h32[:, :, :], ACT.Copy).then_inc(h_hi_done.sem, 1)
                gate(0)
                for f in range(1, FC):
                    gate(f)
                    high(f - 1)
                    if f == 5:
                        affine()
                high(FC - 1)
            turns(act, slot)

        @block.tensor
        def _(pe):
            T = nc.tensor
            pe.wait_ge(w_ready, 3)
            pe.wait_ge(small_ready, 2)

            def slot(b, s):
                def up(f):
                    if at := place(b, s, 0):
                        c, t = at
                        n = FC * t + f
                        if f == 0:
                            pe.wait_ge(h_done.sem, h_done.after(c, t + 1))
                        pe.wait_ge(u_done.sem, u_done.after(c, n - 1))
                        pe.wait_ge(g_done.sem, g_done.after(c, n - 1))
                        for k, (bank, done) in enumerate(((bank_a, up_a), (bank_b, up_b))):
                            for i in range(FT):
                                w_hi = W.up_hi[:, k, i, f * P:(f + 1) * P]
                                w_lo = W.up_lo[:, k, i, f * P:(f + 1) * P]
                                T.matmul(bank[f % 2][:, :], w_hi, h_hi[:, t, i], start=i == 0, stop=False)
                                T.matmul(bank[f % 2][:, :], w_hi, h_lo[:, t, i], start=False, stop=False)
                                mm = T.matmul(bank[f % 2][:, :], w_lo, h_hi[:, t, i], start=False, stop=i == FT - 1)
                            mm.then_inc(done.sem, 1)

                def down(f, lag):
                    if at := place(b, s, lag):
                        c, t = at
                        n = FC * t + f
                        if f == 0:
                            pe.wait_ge(o_ready.sem, o_ready.after(c, t))
                        pe.wait_ge(g_split.sem, g_split.after(c, n + 1))
                        for j in range(CB):
                            o = bank_d[j // 2][:, (j % 2) * D:(j % 2 + 1) * D]
                            tok = slice(j * P, (j + 1) * P)
                            for k, (l, w) in enumerate(((g_hi, W.down_hi), (g_hi, W.down_lo), (g_lo, W.down_hi))):
                                mm = T.matmul(o, l[:, f, tok], w[:, f, :], start=f == k == 0 and j % 2 == 0,
                                              stop=f == FC - 1 and k == 2, skip_group_check=True)
                        mm.then_inc(down_done.sem, 1)

                def turn():
                    if at := place(b, s, -1):
                        c, t = at
                        pe.wait_ge(z_ready.sem, z_ready.after(c, t + 1))
                        pe.wait_ge(logit_copied.sem, logit_copied.after(c, t))
                        for i in range(FT):
                            pe.wait_ge(h32_done.sem, h32_done.after(c, FT * (t - 1) + i + 1))
                            for j in range(CB):
                                mm = T.transpose(bank_t[i][:, j * P:(j + 1) * P], z_sb[:, j, i * P:(i + 1) * P],
                                                 id32[:, :])
                            mm.then_inc(turned.sem, 1)

                def route():
                    if at := place(b, s, -1):
                        c, t = at
                        pe.wait_ge(h_done.sem, h_done.after(c, t + 1))
                        for j in range(CB):
                            tok = slice(j * P, (j + 1) * P)
                            for i in range(FT):
                                for k, (l, w) in enumerate(((h_hi, wr_hi), (h_hi, wr_lo), (h_lo, wr_hi))):
                                    mm = T.matmul(bank_t[0][:, j * 8:j * 8 + EXPERTS], l[:, t, i, tok], w[:, i, :],
                                                  start=i == k == 0, stop=i == FT - 1 and k == 2)
                        mm.then_inc(logit_done.sem, 1)
                up(0)
                down(FC - 2, 1)
                up(1)
                down(FC - 1, 1)
                for f in range(2, FC):
                    up(f)
                    down(f - 2, 0)
                    if f == 5:
                        turn()
                route()
            turns(pe, slot)


def route(nc, logits, gather_rows, scatter_rows, batches):
    TT = logits.shape[1]
    BLOCKS = EXPERTS * SLOT_BLOCKS
    E = EXPERTS
    STEP = 32
    NSTEP = TOP * TT // STEP
    ctx = ExitStack()
    with nc.cleanup_on_exit(), ctx:
        sb, ps = tensors(ctx, nc)
        rank = sb("r_rank", [P, E], F32)
        eq = sb("r_eq", [P, TT, E], F32)
        rk = sb("r_rk", [P, TT, E], F32)
        top = sb("r_top", [P, TT], F32)
        win = sb("r_win", [P, TOP, TT], F32)
        oh = sb("r_oh", [P, TOP, TT, E], BF16)
        left = sb("r_left", [P, TT, E], F32)
        upto = sb("r_upto", [P, P], BF16)
        ones = sb("r_ones", [P, P], BF16)
        run = [sb(f"r_run{i}", [P, TOP * TT, E], F32) for i in range(2)]
        pos = sb("r_pos", [P, TOP * TT, E], F32)
        posn = sb("r_posn", [P, TOP * TT], F32)
        over = sb("r_over", [P, TOP * TT], F32)
        blk = [sb(f"r_blk{i}", [P, TOP * TT], F32) for i in range(2)]
        inner = sb("r_inner", [P, TOP * TT], F32)
        base = sb("r_base", [P, TOP * TT], F32)
        slot_of = sb("r_slot", [P, TOP * TT], F32)
        iota_in = sb("r_iota_in", [P, P], F32)
        iota_bl = sb("r_iota_bl", [P, BLOCKS], F32)
        iota_t = sb("r_iota_t", [P, TOP, TT], F32)
        iota_p = sb("r_iota_p", [P, 1], F32)
        oh_in = sb("r_oh_in", [P, 2, STEP, P], BF16)
        oh_bl = sb("r_oh_bl", [P, 2, STEP, BLOCKS], BF16)
        val = sb("r_val", [P, 2, STEP, 2, BLOCKS], BF16)
        tab = sb("r_tab", [P, 2, BLOCKS], F32)
        tok = sb("r_tok", [P, BLOCKS], F32)
        tok2 = sb("r_tok2", [P, BLOCKS], F32)
        none = sb("r_none", [P, BLOCKS], F32)
        fin = sb("r_fin", [P, 2, BLOCKS], F32)
        banks = [ps(f"r_bank{i}", [P, 512]) for i in range(8)]

        made = nc.alloc_semaphore("r_made")
        raw = nc.alloc_semaphore("r_raw")
        step_done = nc.alloc_semaphore("r_step_done")
        chosen = nc.alloc_semaphore("r_chosen")
        counted = nc.alloc_semaphore("r_counted")
        hot = nc.alloc_semaphore("r_hot")
        placed = nc.alloc_semaphore("r_placed")
        block = ctx.enter_context(nc.Block())

        @block.gpsimd
        def _(pool):
            G = nc.gpsimd
            exact = dict(allow_small_or_imprecise_dtypes=True)
            G.iota(rank[:, :], pattern=[[-1, E]], base=E, channel_multiplier=0, **exact).then_inc(made, 1)
            G.iota(iota_in[:, :], pattern=[[1, P]], base=0, channel_multiplier=0, **exact).then_inc(made, 1)
            G.iota(iota_bl[:, :], pattern=[[1, BLOCKS]], base=0, channel_multiplier=0, **exact).then_inc(made, 1)
            G.iota(iota_t[:, :, :], pattern=[[0, TOP], [1, TT]], base=1, channel_multiplier=0, **exact)\
                .then_inc(made, 1)
            G.iota(iota_p[:, :], pattern=[[0, 1]], base=0, channel_multiplier=1, **exact).then_inc(made, 1)
            G.memset(ones[:, :], 1.0).then_inc(made, 1)
            G.memset(upto[:, :], 1.0).then_inc(raw, 1)
            pool.wait_ge(raw, 1)
            G.affine_select(out=upto[:, :], in_=upto[:, :], compare_op=ALU.is_ge, fill=0.0, base=0,
                            channel_multiplier=-1, pattern=[[1, P]]).then_inc(made, 1)

        @block.vector
        def _(dve):
            V = nc.vector
            n = [0]

            def link(ins):
                n[0] += 1
                ins.then_inc(step_done, 1)
                dve.wait_ge(step_done, n[0])
            full = [P, TT, E]
            dve.wait_ge(made, 7)
            rank_b = rank[:, :].unsqueeze(1).to_broadcast(full)
            src = logits
            for k in range(TOP):
                link(V.tensor_reduce(top[:, :], src[:, :, :], AX.X, ALU.max))
                link(V.tensor_tensor(eq[:, :, :], src[:, :, :], top[:, :].unsqueeze(2).to_broadcast(full), ALU.is_equal))
                link(V.tensor_tensor(rk[:, :, :], eq[:, :, :], rank_b, ALU.mult))
                link(V.tensor_reduce(win[:, k, :], rk[:, :, :], AX.X, ALU.max))
                link(V.tensor_tensor(oh[:, k], rank_b, win[:, k, :].unsqueeze(2).to_broadcast(full), ALU.is_equal))
                if k == 0:
                    link(V.tensor_scalar(eq[:, :, :], oh[:, 0], MASKED, None, ALU.mult))
                    link(V.tensor_tensor(left[:, :, :], eq[:, :, :], src[:, :, :], ALU.add))
                    src = left
            dve.sem_inc(chosen, 1)
            ALL = TOP * TT
            per = TOP * TT // 4
            dve.wait_ge(counted, 2)
            V.memset(run[0][:, 0:1, :], 0.0)
            for i in range(4):
                lo, hi = i * per, min((i + 1) * per, ALL - 1)
                ins = V.tensor_copy(run[0][:, lo + 1:hi + 1, :],
                                    banks[4 + i][:, 0:(hi - lo) * E].rearrange("p (t e) -> p t e", e=E))
            link(ins)
            a, c, d = 0, 1, 1
            while d < ALL:
                V.tensor_copy(run[c][:, 0:d, :], run[a][:, 0:d, :])
                link(V.tensor_tensor(run[c][:, d:ALL, :], run[a][:, d:ALL, :], run[a][:, 0:ALL - d, :], ALU.add))
                a, c, d = c, a, 2 * d
            for i in range(4):
                ins = V.tensor_tensor(pos[:, i * per:(i + 1) * per, :],
                                      banks[i][:, 0:per * E].rearrange("p (t e) -> p t e", e=E),
                                      run[a][:, i * per:(i + 1) * per, :], ALU.add)
            link(ins)
            link(V.tensor_tensor(run[c][:, :, :], pos[:, :, :], oh[:, :, :, :].rearrange("p k t e -> p (k t) e"),
                                 ALU.mult))
            link(V.tensor_reduce(posn[:, :], run[c][:, :, :], AX.X, ALU.add))
            cur = blk[0]
            link(V.tensor_scalar(cur[:, :], posn[:, :], SUB + 0.5, None, ALU.is_gt))
            for m in range(2, SLOT_BLOCKS):
                nxt = blk[(m + 1) % 2]
                link(V.scalar_tensor_tensor(out=nxt[:, :], in0=posn[:, :], scalar=SUB * m + 0.5, in1=cur[:, :],
                                            op0=ALU.is_gt, op1=ALU.add))
                cur = nxt
            link(V.scalar_tensor_tensor(out=inner[:, :], in0=cur[:, :], scalar=-float(SUB), in1=posn[:, :],
                                        op0=ALU.mult, op1=ALU.add))
            link(V.tensor_scalar(over[:, :], posn[:, :], CAPACITY + 0.5, 1000.0, ALU.is_gt, ALU.mult))
            link(V.tensor_tensor(base[:, :], over[:, :], cur[:, :], ALU.add))
            link(V.scalar_tensor_tensor(out=slot_of[:, :], in0=win[:, :, :].rearrange("p k t -> p (k t)"),
                                        scalar=-float(SLOT_BLOCKS), in1=base[:, :], op0=ALU.mult, op1=ALU.add))
            link(V.tensor_scalar(base[:, :], slot_of[:, :], float(SLOT_BLOCKS * E), None, ALU.add))
            link(V.tensor_scalar(posn[:, :], inner[:, :], -1.0, None, ALU.add))
            for m in range(NSTEP):
                tiles = slice(m * STEP, (m + 1) * STEP)
                if m >= 2:
                    dve.wait_ge(placed, m - 1)
                V.tensor_tensor(oh_in[:, m % 2], posn[:, tiles].unsqueeze(2).to_broadcast([P, STEP, P]),
                                iota_in[:, :].unsqueeze(1).to_broadcast([P, STEP, P]), ALU.is_equal)
                wide = [P, STEP, BLOCKS]
                link(V.tensor_tensor(oh_bl[:, m % 2], base[:, tiles].unsqueeze(2).to_broadcast(wide),
                                     iota_bl[:, :].unsqueeze(1).to_broadcast(wide), ALU.is_equal))
                it = iota_t[:, :, :].rearrange("p k t -> p (k t)")[:, tiles]
                V.tensor_tensor(val[:, m % 2, :, 0, :], oh_bl[:, m % 2], it.unsqueeze(2).to_broadcast(wide), ALU.mult)
                V.tensor_scalar(val[:, m % 2, :, 1, :], oh_bl[:, m % 2], iota_p[:, 0:1], None, ALU.mult)\
                    .then_inc(hot, 1)
            dve.wait_ge(placed, NSTEP)
            link(V.tensor_copy(tab[:, :, :], banks[0][:, 0:2 * BLOCKS].rearrange("p (v k) -> p v k", v=2)))
            link(V.scalar_tensor_tensor(out=tok[:, :], in0=tab[:, 0], scalar=float(P), in1=tab[:, 1],
                                        op0=ALU.mult, op1=ALU.add))
            link(V.tensor_scalar(none[:, :], tab[:, 0], 0.5, None, ALU.is_lt))
            link(V.tensor_scalar(tok2[:, :], tok[:, :], -float(P), None, ALU.add))
            link(V.scalar_tensor_tensor(out=fin[:, 0], in0=none[:, :], scalar=float(P), in1=tok2[:, :],
                                        op0=ALU.mult, op1=ALU.add))
            link(V.scalar_tensor_tensor(out=fin[:, 1], in0=none[:, :], scalar=float(NOWHERE), in1=tok2[:, :],
                                        op0=ALU.mult, op1=ALU.add))
            link(V.tensor_copy(gather_rows[:, :], fin[:, 0]))
            link(V.tensor_copy(scatter_rows[:, :], fin[:, 1]))

        @block.tensor
        def _(pe):
            T = nc.tensor
            pe.wait_ge(chosen, 1)
            flat = oh[:, :, :, :].rearrange("p k t e -> p (k t e)")
            width = TOP * TT * E // 4
            for k, left_m in enumerate((upto, ones)):
                for i in range(4):
                    mm = T.matmul(banks[4 * k + i][:, 0:width], left_m[:, :], flat[:, i * width:(i + 1) * width],
                                  start=True, stop=True)
                mm.then_inc(counted, 1)
            for m in range(NSTEP):
                pe.wait_ge(hot, m + 1)
                for t in range(STEP):
                    mm = T.matmul(banks[0][:, 0:2 * BLOCKS], oh_in[:, m % 2, t], val[:, m % 2, t]
                                  .rearrange("p v k -> p (v k)"), start=m == t == 0,
                                  stop=m == NSTEP - 1 and t == STEP - 1)
                mm.then_inc(placed, 1)


def experts(nc, W, persist, ew1, ew3, ew2, gather_rows, scatter_rows, z, out):
    NCH = 2
    CB = CHUNK_BLOCKS
    CT = CB * SUB
    logits, gcol, bcol, wr_hi, wr_lo, id32 = persist
    out_rows = out.rearrange("b t d -> (b t) d")
    LAST_ROW = out_rows.shape[0] - 1
    E = EXPERTS

    ctx = ExitStack()
    with nc.cleanup_on_exit(), ctx:
        sb, ps = tensors(ctx, nc)
        signals = []

        def sig(name, per=NCH, unit=1, credit=1):
            s = Signal(nc, name, per, unit, credit)
            signals.append(s)
            return s

        z_in = sb("e_z_in", [P, CB, D], F32)
        y_in = sb("e_y_in", [P, CB, D], F32)
        o_sb = sb("e_o_sb", [P, CB, D], F32)
        row_g = sb("e_row_g", [P, 2, CB], I32)
        row_s = sb("e_row_s", [P, 2, CB], I32)
        eye = sb("e_eye", [P, E, E], F32)
        mine = sb("e_mine", [P, 2, E], F32)
        h32 = sb("e_h32", [P, FT, CT], F32)
        h_hi = sb("e_h_hi", [P, 2, FT, CT], FP16)
        h_lo = sb("e_h_lo", [P, 2, FT, CT], FP16)
        th = sb("e_th", [P, 2, CT], F32)
        u = sb("e_u", [P, 2, CT], F32)
        g32 = sb("e_g32", [P, 2, CT], F32)
        g_hi = sb("e_g_hi", [P, FC, CT], FP16)
        g_lo = sb("e_g_lo", [P, FC, CT], FP16)
        lg = sb("e_lg", [P, CB, E], F32)
        rest = sb("e_rest", [P, CB, E], F32)
        part = sb("e_part", [P, CB, E], F32)
        best = sb("e_best", [P, CB], F32)
        own = sb("e_own", [P, CB], F32)
        gap = sb("e_gap", [P, CB], F32)
        ex = sb("e_ex", [P, CB], F32)
        ex2 = sb("e_ex2", [P, CB], F32)
        half_gate = sb("e_half_gate", [P, 2, CB], F32)

        bank_a = [ps(f"e_bank_a{i}", [P, 512]) for i in range(2)]
        bank_b = [ps(f"e_bank_b{i}", [P, 512]) for i in range(2)]
        bank_d = [ps(f"e_bank_d{i}", [P, 512]) for i in range(2)]
        bank_t = [ps(f"e_bank_t{i}", [P, 512]) for i in range(2)]

        setup = nc.alloc_semaphore("e_setup")
        passed = nc.alloc_semaphore("e_passed")
        stage_in = sig("e_stage_in", 1, 48)
        z_rows = sig("e_z_rows", NCH * CB, 16, credit=0)
        y_rows = sig("e_y_rows", NCH * CB, 16, credit=0)
        stored = sig("e_stored", NCH * CB, 16, credit=0)
        (rows_set, h_hi_done, h_done, lg_done, lg_copied, rest_done, best_done, part_done, own_done, gap_done,
         ex_done, ex2_done, gate_done, o_ready) = [sig("e_" + n) for n in (
             "rows_set", "h_hi_done", "h_done", "lg_done", "lg_copied", "rest_done", "best_done",
             "part_done", "own_done", "gap_done", "ex_done", "ex2_done", "gate_done", "o_ready")]
        turned = sig("e_turned", FT * NCH)
        h32_done = sig("e_h32_done", FT * NCH)
        (up_a, up_b, gated, u_done, g_done, g_hi_done, g_split, down_done) = [sig("e_" + n, FC * NCH) for n in (
            "up_a", "up_b", "gated", "u_done", "g_done", "g_hi_done", "g_split", "down_done")]
        up_high, up_low, down_high, down_low = [sig("e_" + n, FC) for n in (
            "up_high", "up_low", "down_high", "down_low")]
        block = ctx.enter_context(nc.Block())

        def place(e, s, lag):
            q = s - lag
            at = e + q // NCH
            if isinstance(e, int) and not 0 <= at < E:
                return None
            return at, q % NCH

        def later(e):
            return None if isinstance(e, int) and e + 1 >= E else e + 1

        def turns(engine, body):
            body(0, -1)
            for s in range(NCH):
                body(0, s)
            with engine.Fori(1, E - 1) as e:
                for s in range(NCH):
                    body(e, s)
            for s in range(NCH):
                body(E - 1, s)
            body(E, 0)

        @block.sync
        def _(sp):
            stage_in.start(sp)
            sp.sem_inc(stage_in.sem, 48)

            def slot(e, s):
                nxt = later(e)
                if s == 0 and nxt is not None and not (isinstance(e, int) and e < 0):
                    sp.wait_ge(up_low.sem, up_low.after(e, FC))
                    sp.wait_ge(down_low.sem, down_low.after(e, FC))
                    if isinstance(nxt, int):
                        W.load(sp, ew1[nxt], ew3[nxt], ew2[nxt], stage_in.sem)
                    else:
                        one = bass.ds(nxt, 1)
                        W.load(sp, ew1[one].rearrange("o d f -> (o d) f"), ew3[one].rearrange("o d f -> (o d) f"),
                               ew2[one].rearrange("o f d -> (o f) d"), stage_in.sem)
            turns(sp, slot)

        @block.gpsimd
        def _(pool):
            G = nc.gpsimd
            for s in signals:
                if s is not stage_in:
                    s.start(pool)
            G.memset(eye[:, :, :], 0.0).then_inc(setup, 1)
            G.memset(z_in[:, :, :], 0.0).then_inc(setup, 1)
            pool.wait_ge(setup, 2)
            G.affine_select(out=eye[:, :, :], in_=eye[:, :, :], compare_op=ALU.not_equal, fill=1.0, base=0,
                            channel_multiplier=0, pattern=[[1, E], [-1, E]]).then_inc(setup, 1)
            pool.wait_ge(setup, 3)

            def slot(e, s):
                def low(f):
                    if at := place(e, s, 0):
                        c, t = at
                        n = FC * t + f
                        pool.wait_ge(g_hi_done.sem, g_hi_done.after(c, n + 1))
                        pool.wait_ge(down_done.sem, down_done.after(c, n + 1 - FC))
                        G.tensor_tensor(g_lo[:, f], g32[:, f % 2], g_hi[:, f], ALU.subtract).then_inc(g_split.sem, 1)

                def low_h():
                    if at := place(e, s, -1):
                        c, t = at
                        pool.wait_ge(h_hi_done.sem, h_hi_done.after(c, t + 1))
                        G.tensor_tensor(h_lo[:, t], h32[:, :, :], h_hi[:, t], ALU.subtract).then_inc(h_done.sem, 1)

                def gather_z():
                    if at := place(e, s, -1):
                        c, t = at
                        n = c * SLOT_BLOCKS + t * CB
                        if stored.due(c, CB * (t - 1)):
                            pool.wait_ge(stored.sem, stored.after(c, CB * (t - 1)))
                        pool.wait_ge(gate_done.sem, gate_done.after(c, t - 1))
                        G.tensor_copy(row_g[:, t], gather_rows[:, bass.ds(n, CB)])
                        G.tensor_copy(row_s[:, t], scatter_rows[:, bass.ds(n, CB)])
                        G.tensor_copy(mine[:, t], eye[:, bass.ds(c, 1), :].rearrange("p o e -> p (o e)"))\
                            .then_inc(rows_set.sem, 1)
                        pool.wait_ge(rows_set.sem, rows_set.after(c, t + 1))
                        pool.wait_ge(turned.sem, turned.after(c, FT * t))
                        pool.sem_inc(passed, 1)
                        for j in range(CB):
                            G.indirect_dma_start(out=z_in[0:SUB, j, :], out_offset=None, in_=z,
                                                 in_offset=bass.IndirectOffsetOnAxis(ap=row_g[0:SUB, t, j:j + 1], axis=0))\
                                .then_inc(z_rows.sem, 16)

                def scatter():
                    if at := place(e, s, 1):
                        c, t = at
                        pool.wait_ge(o_ready.sem, o_ready.after(c, t + 1))
                        pool.sem_inc(passed, 1)
                        for j in range(CB):
                            G.indirect_dma_start(out=out_rows, out_offset=bass.IndirectOffsetOnAxis(
                                ap=row_s[0:SUB, t, j:j + 1], axis=0), in_=o_sb[0:SUB, j, :], in_offset=None,
                                bounds_check=LAST_ROW, oob_is_err=False).then_inc(stored.sem, 16)

                def gather_y():
                    if at := place(e, s, 0):
                        c, t = at
                        if stored.due(c, CB * t):
                            pool.wait_ge(stored.sem, stored.after(c, CB * t))
                        pool.sem_inc(passed, 1)
                        for j in range(CB):
                            G.indirect_dma_start(out=y_in[0:SUB, j, :], out_offset=None, in_=out_rows,
                                                 in_offset=bass.IndirectOffsetOnAxis(ap=row_g[0:SUB, t, j:j + 1], axis=0))\
                                .then_inc(y_rows.sem, 16)
                low(0), low(1)
                scatter()
                low(2), low(3)
                gather_z()
                low(4), low(5)
                gather_y()
                low_h()
                low(6), low(7)
            turns(pool, slot)
            pool.wait_ge(stored.sem, stored.after(E - 1, NCH * CB))

        @block.vector
        def _(dve):
            V = nc.vector

            def split_up(e, f):
                dve.wait_ge(up_high.sem, up_high.after(e, f + 1))
                t = slice(f * P, (f + 1) * P)
                w = "p k i o -> p (k i) o"
                V.tensor_tensor(W.up_lo[:, :, :, t].rearrange(w), W.stage_up[:, :, :, t].rearrange(w),
                                W.up_hi[:, :, :, t].rearrange(w), ALU.subtract).then_inc(up_low.sem, 1)

            def split_down(e, f):
                dve.wait_ge(down_high.sem, down_high.after(e, f + 1))
                V.tensor_tensor(W.down_lo[:, f], W.stage_down[:, f], W.down_hi[:, f], ALU.subtract)\
                    .then_inc(down_low.sem, 1)
            dve.wait_ge(setup, 3)
            for f in range(FC):
                split_up(0, f)
            for f in range(FC - 2):
                split_down(0, f)

            def slot(e, s):
                def gate(f):
                    if at := place(e, s, 0):
                        c, t = at
                        n = FC * t + f
                        dve.wait_ge(gated.sem, gated.after(c, n + 1))
                        dve.wait_ge(g_done.sem, g_done.after(c, n - 1))
                        V.scalar_tensor_tensor(out=u[:, f % 2], in0=th[:, f % 2], scalar=1.0, in1=bank_a[f % 2][:, 0:CT],
                                               op0=ALU.add, op1=ALU.mult).then_inc(u_done.sem, 1)
                        dve.wait_ge(u_done.sem, u_done.after(c, n + 1))
                        dve.wait_ge(up_b.sem, up_b.after(c, n + 1))
                        dve.wait_ge(g_split.sem, g_split.after(c, n - 1))
                        V.tensor_tensor(g32[:, f % 2], bank_b[f % 2][:, 0:CT], u[:, f % 2], ALU.mult)\
                            .then_inc(g_done.sem, 1)
                        nxt = later(e)
                        if s == NCH - 1 and nxt is not None:
                            if f >= 1:
                                split_up(nxt, f - 1)
                            if f >= 4:
                                split_down(nxt, f - 4)

                def last_splits():
                    nxt = later(e)
                    if s == NCH - 1 and nxt is not None:
                        split_up(nxt, FC - 1)
                        split_down(nxt, FC - 4), split_down(nxt, FC - 3)

                def last_down():
                    if s == 0 and (not isinstance(e, int) or e < E):
                        split_down(e, FC - 2), split_down(e, FC - 1)

                def finish():
                    if at := place(e, s, 1):
                        c, t = at
                        dve.wait_ge(down_done.sem, down_done.after(c, FC * (t + 1)))
                        dve.wait_ge(y_rows.sem, y_rows.after(c, CB * (t + 1)))
                        if stored.due(c, CB * t):
                            dve.wait_ge(stored.sem, stored.after(c, CB * t))
                        dve.wait_ge(gate_done.sem, gate_done.after(c, t + 1))
                        for j in range(CB):
                            ins = V.scalar_tensor_tensor(
                                out=o_sb[0:SUB, j, :], in0=bank_d[j // 2][0:SUB, (j % 2) * D:(j % 2 + 1) * D],
                                scalar=half_gate[0:SUB, t, j:j + 1], in1=y_in[0:SUB, j, :],
                                op0=ALU.mult, op1=ALU.add)
                        ins.then_inc(o_ready.sem, 1)

                def gates():
                    if at := place(e, s, -1):
                        c, t = at
                        n = t + 1
                        r = slice(0, SUB)
                        me = mine[r, t, :].unsqueeze(1).to_broadcast([SUB, CB, E])
                        dve.wait_ge(lg_done.sem, lg_done.after(c, n))
                        dve.wait_ge(rows_set.sem, rows_set.after(c, n))
                        V.tensor_copy(lg[r, :, :], bank_t[0][r, 0:CB * 8].rearrange("p (j e) -> p j e", e=8)[:, :, 0:E])\
                            .then_inc(lg_copied.sem, 1)
                        dve.wait_ge(lg_copied.sem, lg_copied.after(c, n))
                        V.tensor_tensor(part[r, :, :], lg[r, :, :], me, ALU.mult).then_inc(part_done.sem, 1)
                        V.scalar_tensor_tensor(out=rest[r, :, :], in0=me, scalar=MASKED, in1=lg[r, :, :], op0=ALU.mult,
                                               op1=ALU.add).then_inc(rest_done.sem, 1)
                        dve.wait_ge(part_done.sem, part_done.after(c, n))
                        V.tensor_reduce(own[r, :], part[r, :, :], AX.X, ALU.add).then_inc(own_done.sem, 1)
                        dve.wait_ge(rest_done.sem, rest_done.after(c, n))
                        V.tensor_reduce(best[r, :], rest[r, :, :], AX.X, ALU.max).then_inc(best_done.sem, 1)
                        dve.wait_ge(own_done.sem, own_done.after(c, n))
                        dve.wait_ge(best_done.sem, best_done.after(c, n))
                        V.tensor_tensor(gap[r, :], best[r, :], own[r, :], ALU.subtract).then_inc(gap_done.sem, 1)
                        dve.wait_ge(ex_done.sem, ex_done.after(c, n))
                        V.tensor_scalar(ex2[r, :], ex[r, :], 1.0, 2.0, ALU.add, ALU.mult).then_inc(ex2_done.sem, 1)
                        dve.wait_ge(ex2_done.sem, ex2_done.after(c, n))
                        V.reciprocal(half_gate[r, t, :], ex2[r, :]).then_inc(gate_done.sem, 1)
                gate(0)
                last_down()
                gate(1)
                finish()
                for f in range(2, FC):
                    gate(f)
                last_splits()
                gates()
            turns(dve, slot)

        @block.scalar
        def _(act):
            A = nc.scalar

            def split_up(e, f, first=False):
                act.wait_ge(stage_in.sem, stage_in.after(e, 1))
                if not first:
                    act.wait_ge(up_b.sem, up_b.after(e, f + 1 - FC))
                t = slice(f * P, (f + 1) * P)
                w = "p k i o -> p (k i) o"
                A.activation(W.up_hi[:, :, :, t].rearrange(w), W.stage_up[:, :, :, t].rearrange(w), ACT.Copy)\
                    .then_inc(up_high.sem, 1)

            def split_down(e, f, first=False):
                if not first:
                    act.wait_ge(down_done.sem, down_done.after(e, f + 1 - FC))
                A.activation(W.down_hi[:, f], W.stage_down[:, f], ACT.Copy).then_inc(down_high.sem, 1)
            for f in range(FC):
                split_up(0, f, True)
            for f in range(FC - 2):
                split_down(0, f, True)

            def slot(e, s):
                def gate(f):
                    if at := place(e, s, 0):
                        c, t = at
                        n = FC * t + f
                        act.wait_ge(up_a.sem, up_a.after(c, n + 1))
                        act.wait_ge(u_done.sem, u_done.after(c, n - 1))
                        A.activation(th[:, f % 2], bank_a[f % 2][:, 0:CT], ACT.Tanh, scale=0.5).then_inc(gated.sem, 1)

                def high(f):
                    if at := place(e, s, 0):
                        c, t = at
                        n = FC * t + f
                        act.wait_ge(g_done.sem, g_done.after(c, n + 1))
                        act.wait_ge(down_done.sem, down_done.after(c, n + 1 - FC))
                        A.activation(g_hi[:, f], g32[:, f % 2], ACT.Copy).then_inc(g_hi_done.sem, 1)
                        nxt = later(e)
                        if s == NCH - 1 and nxt is not None:
                            split_up(nxt, f)
                            if f >= 3:
                                split_down(nxt, f - 3)

                def last_down():
                    if s == 0 and (not isinstance(e, int) or e < E):
                        first = isinstance(e, int) and e == 0
                        split_down(e, FC - 2, first), split_down(e, FC - 1, first)

                def affine():
                    if at := place(e, s, -1):
                        c, t = at
                        for i in range(FT):
                            act.wait_ge(turned.sem, turned.after(c, FT * t + i + 1))
                            act.wait_ge(h_done.sem, h_done.after(c, t))
                            A.activation(h32[:, i], bank_t[i][:, 0:CT], ACT.Identity, bias=bcol[:, i:i + 1],
                                         scale=gcol[:, i:i + 1]).then_inc(h32_done.sem, 1)
                        act.wait_ge(h32_done.sem, h32_done.after(c, FT * t + FT))
                        A.activation(h_hi[:, t], h32[:, :, :], ACT.Copy).then_inc(h_hi_done.sem, 1)

                def exp_gap():
                    if at := place(e, s, -1):
                        c, t = at
                        act.wait_ge(gap_done.sem, gap_done.after(c, t + 1))
                        A.activation(ex[0:SUB, :], gap[0:SUB, :], ACT.Exp).then_inc(ex_done.sem, 1)
                gate(0)
                last_down()
                for f in range(1, FC):
                    gate(f)
                    high(f - 1)
                    if f == 6:
                        affine()
                high(FC - 1)
                if s == NCH - 1 and later(e) is not None and place(e, s, 0):
                    split_down(later(e), FC - 3)
                exp_gap()
            turns(act, slot)

        @block.tensor
        def _(pe):
            T = nc.tensor

            def slot(e, s):
                def up(f):
                    if at := place(e, s, 0):
                        c, t = at
                        n = FC * t + f
                        if f == 0:
                            pe.wait_ge(h_done.sem, h_done.after(c, t + 1))
                        if t == 0:
                            pe.wait_ge(up_low.sem, up_low.after(c, f + 1))
                        pe.wait_ge(u_done.sem, u_done.after(c, n - 1))
                        pe.wait_ge(g_done.sem, g_done.after(c, n - 1))
                        for k, (bank, done) in enumerate(((bank_a, up_a), (bank_b, up_b))):
                            for i in range(FT):
                                w_hi = W.up_hi[:, k, i, f * P:(f + 1) * P]
                                w_lo = W.up_lo[:, k, i, f * P:(f + 1) * P]
                                T.matmul(bank[f % 2][:, 0:CT], w_hi, h_hi[:, t, i], start=i == 0, stop=False)
                                T.matmul(bank[f % 2][:, 0:CT], w_hi, h_lo[:, t, i], start=False, stop=False)
                                mm = T.matmul(bank[f % 2][:, 0:CT], w_lo, h_hi[:, t, i], start=False,
                                              stop=i == FT - 1)
                            mm.then_inc(done.sem, 1)

                def down(f, lag):
                    if at := place(e, s, lag):
                        c, t = at
                        n = FC * t + f
                        if f == 0:
                            pe.wait_ge(o_ready.sem, o_ready.after(c, t))
                        if t == 0:
                            pe.wait_ge(down_low.sem, down_low.after(c, f + 1))
                        pe.wait_ge(g_split.sem, g_split.after(c, n + 1))
                        for j in range(CB):
                            o = bank_d[j // 2][0:SUB, (j % 2) * D:(j % 2 + 1) * D]
                            tok = slice(j * SUB, (j + 1) * SUB)
                            for k, (l, w) in enumerate(((g_hi, W.down_hi), (g_hi, W.down_lo), (g_lo, W.down_hi))):
                                mm = T.matmul(o, l[:, f, tok], w[:, f, :], start=f == k == 0 and j % 2 == 0,
                                              stop=f == FC - 1 and k == 2, skip_group_check=True)
                        mm.then_inc(down_done.sem, 1)

                def turn():
                    if at := place(e, s, -1):
                        c, t = at
                        pe.wait_ge(z_rows.sem, z_rows.after(c, CB * (t + 1)))
                        pe.wait_ge(lg_copied.sem, lg_copied.after(c, t))
                        for i in range(FT):
                            pe.wait_ge(h32_done.sem, h32_done.after(c, FT * (t - 1) + i + 1))
                            for j in range(CB):
                                mm = T.transpose(bank_t[i][:, j * SUB:(j + 1) * SUB], z_in[0:SUB, j, i * P:(i + 1) * P],
                                                 id32[0:SUB, 0:SUB])
                            mm.then_inc(turned.sem, 1)

                def score():
                    if at := place(e, s, -1):
                        c, t = at
                        pe.wait_ge(h_done.sem, h_done.after(c, t + 1))
                        for j in range(CB):
                            tok = slice(j * SUB, (j + 1) * SUB)
                            for i in range(FT):
                                for k, (l, w) in enumerate(((h_hi, wr_hi), (h_hi, wr_lo), (h_lo, wr_hi))):
                                    mm = T.matmul(bank_t[0][0:SUB, j * 8:j * 8 + E], l[:, t, i, tok], w[:, i, :],
                                                  start=i == k == 0, stop=i == FT - 1 and k == 2)
                        mm.then_inc(lg_done.sem, 1)
                up(0)
                down(FC - 2, 1)
                up(1)
                down(FC - 1, 1)
                for f in range(2, FC):
                    up(f)
                    down(f - 2, 0)
                    if f == 6:
                        turn()
                score()
            turns(pe, slot)


def program(nc, x, wq, wk, wv, wo, ln_g, ln_b, wr, w1, w3, w2, w1s, w3s, w2s, out):
    batches, seq, _ = x.shape
    y = nc.dram_tensor("y_rows", (batches, seq, D), F32).ap()
    z = nc.dram_tensor("z_rows", (batches * seq, D), F32).ap()
    ctx = ExitStack()
    with ctx:
        sb, _ = tensors(ctx, nc)
        W = Weights(sb)
        TT = batches * seq // P
        logits = sb("logits", [P, TT, EXPERTS], F32)
        gather_rows = sb("gather_rows", [P, EXPERTS * SLOT_BLOCKS], I32)
        scatter_rows = sb("scatter_rows", [P, EXPERTS * SLOT_BLOCKS], I32)
        id32 = sb("id32", [P, P], F32)
        persist = (logits, sb("gcol", [P, FT], F32), sb("bcol", [P, FT], F32), sb("wr_hi", [P, FT, EXPERTS], FP16),
                   sb("wr_lo", [P, FT, EXPERTS], FP16), id32)
        shared_loaded = ctx.enter_context(nc.semaphore("shared_loaded"))
        expert0_loaded = ctx.enter_context(nc.semaphore("expert0_loaded"))
        attention(nc, x, wq, wk, wv, wo, y, id32, W, (w1s, w3s, w2s), shared_loaded)
        shared_ffn(nc, W, persist, shared_loaded, y, ln_g, ln_b, wr, w1, w3, w2, z, out, expert0_loaded)
        route(nc, logits, gather_rows, scatter_rows, batches)
        experts(nc, W, persist, w1, w3, w2, gather_rows, scatter_rows, z, out)


def kernel(L0_attn_x, L0_attn_Wq, L0_attn_Wk, L0_attn_Wv, L0_attn_Wo, L0_ffn_ln_g, L0_ffn_ln_b, L0_ffn_Wr, L0_ffn_W1,
           L0_ffn_W3, L0_ffn_W2, L0_ffn_W1s, L0_ffn_W3s, L0_ffn_W2s):
    import numpy as np
    import concourse.bacc as bacc
    from concourse.bass_utils import run_bass_kernel_spmd

    def column(a):
        return np.asarray(a).reshape(FT, P).T
    arrays = dict(x=L0_attn_x, wq=np.asarray(L0_attn_Wq).T, wk=np.asarray(L0_attn_Wk).T, wv=np.asarray(L0_attn_Wv).T,
                  wo=np.asarray(L0_attn_Wo).T, ln_g=column(L0_ffn_ln_g), ln_b=column(L0_ffn_ln_b), wr=L0_ffn_Wr,
                  w1=L0_ffn_W1, w3=L0_ffn_W3, w2=L0_ffn_W2, w1s=L0_ffn_W1s, w3s=L0_ffn_W3s, w2s=L0_ffn_W2s)
    arrays = {"in_" + n: np.ascontiguousarray(a) for n, a in arrays.items()}
    nc = bacc.Bacc("TRN2", target_bir_lowering=False, num_devices=1)
    args = [nc.dram_tensor(n, a.shape, mybir.dt.from_np(a.dtype), kind="ExternalInput").ap() for n, a in arrays.items()]
    out = nc.dram_tensor("out", arrays["in_x"].shape, F32, kind="ExternalOutput").ap()
    program(nc, *args, out)
    return run_bass_kernel_spmd(nc, [arrays], core_ids=[0]).results[0]["out"]
```

```python
import concourse.bass as bass
from concourse import mybir
from contextlib import ExitStack

F32, BF16, FP16, I32 = mybir.dt.float32, mybir.dt.bfloat16, mybir.dt.float16, mybir.dt.int32
ALU = mybir.AluOpType
ACT = mybir.ActivationFunctionType
AX = mybir.AxisListType

P = 128
D = 256
FT = D // P
HEADS, HD = 16, 16
PAIRS = HEADS // 2
PIECES = 4
SHIFT_PART = 2
SHIFT_UNIT = 1024.0
HALF_W = 32
WIN = P + 2 * HALF_W
SCALE = HD ** -0.5
EPS = 1e-5
MASKED = -1e30


class Signal:

    def __init__(self, nc, name, per, unit=1, credit=1):
        self.sem = nc.alloc_semaphore(name)
        self.per, self.unit, self.credit = per, unit, credit

    def start(self, engine):
        if self.credit:
            engine.sem_inc(self.sem, self.credit * self.per * self.unit)

    def after(self, batch, events):
        if isinstance(batch, int):
            value = ((batch + self.credit) * self.per + events) * self.unit
            assert value > 0
            return value
        return batch * (self.per * self.unit) + (self.credit * self.per + events) * self.unit

    def due(self, batch, events):
        return not isinstance(batch, int) or (batch + self.credit) * self.per + events > 0


def tensors(ctx, nc):
    def sb(name, shape, dt):
        return ctx.enter_context(nc.sbuf_tensor(name, shape, dt))

    def ps(name, shape, dt=F32):
        return ctx.enter_context(nc.psum_tensor(name, shape, dt))
    return sb, ps


def attention(nc, x, wq, wk, wv, wo, y, id32, W, shared, shared_loaded):
    batches, seq, _ = x.shape
    NB = seq // P
    XLEAD = 5
    LAG = dict(stats=-3, norm=-2, spread=-1, project=0, scores=2, maxima=3, weigh=5, gather=7, out=8)
    x_v = x.rearrange("b (s p) d -> b s p d", p=P)
    y_v = y.rearrange("b (s p) d -> b s p d", p=P)
    COLS = seq + 2 * HALF_W

    ctx = ExitStack()
    with nc.cleanup_on_exit(), ctx:
        sb, ps = tensors(ctx, nc)

        def sig(name, per=NB, unit=1):
            s = Signal(nc, name, per, unit)
            signals.append(s)
            return s
        signals = []

        id16 = sb("id16", [P, P], FP16)
        idb = sb("idb", [P, P], BF16)
        band = sb("band", [P, 3, WIN], BF16)
        first_row = sb("first_row", [P, P], F32)
        near0 = sb("near0", [P, 2], F32)
        wstage = W.up_hi[:, :, :, :].rearrange("p k f o -> p (k f o)").bitcast(F32)\
            .rearrange("p (f n o) -> p f n o", f=FT, n=4)
        whi = sb("whi", [P, FT, 4, D], FP16)
        wlo = sb("wlo", [P, FT, 4, D], FP16)
        x_in = sb("x_in", [P, NB, D], F32)
        x_res = sb("x_res", [P, 4, D], F32)
        st = sb("st", [P, 2, 6], F32)
        mv = sb("mv", [P, 2, 2], F32)
        ve = sb("ve", [P, 2], F32)
        mhalf = sb("mhalf", [P, 1], F32)
        rs = sb("rs", [P, 2], F32)
        xn = sb("xn", [P, 2, D], F32)
        xt_hi = sb("xt_hi", [P, FT, P], FP16)
        xt_lo = sb("xt_lo", [P, FT, P], FP16)
        q_tok = sb("q_tok", [P, HEADS, PIECES, HD], FP16)
        k_tok = sb("k_tok", [P, HEADS, PIECES, HD], FP16)
        k_st = sb("k_st", [P, PAIRS, COLS], FP16)
        q_ev = sb("q_ev", [P, PAIRS, COLS], FP16)
        q_od = sb("q_od", [P, PAIRS, COLS], FP16)
        v_sb = sb("v_sb", [P, NB, HEADS, 2 * HD], F32)
        k0 = sb("k0", [P, PAIRS], FP16)
        mx = sb("mx", [P, HEADS], F32)
        mf = sb("mf", [P, HEADS], F32)
        ms = sb("ms", [P, 2, 64], FP16)
        eg = sb("eg", [P, HEADS], F32)
        pg = sb("pg", [P, NB, HEADS], F32)
        pt = sb("pt", [P, 4, 2, WIN], F32)
        o_acc = sb("o_acc", [P, 4, COLS], F32)
        v0 = sb("v0", [P, HEADS, HD], F32)
        pgv = sb("pgv", [P, HEADS, HD], F32)
        den = sb("den", [P, HEADS], F32)
        rec = sb("rec", [P, HEADS], F32)
        onum = sb("onum", [P, HEADS, HD], F32)
        o_tok = sb("o_tok", [P, HEADS, HD], F32)
        ot_hi = sb("ot_hi", [P, FT, P], FP16)
        ot_lo = sb("ot_lo", [P, FT, P], FP16)
        y_sb = sb("y_sb", [P, 2, D], F32)
        z_st = sb("z_st", [P, PAIRS * HEADS], FP16)
        s0 = sb("s0", [HEADS, seq], F32)
        m0 = sb("m0", [HEADS, 1], F32)
        nb0 = sb("nb0", [HEADS, 1], F32)
        p0 = sb("p0", [HEADS, seq], F32)
        l0 = sb("l0", [HEADS, 1], F32)
        r0 = sb("r0", [HEADS, 1], F32)
        p0_t = sb("p0_t", [P, NB, 32], F32)
        v_keep = sb("v_keep", [P, 2, HEADS, HD], F32)
        own = sb("own", [P, HEADS, HD], F32)
        o0_all = sb("o0_all", [P, D], F32)
        one_col = sb("one_col", [P, 1], F32)
        o0 = sb("o0", [1, D], F32)
        o0_dram = nc.dram_tensor("o0_rows", (batches, D), F32).ap()
        o0_rows = sb("o0_rows_sb", [batches, D], F32)
        x0_rows = sb("x0_rows_sb", [batches, D], F32)
        y0_rows = sb("y0_rows_sb", [batches, D], F32)

        bank_qk = ps("bank_qk", [P, 512])
        bank_v = ps("bank_v", [P, 512])
        bank_m = ps("bank_m", [P, 512])
        bank_s = [ps(f"bank_s{i}", [P, 512]) for i in range(2)]
        bank_w = [ps(f"bank_w{i}", [P, 512]) for i in range(2)]
        bank_o = ps("bank_o", [P, 512])
        qk_ps = bank_qk[:, :].rearrange("p (t h d) -> p t h d", t=2, h=HEADS)
        kst_ps = bank_qk[:, :].bitcast(FP16).rearrange("p (j t) -> p j t", j=PAIRS)
        gat_ps = bank_qk[:, :].rearrange("p (h d) -> p h d", h=HEADS)
        v_ps = bank_v[:, 0:D].rearrange("p (h d) -> p h d", h=HEADS)
        qst_ps = bank_v[:, :].bitcast(FP16).rearrange("p (j t) -> p j t", j=PAIRS)
        wo_ps = bank_v[:, 0:D]
        tr_ps = bank_m[:, 0:D].rearrange("p (f t) -> p f t", f=FT)
        mst_ps = bank_m[:, :].bitcast(FP16)
        g_ps = bank_m[:, 0:HEADS]

        w_in = nc.alloc_semaphore("w_in")
        w_hi_done = nc.alloc_semaphore("w_hi_done")
        w_lo_done = nc.alloc_semaphore("w_lo_done")
        setup = nc.alloc_semaphore("setup")
        passed = nc.alloc_semaphore("passed")
        zeroed = nc.alloc_semaphore("zeroed")
        next_high = nc.alloc_semaphore("next_high")
        next_low = nc.alloc_semaphore("next_low")
        fin = nc.alloc_semaphore("fin")
        fin_dma = nc.alloc_semaphore("fin_dma")
        x_loaded = [sig(f"x_loaded{s}", 1, 16) for s in range(NB)]
        res_loaded = [sig(f"res_loaded{s}", 2, 16) for s in range(4)]
        y_stored = [sig(f"y_stored{s}", NB // 2, 16) for s in range(2)]
        o0_stored = sig("o0_stored", 1, 16)
        (stats_raw, stats_done, var_eps, rstd_done, normed, spread, xt_hi_done, xt_split, qk_done, v_done,
         qk_hi, qk_split, v_copied, kst_done, qst_done, kst_copied, g_done, mf_done, ms_done,
         e_done, pg_done, mst_done, shift_ev, shift_od, gat_done, den_done, rec_done, pgv_done,
         num_done, o_done, otr_done, ot_hi_done, ot_split, wo_done, y_ready) = [sig(n) for n in (
             "stats_raw", "stats_done", "var_eps", "rstd_done", "normed", "spread", "xt_hi_done",
             "xt_split", "qk_done", "v_done", "qk_hi", "qk_split", "v_copied", "kst_done", "qst_done",
             "kst_copied", "g_done", "mf_done", "ms_done", "e_done", "pg_done",
             "mst_done", "shift_ev", "shift_od", "gat_done", "den_done", "rec_done", "pgv_done", "num_done",
             "o_done", "otr_done", "ot_hi_done", "ot_split", "wo_done", "y_ready")]
        qst_copied = sig("qst_copied", 2 * NB)
        scored = sig("scored", PAIRS * NB)
        maxed = sig("maxed", PAIRS * NB)
        weighed = sig("weighed", PAIRS * NB)
        exped = sig("exped", PAIRS * NB)
        cut_left = sig("cut_left", PAIRS * NB)
        cut = sig("cut", PAIRS * NB)
        valued = sig("valued", 4 * NB)
        added = sig("added", 2 * NB)
        o_copied = sig("o_copied", 2 * NB)
        (k0_copied, z_copied, v0_done, v0_copied, m0_done, nb0_done, p0_done, r0_done, p0_scaled, p0t_done,
         p0t_copied, o0_done, o0_scaled, o0_sum, o0_copied, v_kept) = [sig(n, 1) for n in (
             "k0_copied", "z_copied", "v0_done", "v0_copied", "m0_done", "nb0_done", "p0_done",
             "r0_done", "p0_scaled", "p0t_done", "p0t_copied", "o0_done", "o0_scaled", "o0_sum", "o0_copied",
             "v_kept")]
        s0_done = sig("s0_done", 2)
        s0_copied = sig("s0_copied", 2)

        def place(b, s, lag):
            q = s - lag
            batch = b + q // NB
            if isinstance(b, int) and not 0 <= batch < batches:
                return None
            return batch, q % NB

        def turns(engine, body):
            for s in range(LAG["stats"], 0):
                body(0, s)
            for s in range(NB):
                body(0, s)
            with engine.Fori(1, batches - 1) as b:
                for s in range(NB):
                    body(b, s)
            for b, n in ((batches - 1, NB), (batches, LAG["out"] + 1)):
                for s in range(n):
                    body(b, s)

        def cols(s, extra=0):
            return slice(HALF_W + s * P - extra, HALF_W + (s + 1) * P + extra)

        block = ctx.enter_context(nc.Block())

        @block.sync
        def _(sp):
            for n, w in enumerate((wq, wk, wv, wo)):
                sp.dma_start(wstage[:, :, n, :], w.rearrange("(f p) o -> p f o", p=P)).then_inc(w_in, 16)
            for s in x_loaded:
                s.start(sp)
            for s in res_loaded:
                s.start(sp)
            for s in y_stored:
                s.start(sp)
            o0_stored.start(sp)

            def slot(b, s):
                if at := place(b, s, -XLEAD):
                    c, t = at
                    sp.wait_ge(normed.sem, normed.after(c, t + 1 - NB))
                    sp.dma_start(x_in[:, t, :], x_v[c, t]).then_inc(x_loaded[t].sem, 16)
                if at := place(b, s, LAG["out"] - 2):
                    c, t = at
                    sp.wait_ge(y_ready.sem, y_ready.after(c, t - 3))
                    sp.sem_inc(passed, 1)
                    sp.dma_start(x_res[:, t % 4, :], x_v[c, t]).then_inc(res_loaded[t % 4].sem, 16)
                if at := place(b, s, LAG["out"]):
                    c, t = at
                    sp.wait_ge(y_ready.sem, y_ready.after(c, t + 1))
                    sp.sem_inc(passed, 1)
                    sp.dma_start(y_v[c, t], y_sb[:, t % 2, :]).then_inc(y_stored[t % 2].sem, 16)
                if s == 5 and (at := place(b, s, NB)):
                    c = at[0]
                    sp.wait_ge(o0_copied.sem, o0_copied.after(c, 1))
                    sp.dma_start(o0_dram[bass.ds(c, 1), :], o0[:, :]).then_inc(o0_stored.sem, 16)
            for s in range(-XLEAD, LAG["stats"]):
                slot(0, s)
            W.load(sp, *shared, shared_loaded)
            turns(sp, slot)
            sp.wait_ge(shared_loaded, 48)
            sp.wait_ge(o0_stored.sem, o0_stored.after(batches - 1, 1))
            sp.dma_start(o0_rows[:, :], o0_dram).then_inc(fin_dma, 16)
            sp.dma_start(x0_rows[:, :], x[:, 0, :]).then_inc(fin_dma, 16)
            for s in y_stored:
                sp.wait_ge(s.sem, s.after(batches - 1, NB // 2))
            sp.wait_ge(fin, 5)
            sp.dma_start(y[:, 0, :], y0_rows[:, :]).then_inc(fin_dma, 16)
            sp.wait_ge(fin_dma, 48)

        @block.gpsimd
        def _(pool):
            for s in signals:
                if s.unit == 1:
                    s.start(pool)
            G = nc.gpsimd
            G.memset(id32[:, :], 0.0).then_inc(zeroed, 1)
            G.memset(idb[:, :], 0.0).then_inc(zeroed, 1)
            G.memset(band[:, :, :], 0.0).then_inc(zeroed, 1)
            G.memset(k_tok[:, :, :, :], 0.0).then_inc(zeroed, 1)
            G.memset(first_row[:, :], 0.0).then_inc(zeroed, 1)
            G.memset(near0[:, :], 0.0).then_inc(zeroed, 1)
            G.memset(own[:, :, :], 0.0).then_inc(zeroed, 1)
            G.memset(one_col[:, :], 1.0).then_inc(setup, 1)
            G.memset(mhalf[:, :], -0.5).then_inc(setup, 1)
            G.memset(v_sb[:, :, :, :], 1.0).then_inc(setup, 1)
            pool.wait_ge(zeroed, 7)

            def fill(out, op, value, base, mult, pattern):
                return G.affine_select(out=out, in_=out, compare_op=op, fill=value, base=base,
                                       channel_multiplier=mult, pattern=pattern)
            fill(id32[:, :], ALU.not_equal, 1.0, 0, 1, [[-1, P]]).then_inc(zeroed, 1)
            fill(idb[:, :], ALU.not_equal, 1.0, 0, 1, [[-1, P]]).then_inc(zeroed, 1)
            fill(band[:, :, :], ALU.is_ge, MASKED, 0, -1, [[0, 3], [1, WIN]]).then_inc(zeroed, 1)
            fill(k_tok[:, :, SHIFT_PART, :], ALU.not_equal, SHIFT_UNIT, 0, 0, [[1, HEADS], [-1, HD]])\
                .then_inc(zeroed, 1)
            fill(first_row[:, :], ALU.not_equal, 1.0, 0, 1, [[0, P]]).then_inc(zeroed, 1)
            fill(near0[:, 1:2], ALU.is_gt, MASKED, -HALF_W, 1, [[0, 1]]).then_inc(zeroed, 1)
            for i in range(4):
                fill(own[:, :, :], ALU.not_equal, 1.0, -32 * i, 1, [[-1, HEADS], [0, HD]]).then_inc(zeroed, 1)
                pool.wait_ge(zeroed, 14 + i)
            fill(band[:, :, :], ALU.is_ge, MASKED, 2 * HALF_W, 1, [[0, 3], [-1, WIN]]).then_inc(zeroed, 1)
            G.tensor_copy(id16[:, :], id32[:, :]).then_inc(setup, 1)
            pool.wait_ge(zeroed, 18)
            G.memset(band[:, 1, 0:HALF_W], MASKED).then_inc(setup, 1)
            G.memset(band[:, 2, HALF_W + P:WIN], MASKED).then_inc(setup, 1)

            def slot(b, s):
                def trim_left(p):
                    if at := place(b, s, LAG["weigh"]):
                        c, t = at
                        pool.wait_ge(exped.sem, exped.after(c, PAIRS * t + p + 1))
                        pool.sem_inc(passed, 1)
                        fill(pt[:, p % 4, :, 0:P], ALU.is_ge, 0.0, 0, -1, [[0, 2], [1, P]])\
                            .then_inc(cut_left.sem, 1)

                def trim_right(p):
                    if at := place(b, s, LAG["weigh"]):
                        c, t = at
                        pool.wait_ge(cut_left.sem, cut_left.after(c, PAIRS * t + p + 1))
                        pool.sem_inc(passed, 1)
                        fill(pt[:, p % 4, :, 2 * HALF_W:WIN], ALU.is_ge, 0.0, 0, 1, [[0, 2], [-1, P]])\
                            .then_inc(cut.sem, 1)

                def share():
                    if at := place(b, s, LAG["gather"]):
                        c, t = at
                        pool.wait_ge(pg_done.sem, pg_done.after(c, t + 1))
                        pool.wait_ge(v0_copied.sem, v0_copied.after(c, 1))
                        pool.wait_ge(num_done.sem, num_done.after(c, t))
                        G.tensor_tensor(pgv[:, :, :], v0[:, :, :],
                                        pg[:, t, :].unsqueeze(2).to_broadcast([P, HEADS, HD]), ALU.mult)\
                            .then_inc(pgv_done.sem, 1)

                for first in (0, 4):
                    trim_left(first)
                    for p in range(first + 1, first + 4):
                        trim_left(p), trim_right(p - 1)
                    trim_right(first + 3)
                    if first == 0:
                        share()
                if at := place(b, s, LAG["gather"]):
                    c, t = at
                    pool.wait_ge(num_done.sem, num_done.after(c, t + 1))
                    pool.wait_ge(otr_done.sem, otr_done.after(c, t))
                    G.tensor_tensor(o_tok[:, :, :], onum[:, :, :],
                                    rec[:, :].unsqueeze(2).to_broadcast([P, HEADS, HD]), ALU.mult)\
                        .then_inc(o_done.sem, 1)
                if at := place(b, s, LAG["stats"]):
                    c, t = at
                    pool.wait_ge(stats_done.sem, stats_done.after(c, t + 1))
                    pool.sem_inc(passed, 1)
                    G.tensor_scalar(ve[:, t % 2:t % 2 + 1], mv[:, t % 2, 1:2], EPS, None, ALU.add)\
                        .then_inc(var_eps.sem, 1)
                    pool.wait_ge(var_eps.sem, var_eps.after(c, t + 1))
                    pool.wait_ge(normed.sem, normed.after(c, t - 1))
                    G.tensor_tensor(rs[:, t % 2:t % 2 + 1], ve[:, t % 2:t % 2 + 1], mhalf[:, :], ALU.pow)\
                        .then_inc(rstd_done.sem, 1)
                if s == 4 and (at := place(b, s, s)):
                    c = at[0]
                    pool.wait_ge(v_copied.sem, v_copied.after(c, 2))
                    pool.wait_ge(o0_done.sem, o0_done.after(c, 0))
                    pool.sem_inc(passed, 1)
                    G.tensor_copy(v_keep[:, :, :, :], v_sb[:, 0:2, :, 0:HD]).then_inc(v_kept.sem, 1)
            turns(pool, slot)

        @block.vector
        def _(dve):
            V = nc.vector
            V.memset(k_st[:, :, :].bitcast(I32), 0).then_inc(setup, 1)
            V.memset(q_ev[:, :, :].bitcast(I32), 0).then_inc(setup, 1)
            V.memset(q_od[:, :, :].bitcast(I32), 0).then_inc(setup, 1)
            V.memset(q_tok[:, :, :, :], 0.0).then_inc(setup, 1)
            V.memset(ms[:, :, :], 0.0).then_inc(setup, 1)
            V.memset(z_st[:, :], 0.0).then_inc(setup, 1)
            V.memset(p0_t[:, :, :], 0.0).then_inc(setup, 1)
            V.memset(o_acc[:, :, :], 0.0).then_inc(setup, 1)
            for n in range(4):
                dve.wait_ge(w_hi_done, n + 1)
                V.tensor_tensor(wlo[:, :, n, :], wstage[:, :, n, :], whi[:, :, n, :], ALU.subtract)\
                    .then_inc(w_lo_done, 1)
            dve.wait_ge(setup, 14)

            def slot(b, s):
                if at := place(b, s, LAG["maxima"]):
                    c, t = at
                    dve.wait_ge(g_done.sem, g_done.after(c, t + 1))
                    dve.wait_ge(maxed.sem, maxed.after(c, PAIRS * (t + 1)))
                    V.tensor_tensor(mf[:, :], g_ps, mx[:, :], ALU.max).then_inc(mf_done.sem, 1)
                    dve.wait_ge(mf_done.sem, mf_done.after(c, t + 1))
                    dve.wait_ge(mst_done.sem, mst_done.after(c, t))
                    V.tensor_scalar(ms[:, :, 32:48], mf[:, :].unsqueeze(1).to_broadcast([P, 2, HEADS]),
                                    -1.0 / SHIFT_UNIT, None, ALU.mult).then_inc(ms_done.sem, 1)
                    dve.wait_ge(pg_done.sem, pg_done.after(c, t))
                    dve.wait_ge(ms_done.sem, ms_done.after(c, t + 1))
                    V.scalar_tensor_tensor(out=eg[:, :], in0=ms[:, 0, 32:48], scalar=SHIFT_UNIT, in1=g_ps,
                                           op0=ALU.mult, op1=ALU.add).then_inc(e_done.sem, 1)
                if s == 2 and (at := place(b, s, LAG["scores"])):
                    c = at[0]
                    dve.wait_ge(kst_copied.sem, kst_copied.after(c, 1))
                    dve.wait_ge(g_done.sem, g_done.after(c, 0))
                    V.tensor_copy(k0[:, :], k_st[:, :, HALF_W]).then_inc(k0_copied.sem, 1)
                    dve.wait_ge(qst_copied.sem, qst_copied.after(c, 2))
                    dve.wait_ge(s0_done.sem, s0_done.after(c, 0))
                    V.tensor_copy(z_st[0:64, 0:PAIRS * HEADS:HEADS + 2], q_ev[0:64, :, HALF_W])
                    V.tensor_copy(z_st[64:P, 1:PAIRS * HEADS:HEADS + 2], q_od[64:P, :, HALF_W])\
                        .then_inc(z_copied.sem, 1)

                def stats():
                    if at := place(b, s, LAG["stats"]):
                        c, t = at
                        dve.wait_ge(x_loaded[t].sem, x_loaded[t].after(c, 1))
                        V.bn_stats(st[:, t % 2, :], x_in[:, t, :]).then_inc(stats_raw.sem, 1)
                        dve.wait_ge(stats_raw.sem, stats_raw.after(c, t + 1))
                        dve.sem_inc(passed, 1)
                        V.bn_aggr(mv[:, t % 2, :], st[:, t % 2, :]).then_inc(stats_done.sem, 1)

                def norm():
                    if at := place(b, s, LAG["norm"]):
                        c, t = at
                        dve.wait_ge(rstd_done.sem, rstd_done.after(c, t + 1))
                        dve.wait_ge(spread.sem, spread.after(c, t - 1))
                        V.tensor_scalar(xn[:, t % 2, :], x_in[:, t, :], mv[:, t % 2, 0:1], rs[:, t % 2:t % 2 + 1],
                                        ALU.subtract, ALU.mult).then_inc(normed.sem, 1)

                def maxima(p):
                    if at := place(b, s, LAG["scores"]):
                        c, t = at
                        n = PAIRS * t + p
                        dve.wait_ge(scored.sem, scored.after(c, n + 1))
                        if p == 0:
                            dve.wait_ge(mf_done.sem, mf_done.after(c, t))
                        V.tensor_reduce(mx[:, 2 * p:2 * p + 2],
                                        bank_s[p % 2][:, 0:2 * WIN].rearrange("p (h k) -> p h k", h=2),
                                        AX.X, ALU.max).then_inc(maxed.sem, 1)

                def split_qk():
                    if at := place(b, s, LAG["project"]):
                        c, t = at
                        dve.wait_ge(qk_hi.sem, qk_hi.after(c, t + 1))
                        V.tensor_tensor(k_tok[:, :, 3, :], qk_ps[:, 1], k_tok[:, :, 0, :], ALU.subtract)
                        V.tensor_tensor(q_tok[:, :, 1, :], qk_ps[:, 0], q_tok[:, :, 0, :], ALU.subtract)\
                            .then_inc(qk_split.sem, 1)

                def shift_rows():
                    if at := place(b, s, LAG["maxima"]):
                        c, t = at
                        dve.wait_ge(mst_done.sem, mst_done.after(c, t + 1))
                        V.tensor_copy(q_ev[32:48, :, cols(t)],
                                      mst_ps[32:48, 0:P].unsqueeze(1).to_broadcast([16, PAIRS, P]))\
                            .then_inc(shift_ev.sem, 1)

                def copy_k():
                    if at := place(b, s, LAG["project"]):
                        c, t = at
                        dve.wait_ge(kst_done.sem, kst_done.after(c, t + 1))
                        if t == 0:
                            dve.wait_ge(s0_done.sem, s0_done.after(c, 0))
                        V.tensor_copy(k_st[:, :, cols(t)], kst_ps).then_inc(kst_copied.sem, 1)

                def split_o():
                    if at := place(b, s, LAG["out"]):
                        c, t = at
                        dve.wait_ge(ot_hi_done.sem, ot_hi_done.after(c, t + 1))
                        V.tensor_tensor(ot_lo[:, :, :], tr_ps, ot_hi[:, :, :], ALU.subtract).then_inc(ot_split.sem, 1)

                def split_x():
                    if at := place(b, s, LAG["spread"]):
                        c, t = at
                        dve.wait_ge(xt_hi_done.sem, xt_hi_done.after(c, t + 1))
                        V.tensor_tensor(xt_lo[:, :, :], tr_ps, xt_hi[:, :, :], ALU.subtract).then_inc(xt_split.sem, 1)

                def add_o(half):
                    if at := place(b, s, LAG["weigh"] + half):
                        c, t = at
                        dve.wait_ge(valued.sem, valued.after(c, 4 * t + 2 * half + 2))
                        src = bank_o[:, :].rearrange("p (g w) -> p g w", g=2)
                        dst = o_acc[:, 2 * half:2 * half + 2, s_of(t):s_of(t) + 2 * HALF_W]
                        dve.wait_ge(o_copied.sem, o_copied.after(c, 2 * t + half - 1))
                        if t == 0:
                            dve.wait_ge(gat_done.sem, gat_done.after(c, 2 - NB))
                            V.tensor_copy(dst, src[:, :, 0:2 * HALF_W]).then_inc(added.sem, 1)
                        else:
                            V.tensor_tensor(dst, src[:, :, 0:2 * HALF_W], dst, ALU.add).then_inc(added.sem, 1)

                def sums():
                    if at := place(b, s, LAG["gather"]):
                        c, t = at
                        dve.wait_ge(gat_done.sem, gat_done.after(c, t + 1))
                        dve.wait_ge(pg_done.sem, pg_done.after(c, t + 1))
                        V.tensor_tensor(den[:, :], gat_ps[:, :, HD], pg[:, t, :], ALU.add).then_inc(den_done.sem, 1)
                        dve.wait_ge(pgv_done.sem, pgv_done.after(c, t + 1))
                        dve.wait_ge(o_done.sem, o_done.after(c, t))
                        V.tensor_tensor(onum[:, :, :], gat_ps[:, :, 0:HD], pgv[:, :, :], ALU.add)
                        dve.wait_ge(den_done.sem, den_done.after(c, t + 1))
                        V.reciprocal(rec[:, :], den[:, :]).then_inc(num_done.sem, 1)

                def residual():
                    if at := place(b, s, LAG["out"]):
                        c, t = at
                        dve.wait_ge(wo_done.sem, wo_done.after(c, t + 1))
                        dve.wait_ge(res_loaded[t % 4].sem, res_loaded[t % 4].after(c, t // 4 + 1))
                        dve.wait_ge(y_stored[t % 2].sem, y_stored[t % 2].after(c, t // 2))
                        V.tensor_tensor(y_sb[:, t % 2, :], wo_ps, x_res[:, t % 4, :], ALU.add)\
                            .then_inc(y_ready.sem, 1)

                def max0():
                    if s == 0 and (at := place(b, s, NB)):
                        c = at[0]
                        dve.wait_ge(s0_copied.sem, s0_copied.after(c, 2))
                        V.tensor_reduce(m0[:, :], s0[:, :], AX.X, ALU.max).then_inc(m0_done.sem, 1)
                        dve.wait_ge(m0_done.sem, m0_done.after(c, 1))
                        V.tensor_scalar(nb0[:, :], m0[:, :], -SCALE, None, ALU.mult).then_inc(nb0_done.sem, 1)

                def sum0():
                    if s == 1 and (at := place(b, s, NB)):
                        c = at[0]
                        dve.wait_ge(p0_done.sem, p0_done.after(c, 1))
                        V.reciprocal(r0[:, :], l0[:, :]).then_inc(r0_done.sem, 1)
                        dve.wait_ge(r0_done.sem, r0_done.after(c, 1))
                        V.tensor_scalar(p0[:, :], p0[:, :], r0[:, 0:1], None, ALU.mult)\
                            .then_inc(p0_scaled.sem, 1)

                def copy_v0():
                    if s == 6 and (at := place(b, s, 6)):
                        c = at[0]
                        dve.wait_ge(v0_done.sem, v0_done.after(c, 1))
                        dve.wait_ge(pgv_done.sem, pgv_done.after(c, 0))
                        V.tensor_copy(v0[:, :, :], bank_m[:, 0:D].rearrange("p (h d) -> p h d", h=HEADS))\
                            .then_inc(v0_copied.sem, 1)

                maxima(0)
                add_o(1)
                maxima(1)
                split_qk()
                split_o()
                maxima(2)
                maxima(3)
                shift_rows()
                maxima(4)
                sum0()
                stats()
                max0()
                maxima(5)
                copy_k()
                split_x()
                maxima(6)
                add_o(0)
                sums()
                norm()
                copy_v0()
                maxima(7)
                residual()
                if isinstance(b, int) and b == batches and s < len(W.pieces()):
                    whole, high, low = W.pieces()[s]
                    dve.wait_ge(next_high, s + 1)
                    V.tensor_tensor(low, whole, high, ALU.subtract).then_inc(next_low, 1)
                if s == 1 and (at := place(b, s, NB)):
                    c = at[0]
                    dve.wait_ge(o0_done.sem, o0_done.after(c, 1))
                    V.tensor_tensor(o0_all[:, :], bank_qk[:, 0:D], own[:, :, :].rearrange("p h d -> p (h d)"),
                                    ALU.mult).then_inc(o0_scaled.sem, 1)

            def s_of(t):
                return t * P
            turns(dve, slot)
            dve.wait_ge(fin, 2)
            V.tensor_tensor(ot_lo[:, :, 0:batches], tr_ps[:, :, 0:batches], ot_hi[:, :, 0:batches],
                            ALU.subtract).then_inc(fin, 1)
            dve.wait_ge(fin, 4)
            dve.wait_ge(fin_dma, 32)
            V.tensor_tensor(y0_rows[:, :], wo_ps[0:batches, :], x0_rows[:, :], ALU.add).then_inc(fin, 1)

        @block.scalar
        def _(act):
            A = nc.scalar
            for n in range(4):
                act.wait_ge(w_in, 64)
                A.activation(whi[:, :, n, :], wstage[:, :, n, :], ACT.Copy).then_inc(w_hi_done, 1)
            act.wait_ge(setup, 14)

            def slot(b, s):
                if isinstance(b, int) and b == batches and s < len(W.pieces()):
                    if s == 0:
                        act.wait_ge(shared_loaded, 48)
                        act.wait_ge(w_lo_done, 4)
                    whole, high, _ = W.pieces()[s]
                    A.activation(high, whole, ACT.Copy).then_inc(next_high, 1)

                def exps(p):
                    if at := place(b, s, LAG["weigh"]):
                        c, t = at
                        n = PAIRS * t + p
                        act.wait_ge(weighed.sem, weighed.after(c, n + 1))
                        act.wait_ge(valued.sem, valued.after(c, 4 * t + p // 2 - 1))
                        A.activation(pt[:, p % 4, :, :], bank_w[p % 2][:, 0:2 * WIN]
                                     .rearrange("p (h k) -> p h k", h=2), ACT.Exp, scale=SCALE)\
                            .then_inc(exped.sem, 1)

                def qk_high():
                    if at := place(b, s, LAG["project"]):
                        c, t = at
                        act.wait_ge(qk_done.sem, qk_done.after(c, t + 1))
                        wide = [P, HEADS, 2, HD]
                        act.wait_ge(qst_done.sem, qst_done.after(c, t))
                        act.wait_ge(kst_done.sem, kst_done.after(c, t))
                        A.activation(q_tok[:, :, 0:4:3, :], qk_ps[:, 0].unsqueeze(2).to_broadcast(wide), ACT.Copy)
                        A.activation(k_tok[:, :, 0:2, :], qk_ps[:, 1].unsqueeze(2).to_broadcast(wide), ACT.Copy)\
                            .then_inc(qk_hi.sem, 1)

                def copy_v():
                    if at := place(b, s, LAG["project"]):
                        c, t = at
                        act.wait_ge(v_done.sem, v_done.after(c, t + 1))
                        if t < 2:
                            act.wait_ge(v_kept.sem, v_kept.after(c, 0))
                        else:
                            act.wait_ge(o0_done.sem, o0_done.after(c, 0))
                        act.wait_ge(v0_done.sem, v0_done.after(c, 0))
                        A.activation(v_sb[:, t, :, 0:HD], v_ps, ACT.Copy).then_inc(v_copied.sem, 1)

                def copy_q(odd):
                    if at := place(b, s, LAG["project"]):
                        c, t = at
                        act.wait_ge(qst_done.sem, qst_done.after(c, t + 1))
                        if t == 0:
                            act.wait_ge(z_copied.sem, z_copied.after(c, 0))
                        rows, to = (slice(64, P), q_od) if odd else (slice(0, 64), q_ev)
                        A.activation(to[rows, :, cols(t)], qst_ps[rows], ACT.Copy).then_inc(qst_copied.sem, 1)

                def o_high():
                    if at := place(b, s, LAG["out"]):
                        c, t = at
                        act.wait_ge(otr_done.sem, otr_done.after(c, t + 1))
                        act.wait_ge(wo_done.sem, wo_done.after(c, t))
                        A.activation(ot_hi[:, :, :], tr_ps, ACT.Copy).then_inc(ot_hi_done.sem, 1)

                def x_high():
                    if at := place(b, s, LAG["spread"]):
                        c, t = at
                        act.wait_ge(spread.sem, spread.after(c, t + 1))
                        act.wait_ge(v_done.sem, v_done.after(c, t))
                        A.activation(xt_hi[:, :, :], tr_ps, ACT.Copy).then_inc(xt_hi_done.sem, 1)

                def weight0():
                    if at := place(b, s, LAG["maxima"]):
                        c, t = at
                        act.wait_ge(e_done.sem, e_done.after(c, t + 1))
                        act.wait_ge(num_done.sem, num_done.after(c, t + 1 - NB))
                        near = near0[:, 1:2] if t == 0 else near0[:, 0:1]
                        A.activation(pg[:, t, :], eg[:, :], ACT.Exp, bias=near, scale=SCALE).then_inc(pg_done.sem, 1)

                def shift_rows():
                    if at := place(b, s, LAG["maxima"]):
                        c, t = at
                        act.wait_ge(mst_done.sem, mst_done.after(c, t + 1))
                        A.activation(q_od[96:112, :, cols(t)],
                                     mst_ps[96:112, 0:P].unsqueeze(1).to_broadcast([16, PAIRS, P]), ACT.Copy)\
                            .then_inc(shift_od.sem, 1)

                def copy_o(half):
                    if at := place(b, s, LAG["weigh"] + half):
                        c, t = at
                        act.wait_ge(added.sem, added.after(c, 2 * t + half + 1))
                        src = bank_o[:, :].rearrange("p (g w) -> p g w", g=2)
                        act.wait_ge(gat_done.sem, gat_done.after(c, t + 2 - NB))
                        A.activation(o_acc[:, 2 * half:2 * half + 2, t * P + 2 * HALF_W:t * P + WIN],
                                     src[:, :, 2 * HALF_W:WIN], ACT.Copy).then_inc(o_copied.sem, 1)

                last = place(b, s, NB)

                def copy_total0():
                    if s == 2 and last:
                        c = last[0]
                        act.wait_ge(o0_sum.sem, o0_sum.after(c, 1))
                        act.wait_ge(o0_stored.sem, o0_stored.after(c, 0))
                        A.activation(o0[:, :], bank_qk[0:1, D:2 * D], ACT.Copy).then_inc(o0_copied.sem, 1)

                def exp0():
                    if s == 0 and last:
                        c = last[0]
                        act.wait_ge(nb0_done.sem, nb0_done.after(c, 1))
                        act.wait_ge(p0t_done.sem, p0t_done.after(c, 0))
                        act.wait_ge(r0_done.sem, r0_done.after(c, 0))
                        A.activation(p0[:, :], s0[:, :], ACT.Exp, bias=nb0[:, 0:1], scale=SCALE, accum_out=l0[:, 0:1])\
                            .then_inc(p0_done.sem, 1)

                def copy_scores0(half):
                    if s == 0 and last:
                        c = last[0]
                        act.wait_ge(s0_done.sem, s0_done.after(c, half + 1))
                        A.activation(s0[:, half * 512:(half + 1) * 512], (bank_m, bank_v)[half][0:HEADS, :], ACT.Copy)\
                            .then_inc(s0_copied.sem, 1)

                exps(0)
                copy_total0()
                weight0()
                copy_scores0(0)
                qk_high()
                copy_scores0(1)
                exps(1)
                o_high()
                copy_v()
                exps(2)
                copy_o(1)
                exps(3)
                shift_rows()
                copy_q(0)
                exps(4)
                x_high()
                exps(5)
                exp0()
                copy_q(1)
                exps(6)
                copy_o(0)
                exps(7)
                if s == 1 and last:
                    c = last[0]
                    act.wait_ge(p0t_done.sem, p0t_done.after(c, 1))
                    A.activation(p0_t[:, :, 0:HEADS], bank_m[:, 0:NB * HEADS].rearrange("p (k h) -> p k h", k=NB), ACT.Copy)\
                        .then_inc(p0t_copied.sem, 1)
            turns(act, slot)
            act.wait_ge(fin, 1)
            A.activation(ot_hi[:, :, 0:batches], tr_ps[:, :, 0:batches], ACT.Copy).then_inc(fin, 1)

        @block.tensor
        def _(pe):
            T = nc.tensor
            pe.wait_ge(w_lo_done, 4)
            pe.wait_ge(setup, 14)

            def halves(out, left_hi, left_lo, n):
                last = None
                for f in range(FT):
                    for k, (l, w) in enumerate(((left_hi, whi), (left_hi, wlo), (left_lo, whi))):
                        last = T.matmul(out, l[:, f, :], w[:, f, n, :], start=f == k == 0,
                                        stop=f == FT - 1 and k == 2)
                return last

            def slot(b, s):
                last = place(b, s, NB)

                def weights0():
                    if s == 1 and last:
                        c = last[0]
                        pe.wait_ge(p0_scaled.sem, p0_scaled.after(c, 1))
                        if prev := place(b, s, LAG["spread"]):
                            pe.wait_ge(xt_split.sem, xt_split.after(prev[0], prev[1] + 1))
                        pe.sem_inc(passed, 1)
                        for k in range(NB):
                            mm = T.transpose(bank_m[:, k * HEADS:(k + 1) * HEADS], p0[:, k * P:(k + 1) * P],
                                             id32[0:HEADS, 0:HEADS])
                        mm.then_inc(p0t_done.sem, 1)

                def values0():
                    if s == 1 and last:
                        c = last[0]
                        pe.wait_ge(p0t_copied.sem, p0t_copied.after(c, 1))
                        pe.wait_ge(v_kept.sem, v_kept.after(c, 1))
                        if prev := place(b, s, LAG["gather"]):
                            pe.wait_ge(num_done.sem, num_done.after(prev[0], prev[1] + 1))
                        for k in range(NB):
                            v = v_keep[:, k, :, :] if k < 2 else v_sb[:, k, :, 0:HD]
                            i = 32 * (k % 4)
                            mm = T.matmul(bank_qk[i:i + 32, 0:D], p0_t[:, k, :], v, start=k < 4, stop=k >= NB - 4)
                        mm.then_inc(o0_done.sem, 1)

                def total0():
                    if s == 2 and last:
                        c = last[0]
                        pe.wait_ge(o0_scaled.sem, o0_scaled.after(c, 1))
                        pe.sem_inc(passed, 1)
                        T.matmul(bank_qk[0:1, D:2 * D], one_col[:, :], o0_all[:, :], start=True, stop=True)\
                            .then_inc(o0_sum.sem, 1)

                def scores0(half):
                    if s == 0 and last:
                        c = last[0]
                        pe.wait_ge(z_copied.sem, z_copied.after(c, 1))
                        pe.wait_ge(kst_copied.sem, kst_copied.after(c, NB))
                        prev = place(b, s, LAG["maxima"])
                        pe.wait_ge(e_done.sem, e_done.after(prev[0], prev[1] + 1))
                        if half == 0:
                            pe.wait_ge(s0_copied.sem, s0_copied.after(c, 0))
                        elif prev := place(b, s - 1, LAG["out"]):
                            pe.wait_ge(y_ready.sem, y_ready.after(prev[0], prev[1] + 1))
                        for j in range(PAIRS):
                            mm = T.matmul((bank_m, bank_v)[half][0:HEADS, :], z_st[:, j * HEADS:(j + 1) * HEADS],
                                          k_st[:, j, HALF_W + half * 512:HALF_W + (half + 1) * 512],
                                          start=j == 0, stop=j == PAIRS - 1)
                        mm.then_inc(s0_done.sem, 1)

                def project_qk():
                    if at := place(b, s, LAG["project"]):
                        c, t = at
                        pe.wait_ge(xt_split.sem, xt_split.after(c, t + 1))
                        pe.wait_ge(num_done.sem, num_done.after(c, t - LAG["gather"]))
                        pe.wait_ge(kst_copied.sem, kst_copied.after(c, t))
                        if s == 2 and last:
                            pe.wait_ge(o0_copied.sem, o0_copied.after(last[0], 1))
                        halves(bank_qk[:, :], xt_hi, xt_lo, slice(0, 2)).then_inc(qk_done.sem, 1)

                def project_v():
                    if at := place(b, s, LAG["project"]):
                        c, t = at
                        pe.wait_ge(qst_copied.sem, qst_copied.after(c, 2 * t))
                        if prev := place(b, s - 1, LAG["out"]):
                            pe.wait_ge(y_ready.sem, y_ready.after(prev[0], prev[1] + 1))
                        if s == 0 and last:
                            pe.wait_ge(s0_copied.sem, s0_copied.after(last[0], 2))
                        halves(bank_v[:, 0:D], xt_hi, xt_lo, 2).then_inc(v_done.sem, 1)

                def scores(p):
                    if at := place(b, s, LAG["scores"]):
                        c, t = at
                        n = PAIRS * t + p
                        bank = bank_s[p % 2]
                        variant = 1 if t == 0 else 2 if t == NB - 1 else 0
                        if p == 0:
                            pe.wait_ge(kst_copied.sem, kst_copied.after(c, min(t + 2, NB)))
                            pe.wait_ge(qst_copied.sem, qst_copied.after(c, 2 * (t + 1)))
                        pe.wait_ge(maxed.sem, maxed.after(c, n - 1))
                        for i, q in enumerate((q_ev, q_od)):
                            T.matmul(bank[:, i * WIN:(i + 1) * WIN], q[:, p, cols(t)],
                                     k_st[:, p, cols(t, HALF_W)], start=i == 0, stop=False,
                                     skip_group_check=True)
                        T.matmul(bank[:, 0:2 * WIN], idb[:, :],
                                 band[:, variant, :].unsqueeze(1).to_broadcast([P, 2, WIN]), start=False, stop=True,
                                 skip_group_check=True).then_inc(scored.sem, 1)

                def weigh(p):
                    if at := place(b, s, LAG["weigh"]):
                        c, t = at
                        n = PAIRS * t + p
                        bank = bank_w[p % 2]
                        if p == 0:
                            pe.wait_ge(shift_ev.sem, shift_ev.after(c, min(t + 2, NB)))
                            pe.wait_ge(shift_od.sem, shift_od.after(c, min(t + 2, NB)))
                            pe.wait_ge(qst_copied.sem, qst_copied.after(c, 2 * min(t + 2, NB)))
                        pe.wait_ge(exped.sem, exped.after(c, n - 1))
                        for i, q in enumerate((q_ev, q_od)):
                            mm = T.matmul(bank[:, i * WIN:(i + 1) * WIN], k_st[:, p, cols(t)],
                                          q[:, p, cols(t, HALF_W)], start=True, stop=True)
                        mm.then_inc(weighed.sem, 1)

                def values(g):
                    if at := place(b, s, LAG["weigh"] + g // 2):
                        c, t = at
                        if g == 0:
                            pe.wait_ge(v_copied.sem, v_copied.after(c, t + 1))
                        if g % 2 == 0:
                            pe.wait_ge(o_copied.sem, o_copied.after(c, 2 * t + g // 2))
                        pe.wait_ge(cut.sem, cut.after(c, PAIRS * t + 2 * g + 2))
                        for i in range(4):
                            h = 4 * g + i
                            mm = T.matmul(bank_o[32 * i:32 * i + 32, (g % 2) * 256:(g % 2) * 256 + WIN],
                                          v_sb[:, t, h, :], pt[:, (h // 2) % 4, h % 2, :], start=True, stop=True)
                        mm.then_inc(valued.sem, 1)

                def rows_of_o():
                    if at := place(b, s, LAG["out"]):
                        c, t = at
                        pe.wait_ge(o_done.sem, o_done.after(c, t + 1))
                        if prev := place(b, s, LAG["maxima"]):
                            pe.wait_ge(e_done.sem, e_done.after(prev[0], prev[1] + 1))
                        if s == 0:
                            pe.wait_ge(s0_copied.sem, s0_copied.after(c, 1))
                        for f in range(FT):
                            mm = T.transpose(tr_ps[:, f, :], o_tok[:, 8 * f:8 * f + 8, :].rearrange("p h d -> p (h d)"),
                                             id32[:, :])
                        mm.then_inc(otr_done.sem, 1)

                def shift_rows():
                    if at := place(b, s, LAG["maxima"]):
                        c, t = at
                        pe.wait_ge(ms_done.sem, ms_done.after(c, t + 1))
                        pe.wait_ge(e_done.sem, e_done.after(c, t + 1))
                        if prev := place(b, s, LAG["out"]):
                            pe.wait_ge(ot_split.sem, ot_split.after(prev[0], prev[1] + 1))
                        T.transpose(mst_ps[:, 0:P], ms[:, :, :].rearrange("p a c -> p (a c)"), id16[:, :]).then_inc(mst_done.sem, 1)

                def stack_k():
                    if at := place(b, s, LAG["project"]):
                        c, t = at
                        pe.wait_ge(qk_split.sem, qk_split.after(c, t + 1))
                        for j in range(PAIRS):
                            mm = T.transpose(kst_ps[:, j, :], k_tok[:, 2 * j:2 * j + 2].rearrange("p h r d -> p (h r d)"),
                                             id16[:, :])
                        mm.then_inc(kst_done.sem, 1)

                def stack_q():
                    if at := place(b, s, LAG["project"]):
                        c, t = at
                        pe.wait_ge(qk_split.sem, qk_split.after(c, t + 1))
                        pe.wait_ge(v_copied.sem, v_copied.after(c, t + 1))
                        for j in range(PAIRS):
                            mm = T.transpose(qst_ps[:, j, :], q_tok[:, 2 * j:2 * j + 2].rearrange("p h r d -> p (h r d)"),
                                             id16[:, :])
                        mm.then_inc(qst_done.sem, 1)

                def gather():
                    if at := place(b, s, LAG["gather"]):
                        c, t = at
                        pe.wait_ge(o_copied.sem, o_copied.after(c, 2 * min(t + 2, NB)))
                        if prev := place(b, s, LAG["project"]):
                            pe.wait_ge(kst_copied.sem, kst_copied.after(prev[0], prev[1] + 1))
                        for g in range(4):
                            mm = T.transpose(bank_qk[:, g * P:(g + 1) * P], o_acc[:, g, cols(t)], id32[:, :])
                        mm.then_inc(gat_done.sem, 1)

                def out():
                    if at := place(b, s, LAG["out"]):
                        c, t = at
                        pe.wait_ge(ot_split.sem, ot_split.after(c, t + 1))
                        if prev := place(b, s, LAG["project"]):
                            pe.wait_ge(qst_copied.sem, qst_copied.after(prev[0], 2 * (prev[1] + 1)))
                        halves(wo_ps, ot_hi, ot_lo, 3).then_inc(wo_done.sem, 1)

                def spread_x():
                    if at := place(b, s, LAG["spread"]):
                        c, t = at
                        pe.wait_ge(normed.sem, normed.after(c, t + 1))
                        if prev := place(b, s, LAG["maxima"]):
                            pe.wait_ge(shift_ev.sem, shift_ev.after(prev[0], prev[1] + 1))
                            pe.wait_ge(shift_od.sem, shift_od.after(prev[0], prev[1] + 1))
                        if prev := place(b, s, LAG["out"]):
                            pe.wait_ge(ot_split.sem, ot_split.after(prev[0], prev[1] + 1))
                        for f in range(FT):
                            mm = T.transpose(tr_ps[:, f, :], xn[:, t % 2, f * P:(f + 1) * P], id32[:, :])
                        mm.then_inc(spread.sem, 1)

                def key0():
                    if at := place(b, s, LAG["scores"]):
                        c, t = at
                        pe.wait_ge(k0_copied.sem, k0_copied.after(c, 1))
                        if s == 1 and last:
                            pe.wait_ge(p0t_copied.sem, p0t_copied.after(last[0], 1))
                        if s == 6:
                            pe.wait_ge(v0_copied.sem, v0_copied.after(c, 1))
                        if prev := place(b, s, LAG["spread"]):
                            pe.wait_ge(xt_split.sem, xt_split.after(prev[0], prev[1] + 1))
                        for j in range(PAIRS):
                            for i, q in enumerate((q_ev, q_od)):
                                mm = T.matmul(g_ps[:, 2 * j + i:2 * j + i + 1], q[:, j, cols(t)], k0[:, j:j + 1],
                                              start=True, stop=True)
                        mm.then_inc(g_done.sem, 1)

                def first_values():
                    if s == 6 and (at := place(b, s, 6)):
                        c = at[0]
                        if prev := place(b, s, LAG["spread"]):
                            pe.wait_ge(xt_split.sem, xt_split.after(prev[0], prev[1] + 1))
                        pe.wait_ge(v_copied.sem, v_copied.after(c, 1))
                        T.matmul(bank_m[:, 0:D], first_row[:, :], v_sb[:, 0, :, 0:HD], start=True, stop=True)\
                            .then_inc(v0_done.sem, 1)

                scores(0), weigh(0)
                values(2)
                total0()
                project_qk()
                values(3)
                scores0(0)
                scores0(1)
                scores(1), weigh(1)
                rows_of_o()
                project_v()
                scores(2), weigh(2)
                scores(3), weigh(3)
                shift_rows()
                stack_q()
                scores(4), weigh(4)
                stack_k()
                values(0)
                scores(5), weigh(5)
                spread_x()
                values(1)
                scores(6), weigh(6)
                gather()
                first_values()
                scores(7), weigh(7)
                weights0()
                out()
                key0()
                values0()
            turns(pe, slot)
            pe.wait_ge(fin_dma, 32)
            for f in range(FT):
                mm = T.transpose(tr_ps[:, f, 0:batches], o0_rows[:, f * P:(f + 1) * P], id32[0:batches, 0:batches])
            mm.then_inc(fin, 1)
            pe.wait_ge(fin, 3)
            for f in range(FT):
                for k, (l, w) in enumerate(((ot_hi, whi), (ot_hi, wlo), (ot_lo, whi))):
                    mm = T.matmul(wo_ps[0:batches, :], l[:, f, 0:batches], w[:, f, 3, :], start=f == k == 0,
                                  stop=f == FT - 1 and k == 2)
            mm.then_inc(fin, 1)


EXPERTS, TOP, FF = 7, 2, 1024
FC = FF // P
CAPACITY = 732
SUB = 122
CHUNK_BLOCKS = 3
SLOT_BLOCKS = CAPACITY // SUB
NOWHERE = 1 << 20


def parts(tensor):
    if len(tensor.shape) == 4:
        return [tensor[:, k, i] for k in range(2) for i in range(FT)]
    return [tensor[:, h * FC // 2:(h + 1) * FC // 2] for h in range(2)]


class Weights:

    def __init__(self, sb):
        self.stage_up = sb("stage_up", [P, 2, FT, FF], F32)
        self.stage_down = sb("stage_down", [P, FC, D], F32)
        self.up_hi = sb("up_hi", [P, 2, FT, FF], FP16)
        self.up_lo = sb("up_lo", [P, 2, FT, FF], FP16)
        self.down_hi = sb("down_hi", [P, FC, D], FP16)
        self.down_lo = sb("down_lo", [P, FC, D], FP16)

    def pieces(self):
        return (list(zip(parts(self.stage_up), parts(self.up_hi), parts(self.up_lo)))
                + list(zip(parts(self.stage_down), parts(self.down_hi), parts(self.down_lo))))

    def load(self, sp, w1, w3, w2, done):
        sp.dma_start(self.stage_up[:, 0], w1.rearrange("(f p) o -> p f o", p=P)).then_inc(done, 16)
        sp.dma_start(self.stage_up[:, 1], w3.rearrange("(f p) o -> p f o", p=P)).then_inc(done, 16)
        sp.dma_start(self.stage_down[:, :, :], w2.rearrange("(f p) o -> p f o", p=P)).then_inc(done, 16)


def shared_ffn(nc, W, persist, w_loaded, y, g, b_, wr, ew1, ew3, ew2, z, out, ew_loaded):
    batches = y.shape[0]
    NCH = 2
    CT = 512
    CB = CT // P
    y_v = y.rearrange("b (s j p) d -> b s p j d", p=P, j=CB)
    z_v = z.rearrange("(b s j p) d -> b s p j d", p=P, j=CB, s=NCH)
    out_v = out.rearrange("b (s j p) d -> b s p j d", p=P, j=CB)
    logits, gcol, bcol, wr_hi, wr_lo, id32 = persist

    ctx = ExitStack()
    with nc.cleanup_on_exit(), ctx:
        sb, ps = tensors(ctx, nc)
        signals = []

        def sig(name, per=NCH, unit=1):
            s = Signal(nc, name, per, unit)
            signals.append(s)
            return s

        y_in = sb("f_y_in", [P, 2, CB, D], F32)
        st = sb("f_st", [P, CB, 6], F32)
        mv = sb("f_mv", [P, CB, 2], F32)
        mhalf = sb("f_mhalf", [P, CB], F32)
        tmp = sb("f_tmp", [P, 6, CB], F32)
        fac = sb("f_fac", [P, CB], F32)
        z_sb = sb("f_z_sb", [P, CB, D], F32)
        h32 = sb("f_h32", [P, FT, CT], F32)
        h_hi = sb("f_h_hi", [P, 2, FT, CT], FP16)
        h_lo = sb("f_h_lo", [P, 2, FT, CT], FP16)
        th = sb("f_th", [P, 2, CT], F32)
        u = sb("f_u", [P, 2, CT], F32)
        g32 = sb("f_g32", [P, 3, CT], F32)
        g_hi = sb("f_g_hi", [P, FC, CT], FP16)
        g_lo = sb("f_g_lo", [P, FC, CT], FP16)
        o_sb = sb("f_o_sb", [P, CB, D], F32)
        wr32 = sb("f_wr32", [P, FT, EXPERTS], F32)

        bank_a = [ps(f"f_bank_a{i}", [P, CT]) for i in range(2)]
        bank_b = [ps(f"f_bank_b{i}", [P, CT]) for i in range(2)]
        bank_d = [ps(f"f_bank_d{i}", [P, CT]) for i in range(2)]
        bank_t = [ps(f"f_bank_t{i}", [P, CT]) for i in range(2)]

        small = nc.alloc_semaphore("f_small")
        small_ready = nc.alloc_semaphore("f_small_ready")
        setup = nc.alloc_semaphore("f_setup")
        passed = nc.alloc_semaphore("f_passed")
        y_loaded = [sig(f"f_y_loaded{i}", 1, 16) for i in range(2)]
        z_stored = sig("f_z_stored", NCH, 16)
        o_stored = sig("f_o_stored", NCH, 16)
        (stats_raw, stats_done, pv1, pv2, pv3, pv4, pv5, pv6, fac_done, z_ready, h_hi_done, h_done,
         logit_done, logit_copied, o_ready) = [sig("f_" + n) for n in (
             "stats_raw", "stats_done", "pv1", "pv2", "pv3", "pv4", "pv5", "pv6", "fac_done", "z_ready",
             "h_hi_done", "h_done", "logit_done", "logit_copied", "o_ready")]
        turned = sig("f_turned", FT * NCH)
        h32_done = sig("f_h32_done", FT * NCH)
        (up_a, up_b, gated, u_done, g_done, g_hi_done, g_split, down_done) = [sig("f_" + n, FC * NCH) for n in (
            "up_a", "up_b", "gated", "u_done", "g_done", "g_hi_done", "g_split", "down_done")]
        block = ctx.enter_context(nc.Block())

        def place(b, s, lag):
            q = s - lag
            batch = b + q // NCH
            if isinstance(b, int) and not 0 <= batch < batches:
                return None
            return batch, q % NCH

        def turns(engine, body):
            body(0, -1)
            for s in range(NCH):
                body(0, s)
            with engine.Fori(1, batches - 1) as b:
                for s in range(NCH):
                    body(b, s)
            for s in range(NCH):
                body(batches - 1, s)
            body(batches, 0)

        @block.sync
        def _(sp):
            for s in signals:
                if s.unit == 16:
                    s.start(sp)
            sp.dma_start(wr32[:, :, :], wr.rearrange("(f p) o -> p f o", p=P)).then_inc(small, 16)
            sp.dma_start(gcol[:, :], g).then_inc(small, 16)
            sp.dma_start(bcol[:, :], b_).then_inc(small, 16)

            def slot(b, s):
                if at := place(b, s, -1):
                    c, t = at
                    sp.wait_ge(o_ready.sem, o_ready.after(c, t - 1))
                    sp.sem_inc(passed, 1)
                    sp.dma_start(y_in[:, t], y_v[c, t]).then_inc(y_loaded[t].sem, 16)
                    sp.wait_ge(z_ready.sem, z_ready.after(c, t + 1))
                    sp.dma_start(z_v[c, t], z_sb[:, :, :]).then_inc(z_stored.sem, 16)
                if at := place(b, s, 1):
                    c, t = at
                    sp.wait_ge(o_ready.sem, o_ready.after(c, t + 1))
                    sp.sem_inc(passed, 1)
                    sp.dma_start(out_v[c, t], o_sb[:, :, :]).then_inc(o_stored.sem, 16)
                if isinstance(b, int) and b == 0 and s == 0:
                    W.load(sp, ew1[0], ew3[0], ew2[0], ew_loaded)
            turns(sp, slot)
            sp.wait_ge(z_stored.sem, z_stored.after(batches - 1, NCH))
            sp.wait_ge(o_stored.sem, o_stored.after(batches - 1, NCH))
            sp.wait_ge(ew_loaded, 48)

        @block.gpsimd
        def _(pool):
            G = nc.gpsimd
            for s in signals:
                if s.unit == 1:
                    s.start(pool)
            G.memset(mhalf[:, :], -0.5).then_inc(setup, 1)
            pool.wait_ge(setup, 1)

            def slot(b, s):
                def factor():
                    if at := place(b, s, -1):
                        c, t = at
                        n = t + 1
                        var = mv[:, :, 1]
                        pool.wait_ge(stats_done.sem, stats_done.after(c, n))
                        pool.sem_inc(passed, 1)
                        G.tensor_scalar(tmp[:, 0], var, EPS, None, ALU.add).then_inc(pv1.sem, 1)
                        pool.wait_ge(pv1.sem, pv1.after(c, n))
                        G.tensor_tensor(tmp[:, 1], tmp[:, 0], mhalf[:, :], ALU.pow).then_inc(pv2.sem, 1)
                        pool.wait_ge(pv2.sem, pv2.after(c, n))
                        G.tensor_tensor(tmp[:, 2], var, tmp[:, 1], ALU.mult).then_inc(pv3.sem, 1)
                        pool.wait_ge(pv3.sem, pv3.after(c, n))
                        G.tensor_tensor(tmp[:, 3], tmp[:, 2], tmp[:, 1], ALU.mult).then_inc(pv4.sem, 1)
                        pool.wait_ge(pv4.sem, pv4.after(c, n))
                        pool.sem_inc(passed, 1)
                        G.tensor_scalar(tmp[:, 4], tmp[:, 3], EPS, None, ALU.add).then_inc(pv5.sem, 1)
                        pool.wait_ge(pv5.sem, pv5.after(c, n))
                        G.tensor_tensor(tmp[:, 5], tmp[:, 4], mhalf[:, :], ALU.pow).then_inc(pv6.sem, 1)
                        pool.wait_ge(pv6.sem, pv6.after(c, n))
                        G.tensor_tensor(fac[:, :], tmp[:, 5], tmp[:, 1], ALU.mult).then_inc(fac_done.sem, 1)

                def low(f):
                    if at := place(b, s, 0):
                        c, t = at
                        n = FC * t + f
                        pool.wait_ge(g_hi_done.sem, g_hi_done.after(c, n + 1))
                        pool.wait_ge(down_done.sem, down_done.after(c, n + 1 - FC))
                        G.tensor_tensor(g_lo[:, f], g32[:, f % 2], g_hi[:, f], ALU.subtract).then_inc(g_split.sem, 1)

                def low_h():
                    if at := place(b, s, -1):
                        c, t = at
                        pool.wait_ge(h_hi_done.sem, h_hi_done.after(c, t + 1))
                        G.tensor_tensor(h_lo[:, t], h32[:, :, :], h_hi[:, t], ALU.subtract).then_inc(h_done.sem, 1)
                low(0), low(1)
                factor()
                low(2), low(3), low(4)
                low_h()
                low(5), low(6), low(7)
            turns(pool, slot)

        @block.vector
        def _(dve):
            V = nc.vector
            dve.wait_ge(small, 48)
            V.tensor_copy(wr_hi[:, :, :], wr32[:, :, :]).then_inc(small_ready, 1)
            dve.wait_ge(small_ready, 1)
            V.tensor_tensor(wr_lo[:, :, :], wr32[:, :, :], wr_hi[:, :, :], ALU.subtract).then_inc(small_ready, 1)

            def slot(b, s):
                def stats():
                    if at := place(b, s, -1):
                        c, t = at
                        dve.wait_ge(y_loaded[t].sem, y_loaded[t].after(c, 1))
                        for j in range(CB):
                            i = V.bn_stats(st[:, j], y_in[:, t, j])
                        i.then_inc(stats_raw.sem, 1)
                        dve.wait_ge(stats_raw.sem, stats_raw.after(c, t + 1))
                        dve.sem_inc(passed, 1)
                        for j in range(CB):
                            i = V.bn_aggr(mv[:, j], st[:, j])
                        i.then_inc(stats_done.sem, 1)

                def norm():
                    if at := place(b, s, -1):
                        c, t = at
                        dve.wait_ge(fac_done.sem, fac_done.after(c, t + 1))
                        dve.wait_ge(z_stored.sem, z_stored.after(c, t))
                        dve.wait_ge(turned.sem, turned.after(c, FT * t))
                        for j in range(CB):
                            i = V.tensor_scalar(z_sb[:, j], y_in[:, t, j], mv[:, j, 0:1], fac[:, j:j + 1],
                                                ALU.subtract, ALU.mult)
                        i.then_inc(z_ready.sem, 1)

                def gate(f):
                    if at := place(b, s, 0):
                        c, t = at
                        n = FC * t + f
                        dve.wait_ge(gated.sem, gated.after(c, n + 1))
                        dve.wait_ge(g_done.sem, g_done.after(c, n - 1))
                        V.scalar_tensor_tensor(out=u[:, f % 2], in0=th[:, f % 2], scalar=1.0, in1=bank_a[f % 2][:, :],
                                               op0=ALU.add, op1=ALU.mult).then_inc(u_done.sem, 1)
                        dve.wait_ge(u_done.sem, u_done.after(c, n + 1))
                        dve.wait_ge(up_b.sem, up_b.after(c, n + 1))
                        dve.wait_ge(g_split.sem, g_split.after(c, n - 1))
                        V.tensor_tensor(g32[:, f % 2], bank_b[f % 2][:, :], u[:, f % 2], ALU.mult)\
                            .then_inc(g_done.sem, 1)

                def finish():
                    if at := place(b, s, 1):
                        c, t = at
                        dve.wait_ge(down_done.sem, down_done.after(c, FC * (t + 1)))
                        dve.wait_ge(o_stored.sem, o_stored.after(c, t))
                        for i in range(2):
                            ins = V.scalar_tensor_tensor(
                                out=o_sb[:, 2 * i:2 * i + 2].rearrange("p j d -> p (j d)"), in0=bank_d[i][:, :], scalar=0.5,
                                in1=y_in[:, t, 2 * i:2 * i + 2].rearrange("p j d -> p (j d)"),
                                op0=ALU.mult, op1=ALU.add)
                        ins.then_inc(o_ready.sem, 1)

                def keep_logits():
                    if at := place(b, s, -1):
                        c, t = at
                        dve.wait_ge(logit_done.sem, logit_done.after(c, t + 1))
                        n = c * (NCH * CB) + t * CB
                        V.tensor_copy(logits[:, bass.ds(n, CB), :],
                                      bank_t[0][:, 0:CB * 8].rearrange("p (j e) -> p j e", e=8)[:, :, 0:EXPERTS])\
                            .then_inc(logit_copied.sem, 1)
                gate(0), gate(1)
                finish()
                stats()
                gate(2), gate(3)
                norm()
                gate(4), gate(5), gate(6), gate(7)
                keep_logits()
            turns(dve, slot)

        @block.scalar
        def _(act):
            A = nc.scalar
            act.wait_ge(w_loaded, 48)

            def slot(b, s):
                def gate(f):
                    if at := place(b, s, 0):
                        c, t = at
                        n = FC * t + f
                        act.wait_ge(up_a.sem, up_a.after(c, n + 1))
                        act.wait_ge(u_done.sem, u_done.after(c, n - 1))
                        A.activation(th[:, f % 2], bank_a[f % 2][:, :], ACT.Tanh, scale=0.5).then_inc(gated.sem, 1)

                def high(f, lag=0):
                    if at := place(b, s, lag):
                        c, t = at
                        n = FC * t + f
                        act.wait_ge(g_done.sem, g_done.after(c, n + 1))
                        act.wait_ge(down_done.sem, down_done.after(c, n + 1 - FC))
                        A.activation(g_hi[:, f], g32[:, f % 2], ACT.Copy).then_inc(g_hi_done.sem, 1)

                def affine():
                    if at := place(b, s, -1):
                        c, t = at
                        for i in range(FT):
                            act.wait_ge(turned.sem, turned.after(c, FT * t + i + 1))
                            act.wait_ge(h_done.sem, h_done.after(c, t))
                            A.activation(h32[:, i], bank_t[i][:, :], ACT.Identity, bias=bcol[:, i:i + 1],
                                         scale=gcol[:, i:i + 1]).then_inc(h32_done.sem, 1)
                        act.wait_ge(h32_done.sem, h32_done.after(c, FT * t + FT))
                        A.activation(h_hi[:, t], h32[:, :, :], ACT.Copy).then_inc(h_hi_done.sem, 1)
                gate(0)
                for f in range(1, FC):
                    gate(f)
                    high(f - 1)
                    if f == 5:
                        affine()
                high(FC - 1)
            turns(act, slot)

        @block.tensor
        def _(pe):
            T = nc.tensor
            pe.wait_ge(small_ready, 2)

            def slot(b, s):
                def up(f):
                    if at := place(b, s, 0):
                        c, t = at
                        n = FC * t + f
                        if f == 0:
                            pe.wait_ge(h_done.sem, h_done.after(c, t + 1))
                        pe.wait_ge(u_done.sem, u_done.after(c, n - 1))
                        pe.wait_ge(g_done.sem, g_done.after(c, n - 1))
                        for k, (bank, done) in enumerate(((bank_a, up_a), (bank_b, up_b))):
                            for i in range(FT):
                                w_hi = W.up_hi[:, k, i, f * P:(f + 1) * P]
                                w_lo = W.up_lo[:, k, i, f * P:(f + 1) * P]
                                T.matmul(bank[f % 2][:, :], w_hi, h_hi[:, t, i], start=i == 0, stop=False)
                                T.matmul(bank[f % 2][:, :], w_hi, h_lo[:, t, i], start=False, stop=False)
                                mm = T.matmul(bank[f % 2][:, :], w_lo, h_hi[:, t, i], start=False, stop=i == FT - 1)
                            mm.then_inc(done.sem, 1)

                def down(f, lag):
                    if at := place(b, s, lag):
                        c, t = at
                        n = FC * t + f
                        if f == 0:
                            pe.wait_ge(o_ready.sem, o_ready.after(c, t))
                        pe.wait_ge(g_split.sem, g_split.after(c, n + 1))
                        for j in range(CB):
                            o = bank_d[j // 2][:, (j % 2) * D:(j % 2 + 1) * D]
                            tok = slice(j * P, (j + 1) * P)
                            for k, (l, w) in enumerate(((g_hi, W.down_hi), (g_hi, W.down_lo), (g_lo, W.down_hi))):
                                mm = T.matmul(o, l[:, f, tok], w[:, f, :], start=f == k == 0 and j % 2 == 0,
                                              stop=f == FC - 1 and k == 2, skip_group_check=True)
                        mm.then_inc(down_done.sem, 1)

                def turn():
                    if at := place(b, s, -1):
                        c, t = at
                        pe.wait_ge(z_ready.sem, z_ready.after(c, t + 1))
                        pe.wait_ge(logit_copied.sem, logit_copied.after(c, t))
                        for i in range(FT):
                            pe.wait_ge(h32_done.sem, h32_done.after(c, FT * (t - 1) + i + 1))
                            for j in range(CB):
                                mm = T.transpose(bank_t[i][:, j * P:(j + 1) * P], z_sb[:, j, i * P:(i + 1) * P],
                                                 id32[:, :])
                            mm.then_inc(turned.sem, 1)

                def route():
                    if at := place(b, s, -1):
                        c, t = at
                        pe.wait_ge(h_done.sem, h_done.after(c, t + 1))
                        for j in range(CB):
                            tok = slice(j * P, (j + 1) * P)
                            for i in range(FT):
                                for k, (l, w) in enumerate(((h_hi, wr_hi), (h_hi, wr_lo), (h_lo, wr_hi))):
                                    mm = T.matmul(bank_t[0][:, j * 8:j * 8 + EXPERTS], l[:, t, i, tok], w[:, i, :],
                                                  start=i == k == 0, stop=i == FT - 1 and k == 2)
                        mm.then_inc(logit_done.sem, 1)
                up(0)
                down(FC - 2, 1)
                up(1)
                down(FC - 1, 1)
                for f in range(2, FC):
                    up(f)
                    down(f - 2, 0)
                    if f == 5:
                        turn()
                route()
            turns(pe, slot)


def route(nc, W, ew_loaded, logits, gather_rows, scatter_rows, batches):
    TT = logits.shape[1]
    BLOCKS = EXPERTS * SLOT_BLOCKS
    E = EXPERTS
    STEP = 32
    NSTEP = TOP * TT // STEP
    ctx = ExitStack()
    with nc.cleanup_on_exit(), ctx:
        sb, ps = tensors(ctx, nc)
        rank = sb("r_rank", [P, E], F32)
        eq = sb("r_eq", [P, TT, E], F32)
        rk = sb("r_rk", [P, TT, E], F32)
        top = sb("r_top", [P, TT], F32)
        win = sb("r_win", [P, TOP, TT], F32)
        oh = sb("r_oh", [P, TOP, TT, E], BF16)
        left = sb("r_left", [P, TT, E], F32)
        upto = sb("r_upto", [P, P], BF16)
        ones = sb("r_ones", [P, P], BF16)
        run = [sb(f"r_run{i}", [P, TOP * TT, E], F32) for i in range(2)]
        pos = sb("r_pos", [P, TOP * TT, E], F32)
        posn = sb("r_posn", [P, TOP * TT], F32)
        over = sb("r_over", [P, TOP * TT], F32)
        blk = [sb(f"r_blk{i}", [P, TOP * TT], F32) for i in range(2)]
        inner = sb("r_inner", [P, TOP * TT], F32)
        base = sb("r_base", [P, TOP * TT], F32)
        slot_of = sb("r_slot", [P, TOP * TT], F32)
        iota_in = sb("r_iota_in", [P, P], F32)
        iota_bl = sb("r_iota_bl", [P, BLOCKS], F32)
        iota_t = sb("r_iota_t", [P, TOP, TT], F32)
        iota_p = sb("r_iota_p", [P, 1], F32)
        oh_in = sb("r_oh_in", [P, 2, STEP, P], BF16)
        oh_bl = sb("r_oh_bl", [P, 2, STEP, BLOCKS], BF16)
        val = sb("r_val", [P, 2, STEP, 2, BLOCKS], BF16)
        tab = sb("r_tab", [P, 2, BLOCKS], F32)
        tok = sb("r_tok", [P, BLOCKS], F32)
        tok2 = sb("r_tok2", [P, BLOCKS], F32)
        none = sb("r_none", [P, BLOCKS], F32)
        fin = sb("r_fin", [P, 2, BLOCKS], F32)
        banks = [ps(f"r_bank{i}", [P, 512]) for i in range(8)]

        made = nc.alloc_semaphore("r_made")
        raw = nc.alloc_semaphore("r_raw")
        step_done = nc.alloc_semaphore("r_step_done")
        chosen = nc.alloc_semaphore("r_chosen")
        counted = nc.alloc_semaphore("r_counted")
        hot = nc.alloc_semaphore("r_hot")
        tiles_in = nc.alloc_semaphore("r_tiles_in")
        rows_in = nc.alloc_semaphore("r_rows_in")
        high0 = nc.alloc_semaphore("r_high0")
        low0 = nc.alloc_semaphore("r_low0")
        placed = nc.alloc_semaphore("r_placed")
        block = ctx.enter_context(nc.Block())

        @block.gpsimd
        def _(pool):
            G = nc.gpsimd
            exact = dict(allow_small_or_imprecise_dtypes=True)
            G.iota(rank[:, :], pattern=[[-1, E]], base=E, channel_multiplier=0, **exact).then_inc(made, 1)
            G.iota(iota_in[:, :], pattern=[[1, P]], base=0, channel_multiplier=0, **exact).then_inc(made, 1)
            G.iota(iota_bl[:, :], pattern=[[1, BLOCKS]], base=0, channel_multiplier=0, **exact).then_inc(made, 1)
            G.iota(iota_t[:, :, :], pattern=[[0, TOP], [1, TT]], base=1, channel_multiplier=0, **exact)\
                .then_inc(made, 1)
            G.iota(iota_p[:, :], pattern=[[0, 1]], base=0, channel_multiplier=1, **exact).then_inc(made, 1)
            G.memset(ones[:, :], 1.0).then_inc(made, 1)
            G.memset(upto[:, :], 1.0).then_inc(raw, 1)
            pool.wait_ge(raw, 1)
            G.affine_select(out=upto[:, :], in_=upto[:, :], compare_op=ALU.is_ge, fill=0.0, base=0,
                            channel_multiplier=-1, pattern=[[1, P]]).then_inc(made, 1)
            pool.wait_ge(made, 7)
            for n, (whole, high, low) in enumerate(W.pieces()):
                pool.wait_ge(high0, n + 1)
                G.tensor_tensor(low, whole, high, ALU.subtract).then_inc(low0, 1)
            for m in range(NSTEP):
                pool.wait_ge(hot, m + 1)
                if m >= 2:
                    pool.wait_ge(placed, m - 1)
                it = iota_t[:, :, :].rearrange("p k t -> p (k t)")[:, m * STEP:(m + 1) * STEP]
                G.tensor_tensor(val[:, m % 2, :, 0, :], oh_bl[:, m % 2],
                                it.unsqueeze(2).to_broadcast([P, STEP, BLOCKS]), ALU.mult).then_inc(tiles_in, 1)

        @block.scalar
        def _(act):
            A = nc.scalar
            act.wait_ge(ew_loaded, 48)
            for whole, high, _ in W.pieces():
                A.activation(high, whole, ACT.Copy).then_inc(high0, 1)
            act.wait_ge(made, 7)
            for m in range(NSTEP):
                act.wait_ge(hot, m + 1)
                if m >= 2:
                    act.wait_ge(placed, m - 1)
                A.activation(val[:, m % 2, :, 1, :], oh_bl[:, m % 2], ACT.Copy, scale=iota_p[:, 0:1])\
                    .then_inc(rows_in, 1)

        @block.vector
        def _(dve):
            V = nc.vector
            n = [0]

            def link(ins):
                n[0] += 1
                ins.then_inc(step_done, 1)
                dve.wait_ge(step_done, n[0])
            full = [P, TT, E]
            dve.wait_ge(made, 7)
            rank_b = rank[:, :].unsqueeze(1).to_broadcast(full)
            src = logits
            for k in range(TOP):
                link(V.tensor_reduce(top[:, :], src[:, :, :], AX.X, ALU.max))
                link(V.tensor_tensor(eq[:, :, :], src[:, :, :], top[:, :].unsqueeze(2).to_broadcast(full), ALU.is_equal))
                link(V.tensor_tensor(rk[:, :, :], eq[:, :, :], rank_b, ALU.mult))
                link(V.tensor_reduce(win[:, k, :], rk[:, :, :], AX.X, ALU.max))
                link(V.tensor_tensor(oh[:, k], rank_b, win[:, k, :].unsqueeze(2).to_broadcast(full), ALU.is_equal))
                if k == 0:
                    link(V.tensor_scalar(eq[:, :, :], oh[:, 0], MASKED, None, ALU.mult))
                    link(V.tensor_tensor(left[:, :, :], eq[:, :, :], src[:, :, :], ALU.add))
                    src = left
            dve.sem_inc(chosen, 1)
            ALL = TOP * TT
            per = TOP * TT // 4
            dve.wait_ge(counted, 2)
            V.memset(run[0][:, 0:1, :], 0.0)
            for i in range(4):
                lo, hi = i * per, min((i + 1) * per, ALL - 1)
                ins = V.tensor_copy(run[0][:, lo + 1:hi + 1, :],
                                    banks[4 + i][:, 0:(hi - lo) * E].rearrange("p (t e) -> p t e", e=E))
            link(ins)
            a, c, d = 0, 1, 1
            while d < ALL:
                V.tensor_copy(run[c][:, 0:d, :], run[a][:, 0:d, :])
                link(V.tensor_tensor(run[c][:, d:ALL, :], run[a][:, d:ALL, :], run[a][:, 0:ALL - d, :], ALU.add))
                a, c, d = c, a, 2 * d
            for i in range(4):
                ins = V.tensor_tensor(pos[:, i * per:(i + 1) * per, :],
                                      banks[i][:, 0:per * E].rearrange("p (t e) -> p t e", e=E),
                                      run[a][:, i * per:(i + 1) * per, :], ALU.add)
            link(ins)
            link(V.tensor_tensor(run[c][:, :, :], pos[:, :, :], oh[:, :, :, :].rearrange("p k t e -> p (k t) e"),
                                 ALU.mult))
            link(V.tensor_reduce(posn[:, :], run[c][:, :, :], AX.X, ALU.add))
            cur = blk[0]
            link(V.tensor_scalar(cur[:, :], posn[:, :], SUB + 0.5, None, ALU.is_gt))
            for m in range(2, SLOT_BLOCKS):
                nxt = blk[(m + 1) % 2]
                link(V.scalar_tensor_tensor(out=nxt[:, :], in0=posn[:, :], scalar=SUB * m + 0.5, in1=cur[:, :],
                                            op0=ALU.is_gt, op1=ALU.add))
                cur = nxt
            link(V.scalar_tensor_tensor(out=inner[:, :], in0=cur[:, :], scalar=-float(SUB), in1=posn[:, :],
                                        op0=ALU.mult, op1=ALU.add))
            link(V.tensor_scalar(over[:, :], posn[:, :], CAPACITY + 0.5, 1000.0, ALU.is_gt, ALU.mult))
            link(V.tensor_tensor(base[:, :], over[:, :], cur[:, :], ALU.add))
            link(V.scalar_tensor_tensor(out=slot_of[:, :], in0=win[:, :, :].rearrange("p k t -> p (k t)"),
                                        scalar=-float(SLOT_BLOCKS), in1=base[:, :], op0=ALU.mult, op1=ALU.add))
            link(V.tensor_scalar(base[:, :], slot_of[:, :], float(SLOT_BLOCKS * E), None, ALU.add))
            link(V.tensor_scalar(posn[:, :], inner[:, :], -1.0, None, ALU.add))
            for m in range(NSTEP):
                tiles = slice(m * STEP, (m + 1) * STEP)
                if m >= 2:
                    dve.wait_ge(placed, m - 1)
                V.tensor_tensor(oh_in[:, m % 2], posn[:, tiles].unsqueeze(2).to_broadcast([P, STEP, P]),
                                iota_in[:, :].unsqueeze(1).to_broadcast([P, STEP, P]), ALU.is_equal)
                wide = [P, STEP, BLOCKS]
                if m >= 2:
                    dve.wait_ge(tiles_in, m - 1)
                    dve.wait_ge(rows_in, m - 1)
                V.tensor_tensor(oh_bl[:, m % 2], base[:, tiles].unsqueeze(2).to_broadcast(wide),
                                iota_bl[:, :].unsqueeze(1).to_broadcast(wide), ALU.is_equal).then_inc(hot, 1)
            dve.wait_ge(placed, NSTEP)
            link(V.tensor_copy(tab[:, :, :], banks[0][:, 0:2 * BLOCKS].rearrange("p (v k) -> p v k", v=2)))
            link(V.scalar_tensor_tensor(out=tok[:, :], in0=tab[:, 0], scalar=float(P), in1=tab[:, 1],
                                        op0=ALU.mult, op1=ALU.add))
            link(V.tensor_scalar(none[:, :], tab[:, 0], 0.5, None, ALU.is_lt))
            link(V.tensor_scalar(tok2[:, :], tok[:, :], -float(P), None, ALU.add))
            link(V.scalar_tensor_tensor(out=fin[:, 0], in0=none[:, :], scalar=float(P), in1=tok2[:, :],
                                        op0=ALU.mult, op1=ALU.add))
            link(V.scalar_tensor_tensor(out=fin[:, 1], in0=none[:, :], scalar=float(NOWHERE), in1=tok2[:, :],
                                        op0=ALU.mult, op1=ALU.add))
            link(V.tensor_copy(gather_rows[:, :], fin[:, 0]))
            link(V.tensor_copy(scatter_rows[:, :], fin[:, 1]))

        @block.tensor
        def _(pe):
            T = nc.tensor
            pe.wait_ge(chosen, 1)
            flat = oh[:, :, :, :].rearrange("p k t e -> p (k t e)")
            width = TOP * TT * E // 4
            for k, left_m in enumerate((upto, ones)):
                for i in range(4):
                    mm = T.matmul(banks[4 * k + i][:, 0:width], left_m[:, :], flat[:, i * width:(i + 1) * width],
                                  start=True, stop=True)
                mm.then_inc(counted, 1)
            for m in range(NSTEP):
                pe.wait_ge(hot, m + 1)
                pe.wait_ge(tiles_in, m + 1)
                pe.wait_ge(rows_in, m + 1)
                for t in range(STEP):
                    mm = T.matmul(banks[0][:, 0:2 * BLOCKS], oh_in[:, m % 2, t], val[:, m % 2, t]
                                  .rearrange("p v k -> p (v k)"), start=m == t == 0,
                                  stop=m == NSTEP - 1 and t == STEP - 1)
                mm.then_inc(placed, 1)


def experts(nc, W, persist, ew1, ew3, ew2, gather_rows, scatter_rows, z, out):
    NCH = 2
    CB = CHUNK_BLOCKS
    CT = CB * SUB
    logits, gcol, bcol, wr_hi, wr_lo, id32 = persist
    out_rows = out.rearrange("b t d -> (b t) d")
    LAST_ROW = out_rows.shape[0] - 1
    E = EXPERTS

    ctx = ExitStack()
    with nc.cleanup_on_exit(), ctx:
        sb, ps = tensors(ctx, nc)
        signals = []

        def sig(name, per=NCH, unit=1, credit=1):
            s = Signal(nc, name, per, unit, credit)
            signals.append(s)
            return s

        z_in = sb("e_z_in", [P, CB, D], F32)
        y_in = sb("e_y_in", [P, CB, D], F32)
        o_sb = sb("e_o_sb", [P, CB, D], F32)
        row_g = sb("e_row_g", [P, 2, CB], I32)
        row_s = sb("e_row_s", [P, CB], I32)
        eye = sb("e_eye", [P, E, E], F32)
        mine = sb("e_mine", [P, 2, E], F32)
        h32 = sb("e_h32", [P, FT, CT], F32)
        h_hi = sb("e_h_hi", [P, 2, FT, CT], FP16)
        h_lo = sb("e_h_lo", [P, 2, FT, CT], FP16)
        th = sb("e_th", [P, 2, CT], F32)
        u = sb("e_u", [P, 2, CT], F32)
        g32 = sb("e_g32", [P, 2, CT], F32)
        g_hi = sb("e_g_hi", [P, FC, CT], FP16)
        g_lo = sb("e_g_lo", [P, FC, CT], FP16)
        lg = sb("e_lg", [P, CB, E], F32)
        rest = sb("e_rest", [P, CB, E], F32)
        part = sb("e_part", [P, CB, E], F32)
        best = sb("e_best", [P, CB], F32)
        own = sb("e_own", [P, CB], F32)
        gap = sb("e_gap", [P, CB], F32)
        ex = sb("e_ex", [P, CB], F32)
        ex2 = sb("e_ex2", [P, CB], F32)
        half_gate = sb("e_half_gate", [P, 2, CB], F32)

        bank_a = [ps(f"e_bank_a{i}", [P, 512]) for i in range(2)]
        bank_b = [ps(f"e_bank_b{i}", [P, 512]) for i in range(2)]
        bank_d = [ps(f"e_bank_d{i}", [P, 512]) for i in range(2)]
        bank_t = [ps(f"e_bank_t{i}", [P, 512]) for i in range(2)]

        setup = nc.alloc_semaphore("e_setup")
        passed = nc.alloc_semaphore("e_passed")
        stage_in = sig("e_stage_in", 1, 48)
        z_rows = sig("e_z_rows", NCH * CB, 16, credit=0)
        y_rows = sig("e_y_rows", NCH * CB, 16, credit=0)
        stored = sig("e_stored", NCH * CB, 16, credit=0)
        (rows_set, targets_set, h_hi_done, h_done, lg_done, lg_copied, rest_done, best_done, part_done, own_done, gap_done,
         ex_done, ex2_done, gate_done, o_ready) = [sig("e_" + n) for n in (
             "rows_set", "targets_set", "h_hi_done", "h_done", "lg_done", "lg_copied", "rest_done", "best_done",
             "part_done", "own_done", "gap_done", "ex_done", "ex2_done", "gate_done", "o_ready")]
        turned = sig("e_turned", FT * NCH)
        h32_done = sig("e_h32_done", FT * NCH)
        (up_a, up_b, gated, u_done, g_done, g_hi_done, g_split, down_done) = [sig("e_" + n, FC * NCH) for n in (
            "up_a", "up_b", "gated", "u_done", "g_done", "g_hi_done", "g_split", "down_done")]
        up_high, up_low, down_high, down_low = [sig("e_" + n, FC) for n in (
            "up_high", "up_low", "down_high", "down_low")]
        block = ctx.enter_context(nc.Block())

        def place(e, s, lag):
            q = s - lag
            at = e + q // NCH
            if isinstance(e, int) and not 0 <= at < E:
                return None
            return at, q % NCH

        def later(e):
            return None if isinstance(e, int) and e + 1 >= E else e + 1

        def turns(engine, body):
            body(0, -1)
            for s in range(NCH):
                body(0, s)
            with engine.Fori(1, E - 1) as e:
                for s in range(NCH):
                    body(e, s)
            for s in range(NCH):
                body(E - 1, s)
            body(E, 0)

        @block.sync
        def _(sp):
            stage_in.start(sp)
            sp.sem_inc(stage_in.sem, 48)

            def slot(e, s):
                nxt = later(e)
                if s == 0 and nxt is not None and not (isinstance(e, int) and e < 0):
                    if isinstance(e, int) and e == 0:
                        sp.wait_ge(z_rows.sem, z_rows.after(0, CB))
                    sp.wait_ge(up_low.sem, up_low.after(e, FC))
                    sp.wait_ge(down_low.sem, down_low.after(e, FC))
                    if isinstance(nxt, int):
                        W.load(sp, ew1[nxt], ew3[nxt], ew2[nxt], stage_in.sem)
                    else:
                        one = bass.ds(nxt, 1)
                        W.load(sp, ew1[one].rearrange("o d f -> (o d) f"), ew3[one].rearrange("o d f -> (o d) f"),
                               ew2[one].rearrange("o f d -> (o f) d"), stage_in.sem)
            turns(sp, slot)

        @block.gpsimd
        def _(pool):
            G = nc.gpsimd
            for s in signals:
                if s is not stage_in:
                    s.start(pool)
            for s in (up_high, up_low, down_high, down_low):
                pool.sem_inc(s.sem, FC)
            G.memset(eye[:, :, :], 0.0).then_inc(setup, 1)
            G.memset(z_in[:, :, :], 0.0).then_inc(setup, 1)
            pool.wait_ge(setup, 2)
            G.affine_select(out=eye[:, :, :], in_=eye[:, :, :], compare_op=ALU.not_equal, fill=1.0, base=0,
                            channel_multiplier=0, pattern=[[1, E], [-1, E]]).then_inc(setup, 1)
            pool.wait_ge(setup, 3)

            def slot(e, s):
                def low(f):
                    if at := place(e, s, 0):
                        c, t = at
                        n = FC * t + f
                        pool.wait_ge(g_hi_done.sem, g_hi_done.after(c, n + 1))
                        pool.wait_ge(down_done.sem, down_done.after(c, n + 1 - FC))
                        G.tensor_tensor(g_lo[:, f], g32[:, f % 2], g_hi[:, f], ALU.subtract).then_inc(g_split.sem, 1)

                def low_h():
                    if at := place(e, s, -1):
                        c, t = at
                        pool.wait_ge(h_hi_done.sem, h_hi_done.after(c, t + 1))
                        G.tensor_tensor(h_lo[:, t], h32[:, :, :], h_hi[:, t], ALU.subtract).then_inc(h_done.sem, 1)

                def gather_z():
                    if at := place(e, s, -1):
                        c, t = at
                        n = c * SLOT_BLOCKS + t * CB
                        pool.wait_ge(gate_done.sem, gate_done.after(c, t - 1))
                        if y_rows.due(c, CB * (t - 1)):
                            pool.wait_ge(y_rows.sem, y_rows.after(c, CB * (t - 1)))
                        G.tensor_copy(row_g[:, t], gather_rows[:, bass.ds(n, CB)])
                        G.tensor_copy(mine[:, t], eye[:, bass.ds(c, 1), :].rearrange("p o e -> p (o e)"))\
                            .then_inc(rows_set.sem, 1)
                        pool.wait_ge(rows_set.sem, rows_set.after(c, t + 1))
                        pool.wait_ge(turned.sem, turned.after(c, FT * t))
                        pool.sem_inc(passed, 1)
                        for j in range(CB):
                            G.indirect_dma_start(out=z_in[0:SUB, j, :], out_offset=None, in_=z,
                                                 in_offset=bass.IndirectOffsetOnAxis(ap=row_g[0:SUB, t, j:j + 1], axis=0))\
                                .then_inc(z_rows.sem, 16)

                def scatter():
                    if at := place(e, s, 1):
                        c, t = at
                        if stored.due(c, CB * t):
                            pool.wait_ge(stored.sem, stored.after(c, CB * t))
                        G.tensor_copy(row_s[:, :], scatter_rows[:, bass.ds(c * SLOT_BLOCKS + t * CB, CB)])\
                            .then_inc(targets_set.sem, 1)
                        pool.wait_ge(targets_set.sem, targets_set.after(c, t + 1))
                        pool.wait_ge(o_ready.sem, o_ready.after(c, t + 1))
                        pool.sem_inc(passed, 1)
                        for j in range(CB):
                            G.indirect_dma_start(out=out_rows, out_offset=bass.IndirectOffsetOnAxis(
                                ap=row_s[0:SUB, j:j + 1], axis=0), in_=o_sb[0:SUB, j, :], in_offset=None,
                                bounds_check=LAST_ROW, oob_is_err=False).then_inc(stored.sem, 16)

                def gather_y():
                    if at := place(e, s, 0):
                        c, t = at
                        if stored.due(c, CB * t):
                            pool.wait_ge(stored.sem, stored.after(c, CB * t))
                        pool.sem_inc(passed, 1)
                        for j in range(CB):
                            G.indirect_dma_start(out=y_in[0:SUB, j, :], out_offset=None, in_=out_rows,
                                                 in_offset=bass.IndirectOffsetOnAxis(ap=row_g[0:SUB, t, j:j + 1], axis=0))\
                                .then_inc(y_rows.sem, 16)
                low(0)
                gather_z()
                low(1)
                low(2)
                low(3)
                scatter()
                low(4)
                low_h()
                low(5)
                low(6)
                gather_y()
                low(7)
            turns(pool, slot)
            pool.wait_ge(stored.sem, stored.after(E - 1, NCH * CB))

        @block.vector
        def _(dve):
            V = nc.vector

            def split_up(e, f):
                dve.wait_ge(up_high.sem, up_high.after(e, f + 1))
                t = slice(f * P, (f + 1) * P)
                w = "p k i o -> p (k i) o"
                V.tensor_tensor(W.up_lo[:, :, :, t].rearrange(w), W.stage_up[:, :, :, t].rearrange(w),
                                W.up_hi[:, :, :, t].rearrange(w), ALU.subtract).then_inc(up_low.sem, 1)

            def split_down(e, f):
                dve.wait_ge(down_high.sem, down_high.after(e, f + 1))
                V.tensor_tensor(W.down_lo[:, f], W.stage_down[:, f], W.down_hi[:, f], ALU.subtract)\
                    .then_inc(down_low.sem, 1)
            dve.wait_ge(setup, 3)

            def slot(e, s):
                def gate(f):
                    if at := place(e, s, 0):
                        c, t = at
                        n = FC * t + f
                        dve.wait_ge(gated.sem, gated.after(c, n + 1))
                        dve.wait_ge(g_done.sem, g_done.after(c, n - 1))
                        V.scalar_tensor_tensor(out=u[:, f % 2], in0=th[:, f % 2], scalar=1.0, in1=bank_a[f % 2][:, 0:CT],
                                               op0=ALU.add, op1=ALU.mult).then_inc(u_done.sem, 1)
                        dve.wait_ge(u_done.sem, u_done.after(c, n + 1))
                        dve.wait_ge(up_b.sem, up_b.after(c, n + 1))
                        dve.wait_ge(g_split.sem, g_split.after(c, n - 1))
                        V.tensor_tensor(g32[:, f % 2], bank_b[f % 2][:, 0:CT], u[:, f % 2], ALU.mult)\
                            .then_inc(g_done.sem, 1)
                        nxt = later(e)
                        if s == NCH - 1 and nxt is not None:
                            if f >= 1:
                                split_up(nxt, f - 1)
                            if f >= 4:
                                split_down(nxt, f - 4)

                def last_splits():
                    nxt = later(e)
                    if s == NCH - 1 and nxt is not None:
                        split_up(nxt, FC - 1)
                        split_down(nxt, FC - 4), split_down(nxt, FC - 3)

                def last_down():
                    if s == 0 and (not isinstance(e, int) or 0 < e < E):
                        split_down(e, FC - 2), split_down(e, FC - 1)

                def finish():
                    if at := place(e, s, 1):
                        c, t = at
                        dve.wait_ge(down_done.sem, down_done.after(c, FC * (t + 1)))
                        dve.wait_ge(y_rows.sem, y_rows.after(c, CB * (t + 1)))
                        if stored.due(c, CB * t):
                            dve.wait_ge(stored.sem, stored.after(c, CB * t))
                        dve.wait_ge(gate_done.sem, gate_done.after(c, t + 1))
                        for j in range(CB):
                            ins = V.scalar_tensor_tensor(
                                out=o_sb[0:SUB, j, :], in0=bank_d[j // 2][0:SUB, (j % 2) * D:(j % 2 + 1) * D],
                                scalar=half_gate[0:SUB, t, j:j + 1], in1=y_in[0:SUB, j, :],
                                op0=ALU.mult, op1=ALU.add)
                        ins.then_inc(o_ready.sem, 1)

                def gates():
                    if at := place(e, s, -1):
                        c, t = at
                        n = t + 1
                        r = slice(0, SUB)
                        me = mine[r, t, :].unsqueeze(1).to_broadcast([SUB, CB, E])
                        dve.wait_ge(lg_done.sem, lg_done.after(c, n))
                        dve.wait_ge(rows_set.sem, rows_set.after(c, n))
                        V.tensor_copy(lg[r, :, :], bank_t[0][r, 0:CB * 8].rearrange("p (j e) -> p j e", e=8)[:, :, 0:E])\
                            .then_inc(lg_copied.sem, 1)
                        dve.wait_ge(lg_copied.sem, lg_copied.after(c, n))
                        V.tensor_tensor(part[r, :, :], lg[r, :, :], me, ALU.mult).then_inc(part_done.sem, 1)
                        V.scalar_tensor_tensor(out=rest[r, :, :], in0=me, scalar=MASKED, in1=lg[r, :, :], op0=ALU.mult,
                                               op1=ALU.add).then_inc(rest_done.sem, 1)
                        dve.wait_ge(part_done.sem, part_done.after(c, n))
                        V.tensor_reduce(own[r, :], part[r, :, :], AX.X, ALU.add).then_inc(own_done.sem, 1)
                        dve.wait_ge(rest_done.sem, rest_done.after(c, n))
                        V.tensor_reduce(best[r, :], rest[r, :, :], AX.X, ALU.max).then_inc(best_done.sem, 1)
                        dve.wait_ge(own_done.sem, own_done.after(c, n))
                        dve.wait_ge(best_done.sem, best_done.after(c, n))
                        V.tensor_tensor(gap[r, :], best[r, :], own[r, :], ALU.subtract).then_inc(gap_done.sem, 1)
                        dve.wait_ge(ex_done.sem, ex_done.after(c, n))
                        V.tensor_scalar(ex2[r, :], ex[r, :], 1.0, 2.0, ALU.add, ALU.mult).then_inc(ex2_done.sem, 1)
                        dve.wait_ge(ex2_done.sem, ex2_done.after(c, n))
                        V.reciprocal(half_gate[r, t, :], ex2[r, :]).then_inc(gate_done.sem, 1)
                gate(0)
                gate(1)
                finish()
                for f in range(2, FC):
                    gate(f)
                    if f == 3:
                        last_down()
                last_splits()
                gates()
            turns(dve, slot)

        @block.scalar
        def _(act):
            A = nc.scalar

            def split_up(e, f):
                act.wait_ge(stage_in.sem, stage_in.after(e, 1))
                act.wait_ge(up_b.sem, up_b.after(e, f + 1 - FC))
                t = slice(f * P, (f + 1) * P)
                w = "p k i o -> p (k i) o"
                A.activation(W.up_hi[:, :, :, t].rearrange(w), W.stage_up[:, :, :, t].rearrange(w), ACT.Copy)\
                    .then_inc(up_high.sem, 1)

            def split_down(e, f):
                act.wait_ge(down_done.sem, down_done.after(e, f + 1 - FC))
                A.activation(W.down_hi[:, f], W.stage_down[:, f], ACT.Copy).then_inc(down_high.sem, 1)

            def slot(e, s):
                def gate(f):
                    if at := place(e, s, 0):
                        c, t = at
                        n = FC * t + f
                        act.wait_ge(up_a.sem, up_a.after(c, n + 1))
                        act.wait_ge(u_done.sem, u_done.after(c, n - 1))
                        A.activation(th[:, f % 2], bank_a[f % 2][:, 0:CT], ACT.Tanh, scale=0.5).then_inc(gated.sem, 1)

                def high(f):
                    if at := place(e, s, 0):
                        c, t = at
                        n = FC * t + f
                        act.wait_ge(g_done.sem, g_done.after(c, n + 1))
                        act.wait_ge(down_done.sem, down_done.after(c, n + 1 - FC))
                        A.activation(g_hi[:, f], g32[:, f % 2], ACT.Copy).then_inc(g_hi_done.sem, 1)
                        nxt = later(e)
                        if s == NCH - 1 and nxt is not None:
                            split_up(nxt, f)
                            if f >= 3:
                                split_down(nxt, f - 3)

                def last_down():
                    if s == 0 and (not isinstance(e, int) or 0 < e < E):
                        split_down(e, FC - 2), split_down(e, FC - 1)

                def affine():
                    if at := place(e, s, -1):
                        c, t = at
                        for i in range(FT):
                            act.wait_ge(turned.sem, turned.after(c, FT * t + i + 1))
                            act.wait_ge(h_done.sem, h_done.after(c, t))
                            A.activation(h32[:, i], bank_t[i][:, 0:CT], ACT.Identity, bias=bcol[:, i:i + 1],
                                         scale=gcol[:, i:i + 1]).then_inc(h32_done.sem, 1)
                        act.wait_ge(h32_done.sem, h32_done.after(c, FT * t + FT))
                        A.activation(h_hi[:, t], h32[:, :, :], ACT.Copy).then_inc(h_hi_done.sem, 1)

                def exp_gap():
                    if at := place(e, s, -1):
                        c, t = at
                        act.wait_ge(gap_done.sem, gap_done.after(c, t + 1))
                        A.activation(ex[0:SUB, :], gap[0:SUB, :], ACT.Exp).then_inc(ex_done.sem, 1)
                gate(0)
                for f in range(1, FC):
                    gate(f)
                    high(f - 1)
                    if f == 3:
                        last_down()
                    if f == 5:
                        affine()
                high(FC - 1)
                if s == NCH - 1 and later(e) is not None and place(e, s, 0):
                    split_down(later(e), FC - 3)
                exp_gap()
            turns(act, slot)

        @block.tensor
        def _(pe):
            T = nc.tensor

            def slot(e, s):
                def up(f):
                    if at := place(e, s, 0):
                        c, t = at
                        n = FC * t + f
                        if f == 0:
                            pe.wait_ge(h_done.sem, h_done.after(c, t + 1))
                        if t == 0:
                            pe.wait_ge(up_low.sem, up_low.after(c, f + 1))
                        pe.wait_ge(u_done.sem, u_done.after(c, n - 1))
                        pe.wait_ge(g_done.sem, g_done.after(c, n - 1))
                        for k, (bank, done) in enumerate(((bank_a, up_a), (bank_b, up_b))):
                            for i in range(FT):
                                w_hi = W.up_hi[:, k, i, f * P:(f + 1) * P]
                                w_lo = W.up_lo[:, k, i, f * P:(f + 1) * P]
                                T.matmul(bank[f % 2][:, 0:CT], w_hi, h_hi[:, t, i], start=i == 0, stop=False)
                                T.matmul(bank[f % 2][:, 0:CT], w_hi, h_lo[:, t, i], start=False, stop=False)
                                mm = T.matmul(bank[f % 2][:, 0:CT], w_lo, h_hi[:, t, i], start=False,
                                              stop=i == FT - 1)
                            mm.then_inc(done.sem, 1)

                def down(f, lag):
                    if at := place(e, s, lag):
                        c, t = at
                        n = FC * t + f
                        if f == 0:
                            pe.wait_ge(o_ready.sem, o_ready.after(c, t))
                        if t == 0:
                            pe.wait_ge(down_low.sem, down_low.after(c, f + 1))
                        pe.wait_ge(g_split.sem, g_split.after(c, n + 1))
                        for j in range(CB):
                            o = bank_d[j // 2][0:SUB, (j % 2) * D:(j % 2 + 1) * D]
                            tok = slice(j * SUB, (j + 1) * SUB)
                            for k, (l, w) in enumerate(((g_hi, W.down_hi), (g_hi, W.down_lo), (g_lo, W.down_hi))):
                                mm = T.matmul(o, l[:, f, tok], w[:, f, :], start=f == k == 0 and j % 2 == 0,
                                              stop=f == FC - 1 and k == 2, skip_group_check=True)
                        mm.then_inc(down_done.sem, 1)

                def turn():
                    if at := place(e, s, -1):
                        c, t = at
                        pe.wait_ge(z_rows.sem, z_rows.after(c, CB * (t + 1)))
                        pe.wait_ge(lg_copied.sem, lg_copied.after(c, t))
                        for i in range(FT):
                            pe.wait_ge(h32_done.sem, h32_done.after(c, FT * (t - 1) + i + 1))
                            for j in range(CB):
                                mm = T.transpose(bank_t[i][:, j * SUB:(j + 1) * SUB], z_in[0:SUB, j, i * P:(i + 1) * P],
                                                 id32[0:SUB, 0:SUB])
                            mm.then_inc(turned.sem, 1)

                def score():
                    if at := place(e, s, -1):
                        c, t = at
                        pe.wait_ge(h_done.sem, h_done.after(c, t + 1))
                        for j in range(CB):
                            tok = slice(j * SUB, (j + 1) * SUB)
                            for i in range(FT):
                                for k, (l, w) in enumerate(((h_hi, wr_hi), (h_hi, wr_lo), (h_lo, wr_hi))):
                                    mm = T.matmul(bank_t[0][0:SUB, j * 8:j * 8 + E], l[:, t, i, tok], w[:, i, :],
                                                  start=i == k == 0, stop=i == FT - 1 and k == 2)
                        mm.then_inc(lg_done.sem, 1)
                up(0)
                down(FC - 2, 1)
                up(1)
                down(FC - 1, 1)
                for f in range(2, FC):
                    up(f)
                    down(f - 2, 0)
                    if f == 4:
                        turn()
                score()
            turns(pe, slot)


def program(nc, x, wq, wk, wv, wo, ln_g, ln_b, wr, w1, w3, w2, w1s, w3s, w2s, out):
    batches, seq, _ = x.shape
    y = nc.dram_tensor("y_rows", (batches, seq, D), F32).ap()
    z = nc.dram_tensor("z_rows", (batches * seq, D), F32).ap()
    ctx = ExitStack()
    with ctx:
        sb, _ = tensors(ctx, nc)
        W = Weights(sb)
        TT = batches * seq // P
        logits = sb("logits", [P, TT, EXPERTS], F32)
        gather_rows = sb("gather_rows", [P, EXPERTS * SLOT_BLOCKS], I32)
        scatter_rows = sb("scatter_rows", [P, EXPERTS * SLOT_BLOCKS], I32)
        id32 = sb("id32", [P, P], F32)
        persist = (logits, sb("gcol", [P, FT], F32), sb("bcol", [P, FT], F32), sb("wr_hi", [P, FT, EXPERTS], FP16),
                   sb("wr_lo", [P, FT, EXPERTS], FP16), id32)
        shared_loaded = ctx.enter_context(nc.semaphore("shared_loaded"))
        expert0_loaded = ctx.enter_context(nc.semaphore("expert0_loaded"))
        attention(nc, x, wq, wk, wv, wo, y, id32, W, (w1s, w3s, w2s), shared_loaded)
        shared_ffn(nc, W, persist, shared_loaded, y, ln_g, ln_b, wr, w1, w3, w2, z, out, expert0_loaded)
        route(nc, W, expert0_loaded, logits, gather_rows, scatter_rows, batches)
        experts(nc, W, persist, w1, w3, w2, gather_rows, scatter_rows, z, out)


def kernel(L0_attn_x, L0_attn_Wq, L0_attn_Wk, L0_attn_Wv, L0_attn_Wo, L0_ffn_ln_g, L0_ffn_ln_b, L0_ffn_Wr, L0_ffn_W1,
           L0_ffn_W3, L0_ffn_W2, L0_ffn_W1s, L0_ffn_W3s, L0_ffn_W2s):
    import numpy as np
    import concourse.bacc as bacc
    from concourse.bass_utils import run_bass_kernel_spmd

    def column(a):
        return np.asarray(a).reshape(FT, P).T
    arrays = dict(x=L0_attn_x, wq=np.asarray(L0_attn_Wq).T, wk=np.asarray(L0_attn_Wk).T, wv=np.asarray(L0_attn_Wv).T,
                  wo=np.asarray(L0_attn_Wo).T, ln_g=column(L0_ffn_ln_g), ln_b=column(L0_ffn_ln_b), wr=L0_ffn_Wr,
                  w1=L0_ffn_W1, w3=L0_ffn_W3, w2=L0_ffn_W2, w1s=L0_ffn_W1s, w3s=L0_ffn_W3s, w2s=L0_ffn_W2s)
    arrays = {"in_" + n: np.ascontiguousarray(a) for n, a in arrays.items()}
    nc = bacc.Bacc("TRN2", target_bir_lowering=False, num_devices=1)
    args = [nc.dram_tensor(n, a.shape, mybir.dt.from_np(a.dtype), kind="ExternalInput").ap() for n, a in arrays.items()]
    out = nc.dram_tensor("out", arrays["in_x"].shape, F32, kind="ExternalOutput").ap()
    program(nc, *args, out)
    return run_bass_kernel_spmd(nc, [arrays], core_ids=[0]).results[0]["out"]
```
